# Optimizing a Trainium2 kernel written in Bass

```python
import numpy as np
import jax
import jax.numpy as jnp

def _softmax(x, axis=-1):
    return jax.nn.softmax(x, axis=axis)

def _gelu(x):
    return jax.nn.gelu(x, approximate=True)

def _silu(x):
    return jax.nn.silu(x)

def _sigmoid(x):
    return jax.nn.sigmoid(x)

def _layernorm(x, axis=-1, eps=1e-05):
    m = jnp.mean(x, axis=axis, keepdims=True)
    v = jnp.var(x, axis=axis, keepdims=True)
    return (x - m) / jnp.sqrt(v + eps)

def _scatter_add(tgt, idx, src, axis=0):
    return tgt.at[idx].add(src)

def _segment_sum(src, seg, n):
    return jax.ops.segment_sum(src, seg, n)
kernel_name = 'mk_conv_preact_d4_conv_nhwc64_r2_b68665'

def setup_inputs(seed: int=0):
    np.random.seed(seed)
    _w = jnp.asarray

    def _rec_inputs():
        import jax
        import jax.numpy as jnp
        _gk = jax.random.key(seed)
        x = -0.0003929 + 0.9999 * jax.random.normal(jax.random.fold_in(_gk, 1), (1, 256, 256, 32), jnp.float32)
        return x
    x = _rec_inputs()

    def _L0_conv_setup():
        import jax, jax.numpy as jnp
        import numpy as np
        B, L, DIM, HID, WIN = (1, 256, 32, 64, 4)

        def _ln(x, scale, bias, eps=1e-06):
            m = jnp.mean(x, axis=-1, keepdims=True)
            v = jnp.var(x, axis=-1, keepdims=True)
            return (x - m) / jnp.sqrt(v + eps) * scale + bias

        def _banded_ingoing(left, right, w):
            n = left.shape[1]
            ii = jnp.arange(n)
            offs = jnp.arange(-w, w + 1)
            rows = ii[:, None] + offs[None, :]
            valid = ((rows >= 0) & (rows < n)).astype(left.dtype)
            rows_c = jnp.clip(rows, 0, n - 1)
            Lb = left[:, rows_c, ii[:, None], :] * valid[None, :, :, None]
            out = jnp.zeros_like(right)
            for di, dd in enumerate(range(-w, w + 1)):
                if dd >= 0:
                    sh = jnp.pad(right[:, dd:], ((0, 0), (0, dd), (0, 0), (0, 0)))
                else:
                    sh = jnp.pad(right[:, :dd], ((0, 0), (-dd, 0), (0, 0), (0, 0)))
                out = out + Lb[:, :, di, None, :] * sh
            return out
        key = jax.random.key(seed)
        ks = jax.random.split(key, 8)
        d = {}
        d['x'] = jax.random.normal(ks[0], (B, L, L, DIM), dtype=jnp.float32)
        d['src_mask'] = jnp.ones((B, L), dtype=jnp.int32)
        d['norm_scale'] = jnp.ones((DIM,), jnp.float32)
        d['norm_bias'] = jnp.zeros((DIM,), jnp.float32)
        for i, nm in enumerate(['l', 'r', 'lg', 'rg', 'og']):
            d[f'W{nm}'] = jax.random.normal(ks[i + 1], (DIM, HID), jnp.float32) * 0.02
            d[f'b{nm}'] = jnp.zeros((HID,), jnp.float32)
        d['out_norm_scale'] = jnp.ones((HID,), jnp.float32)
        d['out_norm_bias'] = jnp.zeros((HID,), jnp.float32)
        d['Wo'] = jax.random.normal(ks[6], (HID, DIM), jnp.float32) * 0.02
        d['bo'] = jnp.zeros((DIM,), jnp.float32)
        return d
    _L0_conv_all = _L0_conv_setup()
    _L0_conv_in = {k: v for k, v in _L0_conv_all.items() if k in ('src_mask', 'norm_scale', 'norm_bias', 'Wl', 'bl', 'Wr', 'br', 'Wlg', 'blg', 'Wrg', 'brg', 'Wog', 'bog', 'out_norm_scale', 'out_norm_bias', 'Wo', 'bo')}
    del _L0_conv_all

    def _L1_conv_setup():
        import jax, jax.numpy as jnp
        import numpy as np
        B, L, DIM, HID, WIN = (1, 256, 32, 64, 4)

        def _ln(x, scale, bias, eps=1e-06):
            m = jnp.mean(x, axis=-1, keepdims=True)
            v = jnp.var(x, axis=-1, keepdims=True)
            return (x - m) / jnp.sqrt(v + eps) * scale + bias

        def _banded_ingoing(left, right, w):
            n = left.shape[1]
            ii = jnp.arange(n)
            offs = jnp.arange(-w, w + 1)
            rows = ii[:, None] + offs[None, :]
            valid = ((rows >= 0) & (rows < n)).astype(left.dtype)
            rows_c = jnp.clip(rows, 0, n - 1)
            Lb = left[:, rows_c, ii[:, None], :] * valid[None, :, :, None]
            out = jnp.zeros_like(right)
            for di, dd in enumerate(range(-w, w + 1)):
                if dd >= 0:
                    sh = jnp.pad(right[:, dd:], ((0, 0), (0, dd), (0, 0), (0, 0)))
                else:
                    sh = jnp.pad(right[:, :dd], ((0, 0), (-dd, 0), (0, 0), (0, 0)))
                out = out + Lb[:, :, di, None, :] * sh
            return out
        key = jax.random.key(seed)
        ks = jax.random.split(key, 8)
        d = {}
        d['x'] = jax.random.normal(ks[0], (B, L, L, DIM), dtype=jnp.float32)
        d['src_mask'] = jnp.ones((B, L), dtype=jnp.int32)
        d['norm_scale'] = jnp.ones((DIM,), jnp.float32)
        d['norm_bias'] = jnp.zeros((DIM,), jnp.float32)
        for i, nm in enumerate(['l', 'r', 'lg', 'rg', 'og']):
            d[f'W{nm}'] = jax.random.normal(ks[i + 1], (DIM, HID), jnp.float32) * 0.02
            d[f'b{nm}'] = jnp.zeros((HID,), jnp.float32)
        d['out_norm_scale'] = jnp.ones((HID,), jnp.float32)
        d['out_norm_bias'] = jnp.zeros((HID,), jnp.float32)
        d['Wo'] = jax.random.normal(ks[6], (HID, DIM), jnp.float32) * 0.02
        d['bo'] = jnp.zeros((DIM,), jnp.float32)
        return d
    _L1_conv_all = _L1_conv_setup()
    _L1_conv_in = {k: v for k, v in _L1_conv_all.items() if k in ('src_mask', 'norm_scale', 'norm_bias', 'Wl', 'bl', 'Wr', 'br', 'Wlg', 'blg', 'Wrg', 'brg', 'Wog', 'bog', 'out_norm_scale', 'out_norm_bias', 'Wo', 'bo')}
    del _L1_conv_all

    def _L2_conv_setup():
        import jax, jax.numpy as jnp
        import numpy as np
        B, L, DIM, HID, WIN = (1, 256, 32, 64, 4)

        def _ln(x, scale, bias, eps=1e-06):
            m = jnp.mean(x, axis=-1, keepdims=True)
            v = jnp.var(x, axis=-1, keepdims=True)
            return (x - m) / jnp.sqrt(v + eps) * scale + bias

        def _banded_ingoing(left, right, w):
            n = left.shape[1]
            ii = jnp.arange(n)
            offs = jnp.arange(-w, w + 1)
            rows = ii[:, None] + offs[None, :]
            valid = ((rows >= 0) & (rows < n)).astype(left.dtype)
            rows_c = jnp.clip(rows, 0, n - 1)
            Lb = left[:, rows_c, ii[:, None], :] * valid[None, :, :, None]
            out = jnp.zeros_like(right)
            for di, dd in enumerate(range(-w, w + 1)):
                if dd >= 0:
                    sh = jnp.pad(right[:, dd:], ((0, 0), (0, dd), (0, 0), (0, 0)))
                else:
                    sh = jnp.pad(right[:, :dd], ((0, 0), (-dd, 0), (0, 0), (0, 0)))
                out = out + Lb[:, :, di, None, :] * sh
            return out
        key = jax.random.key(seed)
        ks = jax.random.split(key, 8)
        d = {}
        d['x'] = jax.random.normal(ks[0], (B, L, L, DIM), dtype=jnp.float32)
        d['src_mask'] = jnp.ones((B, L), dtype=jnp.int32)
        d['norm_scale'] = jnp.ones((DIM,), jnp.float32)
        d['norm_bias'] = jnp.zeros((DIM,), jnp.float32)
        for i, nm in enumerate(['l', 'r', 'lg', 'rg', 'og']):
            d[f'W{nm}'] = jax.random.normal(ks[i + 1], (DIM, HID), jnp.float32) * 0.02
            d[f'b{nm}'] = jnp.zeros((HID,), jnp.float32)
        d['out_norm_scale'] = jnp.ones((HID,), jnp.float32)
        d['out_norm_bias'] = jnp.zeros((HID,), jnp.float32)
        d['Wo'] = jax.random.normal(ks[6], (HID, DIM), jnp.float32) * 0.02
        d['bo'] = jnp.zeros((DIM,), jnp.float32)
        return d
    _L2_conv_all = _L2_conv_setup()
    _L2_conv_in = {k: v for k, v in _L2_conv_all.items() if k in ('src_mask', 'norm_scale', 'norm_bias', 'Wl', 'bl', 'Wr', 'br', 'Wlg', 'blg', 'Wrg', 'brg', 'Wog', 'bog', 'out_norm_scale', 'out_norm_bias', 'Wo', 'bo')}
    del _L2_conv_all

    def _L3_conv_setup():
        import jax, jax.numpy as jnp
        import numpy as np

        def _mamba(xs, W_in, conv_w, conv_b, W_x, W_dt, b_dt, A_log, D_skip, W_out):
            di, d_conv = conv_w.shape
            d_state = A_log.shape[1]
            dtr = W_dt.shape[0]
            xz = xs @ W_in
            xi, z = jnp.split(xz, 2, axis=-1)
            xc = xi.transpose(0, 2, 1)
            k = conv_w[:, None, :]
            xc = jax.lax.conv_general_dilated(xc, k, window_strides=(1,), padding=[(d_conv - 1, 0)], dimension_numbers=('NCH', 'OIH', 'NCH'), feature_group_count=di)
            xc = jax.nn.silu(xc + conv_b[None, :, None]).transpose(0, 2, 1)
            dbl = xc @ W_x
            dt_r, Bc, Cc = jnp.split(dbl, [dtr, dtr + d_state], axis=-1)
            dt = jax.nn.softplus(dt_r @ W_dt + b_dt)
            A = -jnp.exp(A_log)

            def step(h, inp):
                x_t, dt_t, B_t, C_t = inp
                dA = jnp.exp(dt_t[:, :, None] * A)
                h = dA * h + dt_t[:, :, None] * B_t[:, None, :] * x_t[:, :, None]
                y = jnp.einsum('bds,bs->bd', h, C_t)
                return (h, y)
            h0 = jnp.zeros((xc.shape[0], di, d_state), xc.dtype)
            xsT = (xc.transpose(1, 0, 2), dt.transpose(1, 0, 2), Bc.transpose(1, 0, 2), Cc.transpose(1, 0, 2))
            _, yT = jax.lax.scan(step, h0, xsT)
            y = yT.transpose(1, 0, 2) + xc * D_skip
            y = y * jax.nn.silu(z)
            return y @ W_out
        key = jax.random.key(seed)
        B, T, N, Dm = (16, 48, 325, 32)
        d_state, d_conv, expand = (16, 4, 2)
        di = expand * Dm
        dtr = max(1, Dm // 16)
        ks = jax.random.split(key, 8)
        s = 0.02
        return {'x': jax.random.normal(ks[0], (B, T, N, Dm), dtype=jnp.float32), 'W_in': jax.random.normal(ks[1], (Dm, 2 * di), dtype=jnp.float32) * s, 'conv_w': jax.random.normal(ks[2], (di, d_conv), dtype=jnp.float32) * s, 'conv_b': jnp.zeros((di,), jnp.float32), 'W_x': jax.random.normal(ks[3], (di, dtr + 2 * d_state), dtype=jnp.float32) * s, 'W_dt': jax.random.normal(ks[4], (dtr, di), dtype=jnp.float32) * s, 'b_dt': jnp.full((di,), -4.0, jnp.float32) + jax.random.normal(ks[5], (di,), dtype=jnp.float32) * 0.1, 'A_log': jnp.log(jnp.broadcast_to(jnp.arange(1, d_state + 1, dtype=jnp.float32), (di, d_state))), 'D_skip': jnp.ones((di,), jnp.float32), 'W_out': jax.random.normal(ks[6], (di, Dm), dtype=jnp.float32) * s}
    _L3_conv_all = _L3_conv_setup()
    _L3_conv_in = {k: v for k, v in _L3_conv_all.items() if k in ('W_in', 'conv_w', 'conv_b', 'W_x', 'W_dt', 'b_dt', 'A_log', 'D_skip', 'W_out')}
    del _L3_conv_all
    return {'x': x, 'L0_conv_src_mask': _L0_conv_in['src_mask'], 'L0_conv_norm_scale': _L0_conv_in['norm_scale'], 'L0_conv_norm_bias': _L0_conv_in['norm_bias'], 'L0_conv_Wl': _L0_conv_in['Wl'], 'L0_conv_bl': _L0_conv_in['bl'], 'L0_conv_Wr': _L0_conv_in['Wr'], 'L0_conv_br': _L0_conv_in['br'], 'L0_conv_Wlg': _L0_conv_in['Wlg'], 'L0_conv_blg': _L0_conv_in['blg'], 'L0_conv_Wrg': _L0_conv_in['Wrg'], 'L0_conv_brg': _L0_conv_in['brg'], 'L0_conv_Wog': _L0_conv_in['Wog'], 'L0_conv_bog': _L0_conv_in['bog'], 'L0_conv_out_norm_scale': _L0_conv_in['out_norm_scale'], 'L0_conv_out_norm_bias': _L0_conv_in['out_norm_bias'], 'L0_conv_Wo': _L0_conv_in['Wo'], 'L0_conv_bo': _L0_conv_in['bo'], 'L1_conv_src_mask': _L1_conv_in['src_mask'], 'L1_conv_norm_scale': _L1_conv_in['norm_scale'], 'L1_conv_norm_bias': _L1_conv_in['norm_bias'], 'L1_conv_Wl': _L1_conv_in['Wl'], 'L1_conv_bl': _L1_conv_in['bl'], 'L1_conv_Wr': _L1_conv_in['Wr'], 'L1_conv_br': _L1_conv_in['br'], 'L1_conv_Wlg': _L1_conv_in['Wlg'], 'L1_conv_blg': _L1_conv_in['blg'], 'L1_conv_Wrg': _L1_conv_in['Wrg'], 'L1_conv_brg': _L1_conv_in['brg'], 'L1_conv_Wog': _L1_conv_in['Wog'], 'L1_conv_bog': _L1_conv_in['bog'], 'L1_conv_out_norm_scale': _L1_conv_in['out_norm_scale'], 'L1_conv_out_norm_bias': _L1_conv_in['out_norm_bias'], 'L1_conv_Wo': _L1_conv_in['Wo'], 'L1_conv_bo': _L1_conv_in['bo'], 'L2_conv_src_mask': _L2_conv_in['src_mask'], 'L2_conv_norm_scale': _L2_conv_in['norm_scale'], 'L2_conv_norm_bias': _L2_conv_in['norm_bias'], 'L2_conv_Wl': _L2_conv_in['Wl'], 'L2_conv_bl': _L2_conv_in['bl'], 'L2_conv_Wr': _L2_conv_in['Wr'], 'L2_conv_br': _L2_conv_in['br'], 'L2_conv_Wlg': _L2_conv_in['Wlg'], 'L2_conv_blg': _L2_conv_in['blg'], 'L2_conv_Wrg': _L2_conv_in['Wrg'], 'L2_conv_brg': _L2_conv_in['brg'], 'L2_conv_Wog': _L2_conv_in['Wog'], 'L2_conv_bog': _L2_conv_in['bog'], 'L2_conv_out_norm_scale': _L2_conv_in['out_norm_scale'], 'L2_conv_out_norm_bias': _L2_conv_in['out_norm_bias'], 'L2_conv_Wo': _L2_conv_in['Wo'], 'L2_conv_bo': _L2_conv_in['bo'], 'L3_conv_W_in': _L3_conv_in['W_in'], 'L3_conv_conv_w': _L3_conv_in['conv_w'], 'L3_conv_conv_b': _L3_conv_in['conv_b'], 'L3_conv_W_x': _L3_conv_in['W_x'], 'L3_conv_W_dt': _L3_conv_in['W_dt'], 'L3_conv_b_dt': _L3_conv_in['b_dt'], 'L3_conv_A_log': _L3_conv_in['A_log'], 'L3_conv_D_skip': _L3_conv_in['D_skip'], 'L3_conv_W_out': _L3_conv_in['W_out']}

def reference(x, L0_conv_src_mask, L0_conv_norm_scale, L0_conv_norm_bias, L0_conv_Wl, L0_conv_bl, L0_conv_Wr, L0_conv_br, L0_conv_Wlg, L0_conv_blg, L0_conv_Wrg, L0_conv_brg, L0_conv_Wog, L0_conv_bog, L0_conv_out_norm_scale, L0_conv_out_norm_bias, L0_conv_Wo, L0_conv_bo, L1_conv_src_mask, L1_conv_norm_scale, L1_conv_norm_bias, L1_conv_Wl, L1_conv_bl, L1_conv_Wr, L1_conv_br, L1_conv_Wlg, L1_conv_blg, L1_conv_Wrg, L1_conv_brg, L1_conv_Wog, L1_conv_bog, L1_conv_out_norm_scale, L1_conv_out_norm_bias, L1_conv_Wo, L1_conv_bo, L2_conv_src_mask, L2_conv_norm_scale, L2_conv_norm_bias, L2_conv_Wl, L2_conv_bl, L2_conv_Wr, L2_conv_br, L2_conv_Wlg, L2_conv_blg, L2_conv_Wrg, L2_conv_brg, L2_conv_Wog, L2_conv_bog, L2_conv_out_norm_scale, L2_conv_out_norm_bias, L2_conv_Wo, L2_conv_bo, L3_conv_W_in, L3_conv_conv_w, L3_conv_conv_b, L3_conv_W_x, L3_conv_W_dt, L3_conv_b_dt, L3_conv_A_log, L3_conv_D_skip, L3_conv_W_out):
    import jax
    import jax.numpy as jnp

    def _L0_conv_ref(x, src_mask, norm_scale, norm_bias, Wl, bl, Wr, br, Wlg, blg, Wrg, brg, Wog, bog, out_norm_scale, out_norm_bias, Wo, bo):
        import jax, jax.numpy as jnp
        import numpy as np
        B, L, DIM, HID, WIN = (1, 256, 32, 64, 4)

        def _ln(x, scale, bias, eps=1e-06):
            m = jnp.mean(x, axis=-1, keepdims=True)
            v = jnp.var(x, axis=-1, keepdims=True)
            return (x - m) / jnp.sqrt(v + eps) * scale + bias

        def _banded_ingoing(left, right, w):
            n = left.shape[1]
            ii = jnp.arange(n)
            offs = jnp.arange(-w, w + 1)
            rows = ii[:, None] + offs[None, :]
            valid = ((rows >= 0) & (rows < n)).astype(left.dtype)
            rows_c = jnp.clip(rows, 0, n - 1)
            Lb = left[:, rows_c, ii[:, None], :] * valid[None, :, :, None]
            out = jnp.zeros_like(right)
            for di, dd in enumerate(range(-w, w + 1)):
                if dd >= 0:
                    sh = jnp.pad(right[:, dd:], ((0, 0), (0, dd), (0, 0), (0, 0)))
                else:
                    sh = jnp.pad(right[:, :dd], ((0, 0), (-dd, 0), (0, 0), (0, 0)))
                out = out + Lb[:, :, di, None, :] * sh
            return out
        m = src_mask.astype(jnp.float32)
        mask = (m[:, :, None] * m[:, None, :])[..., None]
        xn = _ln(x, norm_scale, norm_bias)
        left = (xn @ Wl + bl) * mask * jax.nn.sigmoid(xn @ Wlg + blg)
        right = (xn @ Wr + br) * mask * jax.nn.sigmoid(xn @ Wrg + brg)
        out_gate = jax.nn.sigmoid(xn @ Wog + bog)
        out = _banded_ingoing(left, right, WIN)
        out = _ln(out, out_norm_scale, out_norm_bias) * out_gate
        return out @ Wo + bo

    def _L1_conv_ref(x, src_mask, norm_scale, norm_bias, Wl, bl, Wr, br, Wlg, blg, Wrg, brg, Wog, bog, out_norm_scale, out_norm_bias, Wo, bo):
        import jax, jax.numpy as jnp
        import numpy as np
        B, L, DIM, HID, WIN = (1, 256, 32, 64, 4)

        def _ln(x, scale, bias, eps=1e-06):
            m = jnp.mean(x, axis=-1, keepdims=True)
            v = jnp.var(x, axis=-1, keepdims=True)
            return (x - m) / jnp.sqrt(v + eps) * scale + bias

        def _banded_ingoing(left, right, w):
            n = left.shape[1]
            ii = jnp.arange(n)
            offs = jnp.arange(-w, w + 1)
            rows = ii[:, None] + offs[None, :]
            valid = ((rows >= 0) & (rows < n)).astype(left.dtype)
            rows_c = jnp.clip(rows, 0, n - 1)
            Lb = left[:, rows_c, ii[:, None], :] * valid[None, :, :, None]
            out = jnp.zeros_like(right)
            for di, dd in enumerate(range(-w, w + 1)):
                if dd >= 0:
                    sh = jnp.pad(right[:, dd:], ((0, 0), (0, dd), (0, 0), (0, 0)))
                else:
                    sh = jnp.pad(right[:, :dd], ((0, 0), (-dd, 0), (0, 0), (0, 0)))
                out = out + Lb[:, :, di, None, :] * sh
            return out
        m = src_mask.astype(jnp.float32)
        mask = (m[:, :, None] * m[:, None, :])[..., None]
        xn = _ln(x, norm_scale, norm_bias)
        left = (xn @ Wl + bl) * mask * jax.nn.sigmoid(xn @ Wlg + blg)
        right = (xn @ Wr + br) * mask * jax.nn.sigmoid(xn @ Wrg + brg)
        out_gate = jax.nn.sigmoid(xn @ Wog + bog)
        out = _banded_ingoing(left, right, WIN)
        out = _ln(out, out_norm_scale, out_norm_bias) * out_gate
        return out @ Wo + bo

    def _L2_conv_ref(x, src_mask, norm_scale, norm_bias, Wl, bl, Wr, br, Wlg, blg, Wrg, brg, Wog, bog, out_norm_scale, out_norm_bias, Wo, bo):
        import jax, jax.numpy as jnp
        import numpy as np
        B, L, DIM, HID, WIN = (1, 256, 32, 64, 4)

        def _ln(x, scale, bias, eps=1e-06):
            m = jnp.mean(x, axis=-1, keepdims=True)
            v = jnp.var(x, axis=-1, keepdims=True)
            return (x - m) / jnp.sqrt(v + eps) * scale + bias

        def _banded_ingoing(left, right, w):
            n = left.shape[1]
            ii = jnp.arange(n)
            offs = jnp.arange(-w, w + 1)
            rows = ii[:, None] + offs[None, :]
            valid = ((rows >= 0) & (rows < n)).astype(left.dtype)
            rows_c = jnp.clip(rows, 0, n - 1)
            Lb = left[:, rows_c, ii[:, None], :] * valid[None, :, :, None]
            out = jnp.zeros_like(right)
            for di, dd in enumerate(range(-w, w + 1)):
                if dd >= 0:
                    sh = jnp.pad(right[:, dd:], ((0, 0), (0, dd), (0, 0), (0, 0)))
                else:
                    sh = jnp.pad(right[:, :dd], ((0, 0), (-dd, 0), (0, 0), (0, 0)))
                out = out + Lb[:, :, di, None, :] * sh
            return out
        m = src_mask.astype(jnp.float32)
        mask = (m[:, :, None] * m[:, None, :])[..., None]
        xn = _ln(x, norm_scale, norm_bias)
        left = (xn @ Wl + bl) * mask * jax.nn.sigmoid(xn @ Wlg + blg)
        right = (xn @ Wr + br) * mask * jax.nn.sigmoid(xn @ Wrg + brg)
        out_gate = jax.nn.sigmoid(xn @ Wog + bog)
        out = _banded_ingoing(left, right, WIN)
        out = _ln(out, out_norm_scale, out_norm_bias) * out_gate
        return out @ Wo + bo

    def _L3_conv_ref(x, W_in, conv_w, conv_b, W_x, W_dt, b_dt, A_log, D_skip, W_out):
        import jax, jax.numpy as jnp
        import numpy as np

        def _mamba(xs, W_in, conv_w, conv_b, W_x, W_dt, b_dt, A_log, D_skip, W_out):
            di, d_conv = conv_w.shape
            d_state = A_log.shape[1]
            dtr = W_dt.shape[0]
            xz = xs @ W_in
            xi, z = jnp.split(xz, 2, axis=-1)
            xc = xi.transpose(0, 2, 1)
            k = conv_w[:, None, :]
            xc = jax.lax.conv_general_dilated(xc, k, window_strides=(1,), padding=[(d_conv - 1, 0)], dimension_numbers=('NCH', 'OIH', 'NCH'), feature_group_count=di)
            xc = jax.nn.silu(xc + conv_b[None, :, None]).transpose(0, 2, 1)
            dbl = xc @ W_x
            dt_r, Bc, Cc = jnp.split(dbl, [dtr, dtr + d_state], axis=-1)
            dt = jax.nn.softplus(dt_r @ W_dt + b_dt)
            A = -jnp.exp(A_log)

            def step(h, inp):
                x_t, dt_t, B_t, C_t = inp
                dA = jnp.exp(dt_t[:, :, None] * A)
                h = dA * h + dt_t[:, :, None] * B_t[:, None, :] * x_t[:, :, None]
                y = jnp.einsum('bds,bs->bd', h, C_t)
                return (h, y)
            h0 = jnp.zeros((xc.shape[0], di, d_state), xc.dtype)
            xsT = (xc.transpose(1, 0, 2), dt.transpose(1, 0, 2), Bc.transpose(1, 0, 2), Cc.transpose(1, 0, 2))
            _, yT = jax.lax.scan(step, h0, xsT)
            y = yT.transpose(1, 0, 2) + xc * D_skip
            y = y * jax.nn.silu(z)
            return y @ W_out
        B, T, N, Dm = x.shape
        xs = x.transpose(0, 2, 1, 3).reshape(B * N, T, Dm)
        out = _mamba(xs, W_in, conv_w, conv_b, W_x, W_dt, b_dt, A_log, D_skip, W_out)
        return out.reshape(B, N, T, Dm).transpose(0, 2, 1, 3)

    def _gn(v, G=32, eps=1e-05):
        B_, H_, W_, C_ = v.shape
        g = v.reshape(B_, H_, W_, G, C_ // G)
        m = jnp.mean(g, axis=(1, 2, 4), keepdims=True)
        s = jnp.var(g, axis=(1, 2, 4), keepdims=True)
        return ((g - m) / jnp.sqrt(s + eps)).reshape(v.shape)

    def _ln_c(v, eps=1e-06):
        m = jnp.mean(v, axis=-1, keepdims=True)
        s = jnp.var(v, axis=-1, keepdims=True)
        return (v - m) / jnp.sqrt(s + eps)

    def _ln_t(v, eps=1e-05):
        m = jnp.mean(v, axis=-1, keepdims=True)
        s = jnp.var(v, axis=-1, keepdims=True)
        return (v - m) / jnp.sqrt(s + eps)

    def _to_tokens(v):
        B_, H_, W_, C_ = v.shape
        return v.reshape(B_, H_ * W_, C_)

    def _from_tokens(t, like):
        return t.reshape(like.shape)
    x = x + _L0_conv_ref(_gn(x), L0_conv_src_mask, L0_conv_norm_scale, L0_conv_norm_bias, L0_conv_Wl, L0_conv_bl, L0_conv_Wr, L0_conv_br, L0_conv_Wlg, L0_conv_blg, L0_conv_Wrg, L0_conv_brg, L0_conv_Wog, L0_conv_bog, L0_conv_out_norm_scale, L0_conv_out_norm_bias, L0_conv_Wo, L0_conv_bo)
    x = x + _L1_conv_ref(_gn(x), L1_conv_src_mask, L1_conv_norm_scale, L1_conv_norm_bias, L1_conv_Wl, L1_conv_bl, L1_conv_Wr, L1_conv_br, L1_conv_Wlg, L1_conv_blg, L1_conv_Wrg, L1_conv_brg, L1_conv_Wog, L1_conv_bog, L1_conv_out_norm_scale, L1_conv_out_norm_bias, L1_conv_Wo, L1_conv_bo)
    x = x + _L2_conv_ref(_gn(x), L2_conv_src_mask, L2_conv_norm_scale, L2_conv_norm_bias, L2_conv_Wl, L2_conv_bl, L2_conv_Wr, L2_conv_br, L2_conv_Wlg, L2_conv_blg, L2_conv_Wrg, L2_conv_brg, L2_conv_Wog, L2_conv_bog, L2_conv_out_norm_scale, L2_conv_out_norm_bias, L2_conv_Wo, L2_conv_bo)
    x = x + _L3_conv_ref(_gn(x), L3_conv_W_in, L3_conv_conv_w, L3_conv_conv_b, L3_conv_W_x, L3_conv_W_dt, L3_conv_b_dt, L3_conv_A_log, L3_conv_D_skip, L3_conv_W_out)
    return x

_drawn_inputs = setup_inputs


def setup_inputs(seed=0):
    import zlib

    import numpy as np

    out = dict(_drawn_inputs(seed))
    spreads = {'L0_conv_norm_scale': (1.0, 0.6),
     'L0_conv_norm_bias': (0.0, 0.792),
     'L0_conv_bl': (0.0, 0.1),
     'L0_conv_br': (0.0, 0.1),
     'L0_conv_blg': (0.0, 2.0),
     'L0_conv_brg': (0.0, 2.0),
     'L0_conv_bog': (0.0, 0.8),
     'L0_conv_out_norm_scale': (1.0, 0.6),
     'L0_conv_out_norm_bias': (0.0, 0.8),
     'L0_conv_bo': (0.0, 0.1),
     'L1_conv_norm_scale': (1.0, 0.6),
     'L1_conv_norm_bias': (0.0, 0.567),
     'L1_conv_bl': (0.0, 0.1),
     'L1_conv_br': (0.0, 0.1),
     'L1_conv_blg': (0.0, 0.8),
     'L1_conv_brg': (0.0, 0.8),
     'L1_conv_bog': (0.0, 0.8),
     'L1_conv_out_norm_scale': (1.0, 0.6),
     'L1_conv_out_norm_bias': (0.0, 0.8),
     'L1_conv_bo': (0.0, 0.1),
     'L2_conv_norm_scale': (1.0, 0.6),
     'L2_conv_norm_bias': (0.0, 0.8),
     'L2_conv_bl': (0.0, 0.1),
     'L2_conv_br': (0.0, 0.1),
     'L2_conv_blg': (0.0, 2.0),
     'L2_conv_brg': (0.0, 2.0),
     'L2_conv_bog': (0.0, 2.0),
     'L2_conv_out_norm_scale': (1.0, 0.6),
     'L2_conv_out_norm_bias': (0.0, 0.8),
     'L2_conv_bo': (0.0, 0.1),
     'L3_conv_conv_b': (0.0, 0.8),
     'L3_conv_D_skip': (1.0, 0.6)}
    factors = {'L0_conv_Wlg': 8.0,
     'L0_conv_Wrg': 8.0,
     'L0_conv_Wog': 8.0,
     'L1_conv_Wlg': 8.0,
     'L1_conv_Wrg': 8.0,
     'L1_conv_Wog': 8.0,
     'L2_conv_Wlg': 8.0,
     'L2_conv_Wrg': 8.0,
     'L2_conv_Wog': 8.0,
     'L3_conv_W_in': 8.0,
     'L3_conv_conv_w': 8.0,
     'L3_conv_W_x': 8.0,
     'L3_conv_b_dt': 8.0,
     'L3_conv_A_log': 8.0,
     'L3_conv_W_out': 8.0}
    for name, (base, spread) in spreads.items():
        noise = np.random.default_rng([zlib.crc32(name.encode()), seed]).standard_normal(out[name].shape)
        drawn = base * np.exp(spread * noise) if base else spread * noise
        out[name] = jnp.asarray(drawn.astype(out[name].dtype))
    for name, factor in factors.items():
        out[name] = (out[name] * factor).astype(out[name].dtype)
    return out
```

```python
from contextlib import ExitStack

import concourse.bass as bass
from concourse import mybir

P = 128
F32 = mybir.dt.float32
BF16 = mybir.dt.bfloat16
I32 = mybir.dt.int32
ALU = mybir.AluOpType
ACT = mybir.ActivationFunctionType


def mamba_layer(nc, x_cm, w, out):
    T, N = x_cm.shape[1], x_cm.shape[2]
    DM = 32
    S = 16
    TAPS = 4
    G = 4
    NG = N // G
    SUB = 2
    CHUNKS = NG // SUB
    HALF = SUB * T
    W = 2 * HALF
    BLK = W // P
    DA_RING = H_RING = C_RING = 4
    LAG = 2

    with ExitStack() as ctx:
        def sb(name, shape, dt=F32):
            return ctx.enter_context(nc.sbuf_tensor("m_" + name, shape, dt))

        def ps(name, shape, dt=F32):
            return ctx.enter_context(nc.psum_tensor("m_" + name, shape, dt))

        def sem(name):
            return ctx.enter_context(nc.semaphore("m_" + name))

        xm = sb("xm", [P, T, NG])
        ident = sb("ident", [P, P])
        avg = sb("avg", [P, P])
        eps = sb("eps", [P, 1])
        stats = sb("stats", [P, T * NG // 512, 6])
        mean_var = sb("mean_var", [P, 2])
        group_dev = sb("group_dev", [P, 2])
        gn_scale = sb("gn_scale", [P, 1])
        gn_bias = sb("gn_bias", [P, 1])
        w_in = sb("w_in", [P, 2, P])
        conv_w = sb("conv_w", [P, TAPS, P])
        w_conv = sb("w_conv", [P, 2, TAPS, P])
        w_z = sb("w_z", [P, 2, P])
        wx_dt = sb("wx_dt", [4, P])
        w_dt = sb("w_dt", [4, P])
        w_dt2 = sb("w_dt2", [P, P])
        w_bc = sb("w_bc", [P, 2, 32])
        w_out = sb("w_out", [P, 2 * DM])
        vecs = sb("vecs", [P, 3])
        conv_b, b_dt, d_skip = (vecs[:, i:i + 1] for i in range(3))
        a_log = sb("a_log", [P, S])
        a_neg = sb("a_neg", [P, S])
        sel = sb("sel", [96, S, P], BF16)

        xg = [sb(f"xg{i}", [P, SUB, TAPS - 1 + T]) for i in range(2)]
        raw = sb("raw", [P, 4 * HALF])
        act = [sb(f"act{i}", [P, 4 * HALF]) for i in range(2)]
        sp_x = sb("sp_x", [P, W])
        sp_v = sb("sp_v", [P, W])
        dt = [sb(f"dt{i}", [P, W]) for i in range(2)]
        dtx = [sb(f"dtx{i}", [P, W]) for i in range(2)]
        bc_hi = sb("bc_hi", [P, HALF], BF16)
        bc_mid = sb("bc_mid", [P, HALF], BF16)
        bc_lo = sb("bc_lo", [P, HALF], BF16)
        bc_rest = sb("bc_rest", [P, HALF])
        b_parts = [sb(f"b_parts{i}", [96, W], BF16) for i in range(2)]
        c_parts = [sb(f"c_parts{i}", [96, W], BF16) for i in range(2)]
        da = sb("da", [P, DA_RING, 2 * SUB, T])
        cs = sb("cs", [P, C_RING, W])
        hs = sb("hs", [P, H_RING, W])
        yt = sb("yt", [P, W])
        gated = sb("gated", [P, W])
        fin = sb("fin", [P, HALF])
        sel_f32 = raw[0:96, :].rearrange("p (s c) -> p s c", c=P)
        sp_u, sp_l = raw[:, 0:W], raw[:, W:2 * W]

        pb = [ps(f"pb{i}", [P, W]) for i in range(2)]
        pc = ps("pc", [P, HALF])
        misc = ps("misc", [P, HALF])
        py = ps("py", [P, W])

        loaded, zeroed, stat_done, avg_done, gn_step, gn_log, gn_ready = (
            sem(n) for n in ("loaded", "zeroed", "stat_done", "avg_done", "gn_step", "gn_log", "gn_ready"))
        w_ready, wdt_ready, wdt_copied, a_exp, a_ready = (
            sem(n) for n in ("w_ready", "wdt_ready", "wdt_copied", "a_exp", "a_ready"))

        with nc.Block() as block:
            @block.sync
            def _(sp):
                for g in range(G):
                    for q in range(4):
                        tt = slice(q * T // 4, (q + 1) * T // 4)
                        sp.dma_start(xm[g * DM:(g + 1) * DM, tt, :],
                                     x_cm[:, tt, g * NG:(g + 1) * NG]).then_inc(loaded, 16)

            @block.scalar
            def _(a):
                for dst, name in ((avg, "avg"), (ident, "ident"), (w_in, "w_in"), (conv_w, "conv_w"), (w_z, "w_z"),
                                  (wx_dt, "wx_dt"), (w_dt, "w_dt"), (w_bc, "w_bc"), (w_out, "w_out"),
                                  (vecs, "vecs"), (a_log, "a_log"), (sel_f32, "sel")):
                    idx = tuple(slice(None) for _ in dst.shape)
                    a.dma_start(dst[idx], w[name]).then_inc(w_ready, 16)
                a.wait_ge(w_ready, 12 * 16)
                nc.scalar.activation(a_neg[:, :], a_log[:, :], ACT.Exp).then_inc(a_exp, 1)
                a.wait_ge(avg_done, 2)
                a.wait_ge(zeroed, 1)
                nc.scalar.activation(gn_scale[:, :], misc[:, 1:2], ACT.Ln, bias=eps[:, 0:1]).then_inc(gn_log, 1)
                a.wait_ge(gn_log, 1)
                nc.scalar.activation(gn_scale[:, :], gn_scale[:, :], ACT.Exp, scale=-0.5).then_inc(gn_ready, 1)
                a.wait_ge(wdt_ready, 1)
                nc.scalar.copy(w_dt2[:, :], pc[:, 0:P]).then_inc(wdt_copied, 1)

            @block.tensor
            def _(pe):
                pe.wait_ge(w_ready, 12 * 16)
                nc.tensor.matmul(pc[:, 0:P], wx_dt[:, :], w_dt[:, :], start=True, stop=True).then_inc(wdt_ready, 1)
                pe.wait_ge(stat_done, 1)
                nc.tensor.matmul(misc[:, 0:1], avg[:, :], mean_var[:, 0:1], start=True, stop=True).then_inc(avg_done, 1)
                pe.wait_ge(stat_done, 2)
                nc.tensor.matmul(misc[:, 1:2], avg[:, :], group_dev[:, 1:2], start=True, stop=True).then_inc(avg_done, 1)

            @block.vector
            def _(v):
                nc.vector.memset(eps[:, :], 1e-5).then_inc(zeroed, 1)
                for i in range(2):
                    nc.vector.memset(xg[i][:, :, 0:TAPS - 1], 0.0)
                nc.vector.memset(da[:, :, :, 0:1], 0.0)
                v.wait_ge(w_ready, 12 * 16)
                for q in range(2):
                    for tap in range(TAPS):
                        nc.vector.tensor_tensor(w_conv[:, q, tap, :], w_in[:, q, :], conv_w[:, tap, :], ALU.mult)
                nc.vector.tensor_copy(sel[:, :, :], sel_f32)
                v.wait_ge(a_exp, 1)
                nc.vector.tensor_scalar(a_neg[:, :], a_neg[:, :], -1.0, None, ALU.mult).then_inc(a_ready, 1)
                v.wait_ge(loaded, 16 * 16)
                for j in range(T * NG // 512):
                    n = 512 // NG
                    last = nc.vector.bn_stats(stats[:, j, :], xm[:, j * n:(j + 1) * n, :])
                last.then_inc(gn_step, 1)
                v.wait_ge(gn_step, 1)
                nc.vector.bn_aggr(mean_var[:, :], stats[:, :, :]).then_inc(stat_done, 1)
                v.wait_ge(avg_done, 1)
                v.wait_ge(stat_done, 1)
                nc.vector.tensor_tensor(group_dev[:, 0:1], misc[:, 0:1], mean_var[:, 0:1], ALU.subtract).then_inc(a_ready, 1)
                v.wait_ge(a_ready, 2)
                nc.vector.scalar_tensor_tensor(group_dev[:, 1:2], group_dev[:, 0:1], group_dev[:, 0:1],
                                               mean_var[:, 1:2], ALU.mult, ALU.add).then_inc(stat_done, 1)
                v.wait_ge(gn_ready, 1)
                nc.vector.scalar_tensor_tensor(gn_bias[:, :], misc[:, 0:1], -1.0, gn_scale[:, :],
                                               ALU.mult, ALU.mult).then_inc(gn_ready, 1)

        names = ("raw_ready", "raw_evac", "silu_done", "dt_psum", "spx_ready", "sp_abs", "sp_exp", "sp_act_done", "sp_step",
                 "dt_done", "bc_psum", "bc_hi_done", "bc_step", "bc_mid_done", "bc_done", "parts_ready", "xg_ready",
                 "xg_used", "b_ready", "c_ready", "c_copied", "da_ready", "u_done", "h_ready", "hc_ready", "hc_used",
                 "y_copied", "yb_ready", "yb_used", "y_gated", "o_ready", "fin_done", "stored")
        (raw_ready, raw_evac, silu_done, dt_psum, spx_ready, sp_abs, sp_exp, sp_act_done, sp_step,
         dt_done, bc_psum, bc_hi_done, bc_step, bc_mid_done, bc_done, parts_ready, xg_ready,
         xg_used, b_ready, c_ready, c_copied, da_ready, u_done, h_ready, hc_ready, hc_used,
         y_copied, yb_ready, yb_used, y_gated, o_ready, fin_done, stored) = map(sem, names)

        POST_AT = {2: ["copy_y"], 3: ["yb0"], 4: ["yb1"], 5: ["out"], 6: ["store"]}
        PRE_AT = {1: ["xg"], 7: ["x0"], 8: ["x1", "z0"], 9: ["z1", "silu"], 10: ["dt0", "dt1"], 11: ["bc"], 12: ["softplus"]}
        POST = [op for s in sorted(POST_AT) for op in POST_AT[s]]
        PRE = [op for s in sorted(PRE_AT) for op in PRE_AT[s]]

        def ops_at(s, first, last):
            return ([] if first else POST_AT.get(s, [])), ([] if last else PRE_AT.get(s, []))

        def schedule(eng, pre, steps, post):
            def chunk(k, par, first=False, last=False):
                for s in range(S):
                    steps(k, par, s, first)
                    after, before = ops_at(s, first, last)
                    for op in after:
                        post(k - 1, 1 - par, op, first)
                    for op in before:
                        pre(k + 1, 1 - par, op)
            for op in PRE:
                pre(0, 0, op)
            chunk(0, 0, first=True)
            with eng.Fori(1, CHUNKS - 2, 2) as k:
                chunk(k, 1)
                chunk(k + 1, 0)
            chunk(CHUNKS - 1, 1, last=True)

        with nc.Block() as block:
            @block.tensor
            def _(pe):
                def pre(k, par, op):
                    if op in ("x0", "x1", "z0", "z1"):
                        i = ("x0", "x1", "z0", "z1").index(op)
                        if i == 0:
                            pe.wait_ge(xg_ready, k + 1)
                            if not isinstance(k, int) or k > 1:
                                pe.wait_ge(fin_done, k - 1)
                        else:
                            pe.wait_ge(raw_evac, 4 * k + i)
                        q = i % 2
                        if i < 2:
                            for tap in range(TAPS):
                                m = nc.tensor.matmul(misc[:, :], w_conv[:, q, tap, :], xg[par][:, :, tap:tap + T],
                                                     start=(tap == 0), stop=(tap == TAPS - 1))
                        else:
                            m = nc.tensor.matmul(misc[:, :], w_z[:, q, :], xg[par][:, :, TAPS - 1:TAPS - 1 + T],
                                                 start=True, stop=True)
                        m.then_inc(raw_ready, 1)
                    elif op in ("dt0", "dt1"):
                        q = int(op[2])
                        if q == 0:
                            pe.wait_ge(raw_evac, 4 * k + 4)
                            pe.wait_ge(silu_done, k + 1)
                        else:
                            pe.wait_ge(spx_ready, 2 * k + 1)
                        nc.tensor.matmul(misc[:, :], w_dt2[:, :], act[par][:, q * HALF:(q + 1) * HALF],
                                         start=True, stop=True).then_inc(dt_psum, 1)
                    elif op == "bc":
                        pe.wait_ge(spx_ready, 2 * k + 2)
                        for bc in range(2):
                            for q in range(2):
                                o = 64 * bc + 32 * q
                                m = nc.tensor.matmul(misc[o:o + 32, :], w_bc[:, bc, :],
                                                     act[par][:, q * HALF:(q + 1) * HALF], start=True, stop=True)
                        m.then_inc(bc_psum, 1)

                def sum_states(k, par, s):
                    g = S * k + s
                    pe.wait_ge(hc_ready, g + 1)
                    if s == 0 and (not isinstance(k, int) or k > 0):
                        pe.wait_ge(y_copied, k)
                    for b in range(BLK):
                        m = nc.tensor.matmul(py[:, b * P:(b + 1) * P], hs[:, s % H_RING, b * P:(b + 1) * P], ident[:, :],
                                             is_transpose=True, start=(s == 0 and b % 4 == 0),
                                             stop=(s == S - 1 and b % 4 == 3), skip_group_check=True)
                    m.then_inc(hc_used, 1)

                def steps(k, par, s, first):
                    g = S * k + s
                    if s == 0:
                        pe.wait_ge(parts_ready, 12 * 16 * (k + 1))
                    if not (first and s < 2):
                        pe.wait_ge(h_ready, g - 1)
                    for q in range(2):
                        m = nc.tensor.matmul(pb[s % 2][:, q * HALF:(q + 1) * HALF], sel[:, s, :],
                                             b_parts[par][:, q * HALF:(q + 1) * HALF], start=True, stop=True)
                    m.then_inc(b_ready, 1)
                    for q in range(2):
                        if not (first and s == 0 and q == 0):
                            pe.wait_ge(c_copied, 2 * g + q)
                        nc.tensor.matmul(pc[:, :], sel[:, s, :], c_parts[par][:, q * HALF:(q + 1) * HALF],
                                         start=True, stop=True).then_inc(c_ready, 1)
                    if s >= LAG:
                        sum_states(k, par, s - LAG)
                    elif not first:
                        sum_states(k - 1, 1 - par, S - LAG + s)

                def post(k, par, op, first=False):
                    if op in ("yb0", "yb1"):
                        q = int(op[2])
                        if q == 0:
                            pe.wait_ge(y_copied, k + 1)
                            pe.wait_ge(bc_done, k + 1 + (1 if not (isinstance(k, int) and k == CHUNKS - 1) else 0))
                        else:
                            pe.wait_ge(yb_used, 2 * k + 1)
                        for b in range(4):
                            m = nc.tensor.matmul(misc[:, b * P:(b + 1) * P], yt[:, (4 * q + b) * P:(4 * q + b + 1) * P],
                                                 ident[:, :], is_transpose=True, start=(b == 0), stop=(b == 3),
                                                 skip_group_check=True)
                        m.then_inc(yb_ready, 1)
                    elif op == "out":
                        pe.wait_ge(yb_used, 2 * k + 2)
                        pe.wait_ge(y_gated, k + 1)
                        for q in range(2):
                            m = nc.tensor.matmul(misc[64 * q:64 * q + 64, :], w_out[:, :],
                                                 gated[:, q * HALF:(q + 1) * HALF], start=True, stop=True)
                        m.then_inc(o_ready, 1)

                schedule(pe, pre, steps, post)
                for s in range(S - LAG, S):
                    sum_states(CHUNKS - 1, 1, s)
                for op in POST:
                    post(CHUNKS - 1, 1, op)

            @block.scalar
            def _(a):
                def pre(k, par, op):
                    if op == "xg":
                        nc.scalar.activation(xg[par][:, :, TAPS - 1:TAPS - 1 + T],
                                             xm[:, :, bass.ds(SUB * k, SUB)].rearrange("p t n -> p n t"),
                                             ACT.Identity, bias=gn_bias[:, 0:1], scale=gn_scale[:, 0:1]).then_inc(xg_ready, 1)
                    elif op in ("x0", "x1", "z0", "z1"):
                        i = ("x0", "x1", "z0", "z1").index(op)
                        a.wait_ge(raw_ready, 4 * k + i + 1)
                        if i == 0 and (not isinstance(k, int) or k > 0):
                            a.wait_ge(dt_done, k)
                        dst = raw[:, i * HALF:(i + 1) * HALF]
                        if i < 2:
                            nc.scalar.activation(dst, misc[:, :], ACT.Identity, bias=conv_b).then_inc(raw_evac, 1)
                        else:
                            nc.scalar.copy(dst, misc[:, :]).then_inc(raw_evac, 1)
                    elif op == "silu":
                        a.wait_ge(raw_evac, 4 * k + 4)
                        if not isinstance(k, int) or k > 1:
                            a.wait_ge(y_gated, k - 1)
                        nc.scalar.activation(act[par][:, :], raw[:, :], ACT.Silu).then_inc(silu_done, 1)
                    elif op in ("dt0", "dt1"):
                        q = int(op[2])
                        a.wait_ge(dt_psum, 2 * k + q + 1)
                        nc.scalar.activation(sp_x[:, q * HALF:(q + 1) * HALF], misc[:, :], ACT.Identity,
                                             bias=b_dt).then_inc(spx_ready, 1)
                    elif op == "bc":
                        a.wait_ge(bc_psum, k + 1)
                        if not isinstance(k, int) or k > 0:
                            a.wait_ge(parts_ready, 12 * 16 * k)
                        nc.scalar.copy(bc_hi[:, :], misc[:, :]).then_inc(bc_hi_done, 1)
                    elif op == "softplus":
                        a.wait_ge(spx_ready, 2 * k + 2)
                        a.wait_ge(silu_done, k + 1)
                        nc.scalar.activation(sp_u, sp_x[:, :], ACT.Abs).then_inc(sp_abs, 1)
                        a.wait_ge(sp_abs, k + 1)
                        nc.scalar.activation(sp_u, sp_u, ACT.Exp, scale=-1.0).then_inc(sp_exp, 1)
                        a.wait_ge(sp_exp, k + 1)
                        nc.scalar.activation(sp_l, sp_u, ACT.Ln, bias=1.0)
                        nc.scalar.activation(sp_v[:, :], sp_u, ACT.Identity, bias=1.0).then_inc(sp_act_done, 1)

                def steps(k, par, s, first):
                    g = S * k + s
                    if s == 0:
                        a.wait_ge(dt_done, k + 1)
                    if not (first and s < DA_RING):
                        a.wait_ge(h_ready, g - DA_RING + 1)
                    nc.scalar.activation(da[:, s % DA_RING, :, 1:T],
                                         dt[par][:, :].rearrange("p (r t) -> p r t", t=T)[:, :, 1:T],
                                         ACT.Exp, scale=a_neg[:, s:s + 1]).then_inc(da_ready, 1)
                    for q in range(2):
                        a.wait_ge(c_ready, 2 * g + q + 1)
                        if q == 0 and not (first and s < C_RING):
                            a.wait_ge(hc_ready, g - C_RING + 1)
                        nc.scalar.copy(cs[:, s % C_RING, q * HALF:(q + 1) * HALF], pc[:, :]).then_inc(c_copied, 1)

                def post(k, par, op, first=False):
                    if op == "copy_y":
                        a.wait_ge(hc_used, S * (k + 1))
                        if not isinstance(k, int) or k > 0:
                            a.wait_ge(yb_ready, 2 * k)
                        nc.scalar.copy(yt[:, :], py[:, :]).then_inc(y_copied, 1)
                    elif op == "store":
                        a.wait_ge(fin_done, k + 1)
                        for g in range(G):
                            a.dma_start(out[:, bass.ds(SUB * k + g * NG, SUB), :],
                                        fin[DM * g:DM * g + DM, :].rearrange("p (n t) -> p n t", n=SUB)).then_inc(stored, 16)

                schedule(a, pre, steps, post)
                for op in POST:
                    post(CHUNKS - 1, 1, op)

            @block.vector
            def _(v):
                def pre(k, par, op):
                    if op == "bc":
                        v.wait_ge(bc_hi_done, k + 1)
                        nc.vector.tensor_tensor(bc_rest[:, :], misc[:, :], bc_hi[:, :], ALU.subtract).then_inc(bc_done, 1)
                        v.wait_ge(bc_done, k + 1)
                        nc.vector.tensor_copy(bc_mid[:, :], bc_rest[:, :]).then_inc(bc_mid_done, 1)
                        v.wait_ge(bc_mid_done, k + 1)
                        nc.vector.tensor_tensor(bc_lo[:, :], bc_rest[:, :], bc_mid[:, :], ALU.subtract).then_inc(bc_step, 1)
                    elif op == "softplus":
                        v.wait_ge(sp_act_done, k + 1)
                        nc.vector.scalar_tensor_tensor(sp_v[:, :], sp_v[:, :], 1.0, sp_u, ALU.subtract,
                                                       ALU.subtract).then_inc(sp_step, 1)
                        v.wait_ge(sp_step, 3 * k + 1)
                        nc.vector.tensor_tensor(sp_l, sp_l, sp_v[:, :], ALU.subtract).then_inc(sp_step, 1)
                        v.wait_ge(sp_step, 3 * k + 2)
                        nc.vector.scalar_tensor_tensor(dt[par][:, :], sp_x[:, :], 0.0, sp_l, ALU.max,
                                                       ALU.add).then_inc(sp_step, 1)
                        v.wait_ge(sp_step, 3 * k + 3)
                        nc.vector.tensor_tensor(dtx[par][:, :], dt[par][:, :], act[par][:, 0:W], ALU.mult).then_inc(dt_done, 1)

                def steps(k, par, s, first):
                    g = S * k + s
                    if s == 0:
                        v.wait_ge(dt_done, k + 1)
                    v.wait_ge(b_ready, g + 1)
                    nc.vector.tensor_tensor(pb[s % 2][:, :], pb[s % 2][:, :], dtx[par][:, :], ALU.mult).then_inc(u_done, 1)
                    v.wait_ge(u_done, g + 1)
                    v.wait_ge(da_ready, g + 1)
                    if not (first and s < H_RING):
                        v.wait_ge(hc_used, g - H_RING + 1)
                    nc.vector.tensor_tensor_scan(hs[:, s % H_RING, :], da[:, s % DA_RING, :, :].rearrange("p r t -> p (r t)"),
                                                 pb[s % 2][:, :], 0.0, ALU.mult, ALU.add).then_inc(h_ready, 1)

                def post(k, par, op, first=False):
                    if op in ("yb0", "yb1"):
                        q = int(op[2])
                        v.wait_ge(yb_ready, 2 * k + q + 1)
                        if q == 0 and (not isinstance(k, int) or k > 0):
                            v.wait_ge(o_ready, k)
                        cols = slice(q * HALF, (q + 1) * HALF)
                        nc.vector.scalar_tensor_tensor(gated[:, cols], act[par][:, cols], d_skip, misc[:, :],
                                                       ALU.mult, ALU.add).then_inc(yb_used, 1)
                    elif op == "out":
                        v.wait_ge(o_ready, k + 1)
                        if not isinstance(k, int) or k > 0:
                            v.wait_ge(stored, 16 * G * k)
                        nc.vector.tensor_tensor(fin[:, :].rearrange("p (n t) -> p n t", n=SUB),
                                                misc[:, :].rearrange("p (n t) -> p n t", n=SUB),
                                                xm[:, :, bass.ds(SUB * k, SUB)].rearrange("p t n -> p n t"),
                                                ALU.add).then_inc(fin_done, 1)

                schedule(v, pre, steps, post)
                for op in POST:
                    post(CHUNKS - 1, 1, op)

            @block.gpsimd
            def _(g_):
                def steps(k, par, s, first):
                    g = S * k + s
                    g_.wait_ge(c_copied, 2 * g + 2)
                    g_.wait_ge(h_ready, g + 1)
                    nc.gpsimd.tensor_tensor(hs[:, s % H_RING, :], hs[:, s % H_RING, :], cs[:, s % C_RING, :],
                                            ALU.mult).then_inc(hc_ready, 1)

                def post(k, par, op, first=False):
                    if op == "yb1":
                        g_.wait_ge(yb_used, 2 * k + 2)
                        nc.gpsimd.tensor_tensor(gated[:, :], gated[:, :], act[par][:, W:2 * W], ALU.mult).then_inc(y_gated, 1)

                schedule(g_, lambda k, par, op: None, steps, post)
                for op in POST:
                    post(CHUNKS - 1, 1, op)

            @block.sync
            def _(sp):
                def pre(k, par, op):
                    if op == "bc":
                        sp.wait_ge(bc_step, k + 1)
                        for part, src in enumerate((bc_hi, bc_mid, bc_lo)):
                            for i, dst in enumerate((b_parts[par], c_parts[par])):
                                for q in range(2):
                                    o = 64 * i + 32 * q
                                    sp.dma_start(dst[32 * part:32 * part + 32, q * HALF:(q + 1) * HALF],
                                                 src[o:o + 32, :]).then_inc(parts_ready, 16)

                schedule(sp, pre, lambda k, par, s, first: None, lambda k, par, op, first: None)
                sp.wait_ge(stored, 16 * G * CHUNKS)
ROWS = COLS = 256
C = 32
HID = 64
BAND = 4
TAPS_B = 2 * BAND + 1
RB = 64
UNIT = 512
UNITS = RB * COLS // UNIT
PADDED = ROWS + 2 * BAND


def triangle_layer(nc, layer, xc, xn, share, w, right_dram):
    BR = 8
    BLOCKS = RB // BR
    SUBS = BR * COLS // UNIT
    LJ = 128 + 2 * BAND

    with ExitStack() as ctx:
        def sb(name, shape, dt=F32):
            return ctx.enter_context(nc.sbuf_tensor(f"l{layer}_{name}", shape, dt))

        def ps(name, shape, dt=F32):
            return ctx.enter_context(nc.psum_tensor(f"l{layer}_{name}", shape, dt))

        def sem(name):
            sems.append(nc.alloc_semaphore(name=f"l{layer}_{name}"))
            return sems[-1]

        sems = []
        avg, center32, mean32, center64, mean64, eps = (
            share[n] for n in ("avg", "center32", "mean32", "center64", "mean64", "eps"))
        w_r, w_rg, w_og = (sb(n, [P, 2, P]) for n in ("w_r", "w_rg", "w_og"))
        w_l, w_lg = (sb(n, [P, HID]) for n in ("w_l", "w_lg"))
        w_o, w_ob = (sb(n, [P, 2 * C]) for n in ("w_o", "w_ob"))
        vec32 = sb("vec32", [P, 3])
        vec64 = sb("vec64", [P, 7])
        bias = sb("bias", [P, 5])
        mask_rows = sb("mask_rows", [P, LJ + 2 * BAND])
        mask_sq = sb("mask_sq", [P, LJ])
        mask_k = sb("mask_k", [P, COLS])
        mean_var = sb("mean_var", [P, 2])
        group_dev = sb("group_dev", [P, 2])
        gn_scale = sb("gn_scale", [P, 1])
        gn_mean = sb("gn_mean", [P, 1])
        norm_w = sb("norm_w", [P, P])
        norm_b = sb("norm_b", [P, 1])
        left = sb("left", [P, LJ, TAPS_B])
        win = [sb(f"win{i}", [P, BR + 2 * BAND, COLS]) for i in range(2)]
        band = [sb(f"band{i}", [P, BR, COLS]) for i in range(2)]
        gate = sb("gate", [P, BR * COLS])
        first_ctx = ctx.enter_context(ExitStack())
        mask_i, mask_ki, stats = (
            first_ctx.enter_context(nc.sbuf_tensor(f"l{layer}_{n}", shape, dt)) for n, shape, dt in (
                ("mask_i", [P, LJ + 2 * BAND], I32), ("mask_ki", [P, COLS], I32), ("stats", [P, UNITS, 6], F32)))
        bank = [ps(f"bank{i}", [P, UNIT]) for i in range(8)]

        def unit(t, u, n=1):
            return t[:, bass.ds(u * UNIT, UNIT * n)]

        def xn_unit(u):
            return xn[:, bass.ds(u * UNIT + BAND, UNIT)]

        w_ready, masks_done, stat_done, avg_done, gn_log, gn_rs, gn_mid, gn_out = map(sem, (
            "w_ready", "masks_done", "stat_done", "avg_done", "gn_log", "gn_rs", "gn_mid", "gn_out"))
        wb_ready, nb_ready, bias_done, scaled, stats_in = map(
            sem, ("wb_ready", "nb_ready", "bias_done", "scaled", "stats_in"))
        loads = ((w_r, "w_r"), (w_rg, "w_rg"), (w_og, "w_og"), (w_l, "w_l"), (w_lg, "w_lg"), (w_o, "w_o"),
                 (vec32, "vec32"), (vec64, "vec64"), (mask_i, "mask_rows"), (mask_ki, "mask_cols"))
        ALL_W = 16 * len(loads)

        with nc.Block() as block:
            @block.sync
            def _(sp):
                for dst, name in loads:
                    sp.dma_start(dst[tuple(slice(None) for _ in dst.shape)], w[f"l{layer}_{name}"]).then_inc(w_ready, 16)

            @block.vector
            def _(v):
                for u in range(UNITS):
                    last = nc.vector.bn_stats(stats[:, u, :], xc[:, u * UNIT:(u + 1) * UNIT])
                last.then_inc(stats_in, 1)
                v.wait_ge(stats_in, 1)
                nc.vector.bn_aggr(mean_var[:, :], stats[:, :, :]).then_inc(stat_done, 1)
                v.wait_ge(avg_done, 1)
                v.wait_ge(stat_done, 1)
                nc.vector.tensor_tensor(group_dev[:, 0:1], bank[0][:, 0:1], mean_var[:, 0:1], ALU.subtract).then_inc(gn_mid, 1)
                nc.vector.tensor_copy(gn_mean[:, :], bank[0][:, 0:1]).then_inc(gn_out, 1)
                v.wait_ge(gn_mid, 1)
                nc.vector.scalar_tensor_tensor(group_dev[:, 1:2], group_dev[:, 0:1], group_dev[:, 0:1],
                                               mean_var[:, 1:2], ALU.mult, ALU.add).then_inc(stat_done, 1)
                v.wait_ge(gn_rs, 1)
                nc.vector.tensor_scalar(norm_w[:, :], center32[:, :], gn_scale[:, 0:1], None, ALU.mult).then_inc(gn_out, 1)
                v.wait_ge(nb_ready, 1)
                nc.vector.tensor_scalar(norm_b[:, :], bank[2][:, 0:1], -1.0, None, ALU.mult)
                v.wait_ge(w_ready, ALL_W)
                v.wait_ge(wb_ready, 1)
                nc.vector.tensor_tensor(bias[:, :], bank[3][:, 0:5], vec64[:, 0:5], ALU.add).then_inc(bias_done, 1)
                for t in (w_r, w_rg, w_og):
                    nc.vector.tensor_scalar(t[:, :, :], t[:, :, :], vec32[:, 0:1], None, ALU.mult)
                for t in (w_l, w_lg):
                    nc.vector.tensor_scalar(t[:, :], t[:, :], vec32[:, 0:1], None, ALU.mult)
                nc.vector.tensor_scalar(w_ob[:, :], w_o[:, :], vec64[:, 6:7], None, ALU.mult).then_inc(scaled, 1)
                v.wait_ge(scaled, 1)
                nc.vector.tensor_scalar(w_o[:, :], w_o[:, :], vec64[:, 5:6], None, ALU.mult)
                nc.vector.tensor_copy(mask_rows[:, :], mask_i[:, :]).then_inc(masks_done, 1)
                nc.vector.tensor_copy(mask_k[:, :], mask_ki[:, :])
                v.wait_ge(masks_done, 1)
                nc.vector.tensor_tensor(mask_sq[:, :], mask_rows[:, BAND:BAND + LJ], mask_rows[:, BAND:BAND + LJ], ALU.mult)
                nc.vector.memset(left[:, :, :], 0.0)

            @block.tensor
            def _(pe):
                pe.wait_ge(stat_done, 1)
                nc.tensor.matmul(bank[0][:, 0:1], avg[:, :], mean_var[:, 0:1], start=True, stop=True).then_inc(avg_done, 1)
                pe.wait_ge(stat_done, 2)
                nc.tensor.matmul(bank[1][:, 0:1], avg[:, :], group_dev[:, 1:2], start=True, stop=True).then_inc(avg_done, 1)
                pe.wait_ge(w_ready, ALL_W)
                first = True
                for col, t in ((1, w_r), (3, w_rg), (4, w_og)):
                    nc.tensor.matmul(bank[3][:, col:col + 1], t[:, 0, :], vec32[:, 1:2], start=first, stop=False,
                                     skip_group_check=True)
                    first = False
                for half in range(2):
                    for col, t in ((0, w_l), (2, w_lg)):
                        last = nc.tensor.matmul(bank[3][HID * half:HID * half + HID, col:col + 1], t[0:C, :],
                                                vec32[0:C, 1:2], start=False, stop=True, skip_group_check=True)
                last.then_inc(wb_ready, 1)
                pe.wait_ge(gn_out, 2)
                nc.tensor.matmul(bank[2][:, 0:1], norm_w[:, :], gn_mean[:, :], start=True, stop=True).then_inc(nb_ready, 1)

            @block.scalar
            def _(a):
                a.wait_ge(avg_done, 2)
                nc.scalar.activation(gn_scale[:, :], bank[1][:, 0:1], ACT.Ln, bias=eps[:, 0:1]).then_inc(gn_log, 1)
                a.wait_ge(gn_log, 1)
                nc.scalar.activation(gn_scale[:, :], gn_scale[:, :], ACT.Exp, scale=-0.5).then_inc(gn_rs, 1)

        first_ctx.close()
        sq = [sb(f"sq{i}", [P, UNIT]) for i in range(2)]
        rstd = [sb(f"rstd{i}", [P, UNIT]) for i in range(2)]
        lslab = [sb(f"lslab{i}", [P, BR + 2 * BAND, TAPS_B]) for i in range(2)]

        cent_ready, sq_done, var_ready, log_done, rstd_done, xn_done = map(
            sem, ("cent_ready", "sq_done", "var_ready", "log_done", "rstd_done", "xn_done"))
        cent, var = bank[0:2], bank[2:4]

        def units(eng, body):
            body(0, 0, True)
            body(1, 1, True)
            with eng.Fori(2, UNITS - 1, 2) as u:
                body(u, 0, False)
                body(u + 1, 1, False)

        with nc.Block() as block:
            @block.tensor
            def _(pe):
                def body(u, par, first):
                    if not first:
                        pe.wait_ge(xn_done, u - 1)
                    nc.tensor.matmul(cent[par][:, :], norm_w[:, :], unit(xc, u), start=True, stop=True).then_inc(cent_ready, 1)
                    if first and u == 0:
                        return
                    variance(u - 1, 1 - par, first)

                def variance(u, par, first):
                    pe.wait_ge(sq_done, u + 1)
                    if not isinstance(u, int) or u > 1:
                        pe.wait_ge(log_done, u - 1)
                    nc.tensor.matmul(var[par][:, :], mean32[:, :], sq[par][:, :], start=True, stop=True).then_inc(var_ready, 1)

                units(pe, body)
                variance(UNITS - 1, 1, False)

            @block.scalar
            def _(a):
                def body(u, par, first):
                    a.wait_ge(cent_ready, u + 1)
                    if not first:
                        a.wait_ge(var_ready, u - 1)
                    nc.scalar.activation(sq[par][:, :], cent[par][:, :], ACT.Square, bias=norm_b[:, 0:1]).then_inc(sq_done, 1)
                    if first and u == 0:
                        return
                    root(u - 1, 1 - par)

                def root(u, par):
                    a.wait_ge(var_ready, u + 1)
                    if not isinstance(u, int) or u > 1:
                        a.wait_ge(xn_done, u - 1)
                    nc.scalar.activation(rstd[par][:, :], var[par][:, :], ACT.Ln, bias=eps[:, 1:2]).then_inc(log_done, 1)
                    a.wait_ge(log_done, u + 1)
                    nc.scalar.activation(rstd[par][:, :], rstd[par][:, :], ACT.Exp, scale=-0.5).then_inc(rstd_done, 1)

                units(a, body)
                root(UNITS - 1, 1)

            @block.vector
            def _(v):
                def body(u, par, first):
                    v.wait_ge(rstd_done, u + 1)
                    nc.vector.scalar_tensor_tensor(xn_unit(u), cent[par][:, :], norm_b[:, 0:1], rstd[par][:, :],
                                                   ALU.add, ALU.mult).then_inc(xn_done, 1)
                units(v, body)

        left_ready, left_sig, left_done, left_mul = map(sem, ("left_ready", "left_sig", "left_done", "left_mul"))
        pieces = [(32 * h, 32, BAND + 64 * p + 32 * h, [(0, 2 * p), (1, 2 * p + 1)]) for p in range(2) for h in range(2)]
        pieces += [(RB - BAND, BAND, 0, [(1, 2)]),
                   (0, BAND, BAND + 128, [(0, 1)])]

        def first_row(g):
            return 128 * (g % 2) + RB * (g // 2)

        with nc.Block() as block:
            @block.tensor
            def _(pe):
                for n, (r0, nr, _, parts) in enumerate(pieces):
                    if n >= 2:
                        pe.wait_ge(left_done, n - 1)
                    for t, dst in ((w_l, bank[2 * (n % 2)]), (w_lg, bank[2 * (n % 2) + 1])):
                        for half, g in parts:
                            base = xn[C * g:C * g + C, 0:1]
                            diag = bass.AP(base.tensor, base.offset + r0 * (COLS + 1) + first_row(g),
                                           [list(base.ap[0]), [COLS + 1, nr], [1, TAPS_B]])
                            m = nc.tensor.matmul(dst[HID * half:HID * half + HID, 0:nr * TAPS_B],
                                                 t[C * g:C * g + C, :], diag, start=True, stop=True)
                    m.then_inc(left_ready, 1)

            @block.scalar
            def _(a):
                for n, (r0, nr, l0, parts) in enumerate(pieces):
                    a.wait_ge(left_ready, n + 1)
                    if n >= 2:
                        a.wait_ge(left_done, n - 1)
                    lo, hi = HID * parts[0][0], HID * parts[-1][0] + HID
                    nc.scalar.activation(sq[n % 2][lo:hi, 0:nr * TAPS_B], bank[2 * (n % 2) + 1][lo:hi, 0:nr * TAPS_B],
                                         ACT.Sigmoid, bias=bias[lo:hi, 2:3]).then_inc(left_sig, 1)

            @block.vector
            def _(v):
                for n, (r0, nr, l0, parts) in enumerate(pieces):
                    v.wait_ge(left_sig, n + 1)
                    lo, hi = HID * parts[0][0], HID * parts[-1][0] + HID
                    nc.vector.scalar_tensor_tensor(left[lo:hi, l0:l0 + nr, :].rearrange("p j d -> p (j d)"),
                                                   bank[2 * (n % 2)][lo:hi, 0:nr * TAPS_B], bias[lo:hi, 0:1],
                                                   sq[n % 2][lo:hi, 0:nr * TAPS_B], ALU.add, ALU.mult).then_inc(left_done, 1)
                v.wait_ge(left_done, len(pieces))
                for d in range(TAPS_B):
                    nc.vector.tensor_tensor(left[:, :, d], left[:, :, d], mask_sq[:, :], ALU.mult).then_inc(left_mul, 1)
                for d in range(TAPS_B):
                    v.wait_ge(left_mul, d + 1)
                    nc.vector.tensor_tensor(left[:, :, d], left[:, :, d], mask_rows[:, d:d + LJ], ALU.mult).then_inc(left_mul, 1)

        rp_ready, rg_ready, rsig_done, r_done, r_masked = map(
            sem, ("rp_ready", "rg_ready", "rsig_done", "r_done", "r_masked"))
        r_stored = [sem(f"r_stored{i}") for i in range(4)]
        r_tile = [band[i][:, 2 * p:2 * p + 2, :].rearrange("p r k -> p (r k)") for i in range(2) for p in range(2)]
        sig = [gate[:, i * UNIT:(i + 1) * UNIT] for i in range(4)]
        with nc.Block() as block:
            @block.tensor
            def _(pe):
                def body(u, par, first):
                    for p in range(2):
                        n, slot = 2 * u + p, 2 * par + p
                        if not first:
                            pe.wait_ge(r_done, n - 3)
                        nc.tensor.matmul(bank[slot][:, :], w_rg[:, p, :], xn_unit(u), start=True, stop=True).then_inc(rg_ready, 1)
                        nc.tensor.matmul(bank[4 + slot][:, :], w_r[:, p, :], xn_unit(u), start=True, stop=True).then_inc(rp_ready, 1)
                units(pe, body)

            @block.scalar
            def _(a):
                def store(u, par):
                    for p in range(2):
                        a.wait_ge(r_masked, 2 * u + p + 1)
                        for half in range(2):
                            dst = right_dram[:, :, :].rearrange("h r k -> h (r k)")
                            a.dma_start(dst[:, bass.ds(u * UNIT + (BAND + 128 * half + RB * p) * COLS, UNIT)],
                                        r_tile[2 * par + p][HID * half:HID * half + HID, :]).then_inc(r_stored[2 * par + p], 16)

                def body(u, par, first):
                    for p in range(2):
                        n, slot = 2 * u + p, 2 * par + p
                        a.wait_ge(rg_ready, n + 1)
                        if not first:
                            a.wait_ge(r_done, n - 3)
                        nc.scalar.activation(sig[slot], bank[slot][:, :], ACT.Sigmoid, bias=bias[:, 3:4]).then_inc(rsig_done, 1)
                    if not (first and u == 0):
                        store(u - 1, 1 - par)
                units(a, body)
                store(UNITS - 1, 1)
                for slot in range(4):
                    a.wait_ge(r_stored[slot], 32 * (UNITS // 2))

            @block.vector
            def _(v):
                def body(u, par, first):
                    for p in range(2):
                        n, slot = 2 * u + p, 2 * par + p
                        v.wait_ge(rsig_done, n + 1)
                        v.wait_ge(rp_ready, n + 1)
                        if not first:
                            v.wait_ge(r_stored[slot], 16 * u - 16 * par)
                        nc.vector.scalar_tensor_tensor(r_tile[slot], bank[4 + slot][:, :], bias[:, 1:2], sig[slot],
                                                       ALU.add, ALU.mult).then_inc(r_done, 1)
                units(v, body)

            @block.gpsimd
            def _(g):
                def body(u, par, first):
                    for p in range(2):
                        n, slot = 2 * u + p, 2 * par + p
                        g.wait_ge(r_done, n + 1)
                        t = r_tile[slot].rearrange("p (r k) -> p r k", k=COLS)
                        nc.gpsimd.tensor_tensor(t, t, mask_k[:, :].unsqueeze(1).to_broadcast([P, 2, COLS]),
                                                ALU.mult).then_inc(r_masked, 1)
                units(g, body)

        win_loaded = [sem(f"win_loaded{i}") for i in range(2)]
        tap_done, slab_done, g_ready, gate_done, c_ready, sq2_done, v_ready, log2_done, rstd2_done, \
            z_done, zg_done, y_ready, x_done = map(sem, (
                "tap_done", "slab_done", "g_ready", "gate_done", "c_ready", "sq2_done", "v_ready",
                "log2_done", "rstd2_done", "z_done", "zg_done", "y_ready", "x_done"))
        gb, cb, vb, yb = bank[6:8], bank[0:4], bank[4:5], bank[5:6]
        NB = 2 * BLOCKS

        def blocks(eng, body, tail):
            for p in range(2):
                body(BLOCKS * p, 0, p, 0, "first" if p == 0 else "")
                if p == 1:
                    tail(BLOCKS - 1, BLOCKS - 1, 0, 1)
                body(BLOCKS * p + 1, 1, p, 1, "second" if p == 0 else "")
                tail(BLOCKS * p, 0, p, 0)
                with eng.Fori(2, BLOCKS - 1, 2) as b:
                    body(b + BLOCKS * p, b, p, 0, "")
                    tail(b + (BLOCKS * p - 1), b - 1, p, 1)
                    body(b + (BLOCKS * p + 1), b + 1, p, 1, "")
                    tail(b + BLOCKS * p, b, p, 0)
            tail(NB - 1, BLOCKS - 1, 1, 1)

        def nothing(*_):
            pass

        with nc.Block() as block:
            @block.sync
            def _(sp):
                for n in range(NB):
                    if n >= 2:
                        sp.wait_ge(tap_done, (n - 1) * TAPS_B * BR)
                    for half in range(2):
                        r0 = 128 * half + BR * n
                        sp.dma_start(win[n % 2][HID * half:HID * half + HID, :, :],
                                     right_dram[:, r0:r0 + BR + 2 * BAND, :]).then_inc(win_loaded[n % 2], 16)

            @block.vector
            def _(v):
                def body(n, b, p, par, at):
                    nc.vector.tensor_copy(lslab[par][:, :, :].rearrange("p j d -> p (j d)"),
                                          left[:, :, :].rearrange("p j d -> p (j d)")[
                                              :, bass.ds(b * (BR * TAPS_B) + RB * p * TAPS_B, (BR + 2 * BAND) * TAPS_B)]
                                          ).then_inc(slab_done, 1)
                    v.wait_ge(slab_done, n + 1)
                    v.wait_ge(win_loaded[par], 16 * n + (32 - 16 * par))
                    if at == "":
                        v.wait_ge(y_ready, SUBS * n - SUBS)
                    for tap in range(TAPS_B):
                        for r in range(BR):
                            src = win[par][:, r + tap, :]
                            dst = band[par][:, r, :]
                            coef = lslab[par][:, r + tap, TAPS_B - 1 - tap:TAPS_B - tap]
                            if tap == 0:
                                m = nc.vector.tensor_scalar(dst, src, coef, None, ALU.mult)
                            else:
                                v.wait_ge(tap_done, n * (TAPS_B * BR) + (tap - 1) * BR + r + 1)
                                m = nc.vector.scalar_tensor_tensor(dst, src, coef, dst, ALU.mult, ALU.add)
                            m.then_inc(tap_done, 1)

                def tail(n, b, p, par):
                    for j in range(SUBS):
                        i = SUBS * n + j
                        v.wait_ge(rstd2_done, i + 1)
                        o = band[par][:, 2 * j:2 * j + 2, :].rearrange("p r k -> p (r k)")
                        nc.vector.tensor_tensor(o, cb[j][:, :], rstd[j % 2][:, :], ALU.mult).then_inc(z_done, 1)
                    for j in range(SUBS):
                        v.wait_ge(y_ready, SUBS * n + j + 1)
                        x = xc[2 * C * p:2 * C * p + 2 * C, bass.ds(b * (BR * COLS) + j * UNIT, UNIT)]
                        nc.vector.scalar_tensor_tensor(x, yb[0][2 * C * p:2 * C * p + 2 * C, :],
                                                       vec32[2 * C * p:2 * C * p + 2 * C, 2:3], x,
                                                       ALU.add, ALU.add).then_inc(x_done, 1)
                blocks(v, body, tail)

            @block.tensor
            def _(pe):
                def body(n, b, p, par, at):
                    pass

                def tail(n, b, p, par):
                    for j in range(SUBS):
                        if not (isinstance(n, int) and n == 0 and j < 2):
                            pe.wait_ge(gate_done, SUBS * n + j - 1)
                        nc.tensor.matmul(gb[j % 2][:, :], w_og[:, p, :],
                                         xn[:, bass.ds(b * (BR * COLS) + (j * UNIT + BAND), UNIT)],
                                         start=True, stop=True).then_inc(g_ready, 1)
                    pe.wait_ge(tap_done, (TAPS_B * BR) * n + TAPS_B * BR)
                    if not (isinstance(n, int) and n == 0):
                        pe.wait_ge(z_done, SUBS * n)
                    for j in range(SUBS):
                        o = band[par][:, 2 * j:2 * j + 2, :].rearrange("p r k -> p (r k)")
                        nc.tensor.matmul(cb[j][:, :], center64[:, :], o, start=True, stop=True).then_inc(c_ready, 1)
                    for j in range(SUBS):
                        i = SUBS * n + j
                        pe.wait_ge(sq2_done, i + 1)
                        if not (isinstance(n, int) and n == 0 and j == 0):
                            pe.wait_ge(log2_done, i)
                        nc.tensor.matmul(vb[0][:, :], mean64[:, :], sq[j % 2][:, :], start=True, stop=True).then_inc(v_ready, 1)
                    for j in range(SUBS):
                        i = SUBS * n + j
                        pe.wait_ge(zg_done, i + 1)
                        if not (isinstance(n, int) and n == 0 and j == 0):
                            pe.wait_ge(x_done, i)
                        y = yb[0][2 * C * p:2 * C * p + 2 * C, :]
                        o = band[par][:, 2 * j:2 * j + 2, :].rearrange("p r k -> p (r k)")
                        nc.tensor.matmul(y, w_ob[:, :], gate[:, j * UNIT:(j + 1) * UNIT], start=True, stop=False)
                        nc.tensor.matmul(y, w_o[:, :], o, start=False, stop=True).then_inc(y_ready, 1)
                blocks(pe, body, tail)

            @block.scalar
            def _(a):
                def body(n, b, p, par, at):
                    pass

                def tail(n, b, p, par):
                    for j in range(SUBS):
                        a.wait_ge(g_ready, SUBS * n + j + 1)
                        nc.scalar.activation(gate[:, j * UNIT:(j + 1) * UNIT], gb[j % 2][:, :], ACT.Sigmoid,
                                             bias=bias[:, 4:5]).then_inc(gate_done, 1)
                    for j in range(SUBS):
                        i = SUBS * n + j
                        a.wait_ge(c_ready, i + 1)
                        if not (isinstance(n, int) and n == 0 and j < 2):
                            a.wait_ge(v_ready, i - 1)
                        nc.scalar.activation(sq[j % 2][:, :], cb[j][:, :], ACT.Square).then_inc(sq2_done, 1)
                        if j >= 1:
                            root(n, j - 1)
                    root(n, SUBS - 1)

                def root(n, j):
                    i = SUBS * n + j
                    a.wait_ge(v_ready, i + 1)
                    if not (isinstance(n, int) and n == 0 and j < 2):
                        a.wait_ge(z_done, i - 1)
                    nc.scalar.activation(rstd[j % 2][:, :], vb[0][:, :], ACT.Ln, bias=eps[:, 1:2]).then_inc(log2_done, 1)
                    a.wait_ge(log2_done, i + 1)
                    nc.scalar.activation(rstd[j % 2][:, :], rstd[j % 2][:, :], ACT.Exp, scale=-0.5).then_inc(rstd2_done, 1)
                blocks(a, body, tail)

            @block.gpsimd
            def _(g):
                def tail(n, b, p, par):
                    g.wait_ge(gate_done, SUBS * n + SUBS)
                    for j in range(SUBS):
                        g.wait_ge(z_done, SUBS * n + j + 1)
                        o = band[par][:, 2 * j:2 * j + 2, :].rearrange("p r k -> p (r k)")
                        nc.gpsimd.tensor_tensor(o, o, gate[:, j * UNIT:(j + 1) * UNIT], ALU.mult).then_inc(zg_done, 1)
                blocks(g, nothing, tail)
        nc.clear_and_free_semaphores(sems)


def build(nc, x_cm, w, right_dram, x3, out):
    with ExitStack() as sems, ExitStack() as ctx:
        def sb(name, shape, dt=F32):
            return ctx.enter_context(nc.sbuf_tensor(name, shape, dt))

        xc = sb("xc", [P, RB * COLS])
        xn = sb("xn", [P, RB * COLS + 2 * BAND])
        share = {n: sb(n, [P, P]) for n in ("avg", "center32", "mean32", "center64", "mean64")}
        share["eps"] = sb("eps", [P, 2])
        zero_ctx = ctx.enter_context(ExitStack())
        zero_rows = zero_ctx.enter_context(nc.sbuf_tensor("zero_rows", [HID, BAND * COLS], F32))
        x_loaded, zeroed, padded, consts = (sems.enter_context(nc.semaphore(n)) for n in (
            "x_loaded", "zeroed", "padded", "consts"))
        x_stored = sems.enter_context(nc.semaphore("x_stored"))
        with nc.Block() as block:
            @block.sync
            def _(sp):
                for g in range(4):
                    r0 = 128 * (g % 2) + RB * (g // 2)
                    for q in range(4):
                        sp.dma_start(xc[C * g:C * g + C, q * 4096:(q + 1) * 4096],
                                     x_cm[:, r0 + 16 * q:r0 + 16 * q + 16, :].rearrange("c r k -> c (r k)")
                                     ).then_inc(x_loaded, 16)
                sp.wait_ge(zeroed, 1)
                for r in (0, BAND + ROWS):
                    sp.dma_start(right_dram[:, r:r + BAND, :].rearrange("h r k -> h (r k)"),
                                 zero_rows[:, :]).then_inc(padded, 16)
                sp.wait_ge(padded, 32)
                sp.wait_ge(x_loaded, 256)

            @block.scalar
            def _(a):
                for n in ("avg", "center32", "mean32", "center64", "mean64"):
                    a.dma_start(share[n][:, :], w[n]).then_inc(consts, 16)
                a.wait_ge(consts, 80)

            @block.vector
            def _(v):
                nc.vector.memset(zero_rows[:, :], 0.0).then_inc(zeroed, 1)
                nc.vector.memset(xn[:, 0:BAND], 0.0)
                nc.vector.memset(xn[:, BAND + RB * COLS:], 0.0)
                nc.vector.memset(share["eps"][:, 0:1], 1e-5)
                nc.vector.memset(share["eps"][:, 1:2], 1e-6)

        zero_ctx.close()
        for layer in range(3):
            triangle_layer(nc, layer, xc, xn, share, w, right_dram)
            nc.all_engine_barrier()

        with nc.Block() as block:
            @block.sync
            def _(sp):
                for g in range(4):
                    r0 = 128 * (g % 2) + RB * (g // 2)
                    sp.dma_start(x3[:, r0:r0 + RB, :].rearrange("c r k -> c (r k)"),
                                 xc[C * g:C * g + C, :]).then_inc(x_stored, 16)
                sp.wait_ge(x_stored, 64)
        ctx.close()
        mamba_layer(nc, x3, w, out)


def _layout(f):
    import numpy as np

    def zeros(*s):
        return np.zeros(s, np.float32)

    a = {"x_cm": f["x"][0].transpose(2, 0, 1), "ident": np.eye(P, dtype=np.float32)}
    a["avg"] = np.kron(np.ones((4, 4), np.float32) / 4, np.eye(C, dtype=np.float32))
    a["mean32"] = np.kron(np.eye(4, dtype=np.float32), np.full((32, 32), 1 / 32, np.float32))
    a["center32"] = np.eye(P, dtype=np.float32) - a["mean32"]
    a["mean64"] = np.kron(np.eye(2, dtype=np.float32), np.full((64, 64), 1 / 64, np.float32))
    a["center64"] = np.eye(P, dtype=np.float32) - a["mean64"]
    for layer in range(3):
        k = lambda n: f[f"L{layer}_conv_{n}"]
        o = f"l{layer}_"
        for dst, name in (("w_r", "Wr"), ("w_rg", "Wrg"), ("w_og", "Wog")):
            t = zeros(P, 2, P)
            for pair in range(2):
                for half in range(2):
                    r = 64 * pair + 32 * half
                    t[r:r + 32, pair, 64 * half:64 * half + 64] = k(name)
            a[o + dst] = t
        a[o + "w_l"], a[o + "w_lg"] = np.tile(k("Wl"), (4, 1)), np.tile(k("Wlg"), (4, 1))
        t = zeros(P, 64)
        for half in range(2):
            t[64 * half:64 * half + 64, 32 * half:32 * half + 32] = k("Wo")
        a[o + "w_o"] = t
        a[o + "vec32"] = np.tile(np.stack([k("norm_scale"), k("norm_bias"), k("bo")], 1), (4, 1))
        a[o + "vec64"] = np.tile(np.stack([k(n) for n in (
            "bl", "br", "blg", "brg", "bog", "out_norm_scale", "out_norm_bias")], 1), (2, 1))
        m = k("src_mask")[0]
        padded = np.zeros(ROWS + 16, m.dtype)
        padded[8:8 + ROWS] = m
        a[o + "mask_rows"] = np.repeat(np.stack([padded[0:144], padded[128:272]]), 64, axis=0)
        a[o + "mask_cols"] = np.repeat(m[None], P, axis=0)
    W_in, conv_w, W_x = f["L3_conv_W_in"], f["L3_conv_conv_w"], f["L3_conv_W_x"]
    w_in, w_z = zeros(P, 2, P), zeros(P, 2, P)
    for q in range(2):
        for n in range(2):
            r = 64 * q + 32 * n
            w_in[r:r + 32, q, 64 * n:64 * n + 64] = W_in[:, :64]
            w_z[r:r + 32, q, 64 * n:64 * n + 64] = W_in[:, 64:]
    a["w_in"], a["w_z"] = w_in, w_z
    a["conv_w"] = np.broadcast_to(np.tile(conv_w.T, (1, 2))[None], (P, 4, P))
    wx_dt, w_dt, w_bc, w_out = zeros(4, P), zeros(4, P), zeros(P, 2, 32), zeros(P, 64)
    for n in range(2):
        wx_dt[2 * n:2 * n + 2, 64 * n:64 * n + 64] = W_x[:, 0:2].T
        w_dt[2 * n:2 * n + 2, 64 * n:64 * n + 64] = f["L3_conv_W_dt"]
        for b in range(2):
            w_bc[64 * n:64 * n + 64, b, 16 * n:16 * n + 16] = W_x[:, 2 + 16 * b:18 + 16 * b]
        w_out[64 * n:64 * n + 64, 32 * n:32 * n + 32] = f["L3_conv_W_out"]
    a["wx_dt"], a["w_dt"], a["w_bc"], a["w_out"] = wx_dt, w_dt, w_bc, w_out
    a["vecs"] = np.tile(np.stack([f["L3_conv_conv_b"], f["L3_conv_b_dt"], f["L3_conv_D_skip"]], 1), (2, 1))
    a["a_log"] = np.tile(f["L3_conv_A_log"], (2, 1))
    sel = zeros(3, 2, 16, 16, 2, 64)
    for n in range(2):
        for s in range(16):
            sel[:, n, s, s, n, :] = 1
    a["sel"] = sel.reshape(96, 16, P)
    return {n: np.ascontiguousarray(t) for n, t in a.items()}


def kernel(**inputs):
    import numpy as np
    import concourse.bacc as bacc
    from concourse.bass_utils import run_bass_kernel_spmd

    nc = bacc.Bacc("TRN2", target_bir_lowering=False, num_devices=1)
    arrays = _layout({n: np.asarray(v) for n, v in inputs.items()})
    w = {n: nc.dram_tensor("in_" + n, t.shape, mybir.dt.from_np(t.dtype), kind="ExternalInput").ap()
         for n, t in arrays.items()}
    right_dram = nc.dram_tensor("right_factor", (HID, PADDED, COLS), F32, kind="Internal").ap()
    x3 = nc.dram_tensor("x_layer3", (C, ROWS, COLS), F32, kind="Internal").ap()
    out = nc.dram_tensor("out_cm", (C, COLS, ROWS), F32, kind="ExternalOutput").ap()
    build(nc, w["x_cm"], w, right_dram, x3, out)
    r = run_bass_kernel_spmd(nc, [{"in_" + n: t for n, t in arrays.items()}], core_ids=[0])
    return r.results[0]["out_cm"].transpose(2, 1, 0)[None]
```

```python
from contextlib import ExitStack

import concourse.bass as bass
from concourse import mybir

P = 128
F32 = mybir.dt.float32
BF16 = mybir.dt.bfloat16
I32 = mybir.dt.int32
ALU = mybir.AluOpType
ACT = mybir.ActivationFunctionType


def mamba_layer(nc, x_cm, w, out):
    T, N = x_cm.shape[1], x_cm.shape[2]
    DM = 32
    S = 16
    TAPS = 4
    G = 4
    NG = N // G
    SUB = 2
    CHUNKS = NG // SUB
    HALF = SUB * T
    W = 2 * HALF
    BLK = W // P
    DA_RING = H_RING = C_RING = 4
    LAG = 2

    with ExitStack() as ctx:
        def sb(name, shape, dt=F32):
            return ctx.enter_context(nc.sbuf_tensor("m_" + name, shape, dt))

        def ps(name, shape, dt=F32):
            return ctx.enter_context(nc.psum_tensor("m_" + name, shape, dt))

        def sem(name):
            return ctx.enter_context(nc.semaphore("m_" + name))

        xm = sb("xm", [P, T, NG])
        ident = sb("ident", [P, P])
        avg = sb("avg", [P, P])
        eps = sb("eps", [P, 1])
        stats = sb("stats", [P, T * NG // 512, 6])
        mean_var = sb("mean_var", [P, 2])
        group_dev = sb("group_dev", [P, 2])
        gn_scale = sb("gn_scale", [P, 1])
        gn_bias = sb("gn_bias", [P, 1])
        w_in = sb("w_in", [P, 2, P])
        conv_w = sb("conv_w", [P, TAPS, P])
        w_conv = sb("w_conv", [P, 2, TAPS, P])
        w_z = sb("w_z", [P, 2, P])
        wx_dt = sb("wx_dt", [4, P])
        w_dt = sb("w_dt", [4, P])
        w_dt2 = sb("w_dt2", [P, P])
        w_bc = sb("w_bc", [P, 2, 32])
        w_out = sb("w_out", [P, 2 * DM])
        vecs = sb("vecs", [P, 3])
        conv_b, b_dt, d_skip = (vecs[:, i:i + 1] for i in range(3))
        a_log = sb("a_log", [P, S])
        a_neg = sb("a_neg", [P, S])
        sel = sb("sel", [96, S, P], BF16)

        xg = [sb(f"xg{i}", [P, SUB, TAPS - 1 + T]) for i in range(2)]
        raw = sb("raw", [P, 4 * HALF])
        act = [sb(f"act{i}", [P, 4 * HALF]) for i in range(2)]
        sp_x = sb("sp_x", [P, W])
        sp_v = sb("sp_v", [P, W])
        dt = [sb(f"dt{i}", [P, W]) for i in range(2)]
        dtx = [sb(f"dtx{i}", [P, W]) for i in range(2)]
        bc_hi = sb("bc_hi", [P, HALF], BF16)
        bc_mid = sb("bc_mid", [P, HALF], BF16)
        bc_lo = sb("bc_lo", [P, HALF], BF16)
        bc_rest = sb("bc_rest", [P, HALF])
        b_parts = [sb(f"b_parts{i}", [96, W], BF16) for i in range(2)]
        c_parts = [sb(f"c_parts{i}", [96, W], BF16) for i in range(2)]
        da = sb("da", [P, DA_RING, 2 * SUB, T])
        cs = sb("cs", [P, C_RING, W])
        hs = sb("hs", [P, H_RING, W])
        yt = sb("yt", [P, W])
        gated = sb("gated", [P, W])
        fin = sb("fin", [P, HALF])
        sel_f32 = raw[0:96, :].rearrange("p (s c) -> p s c", c=P)
        sp_u, sp_l = raw[:, 0:W], raw[:, W:2 * W]

        pb = [ps(f"pb{i}", [P, W]) for i in range(2)]
        pc = ps("pc", [P, HALF])
        misc = ps("misc", [P, HALF])
        py = ps("py", [P, W])

        loaded, zeroed, stat_done, avg_done, gn_step, gn_log, gn_ready = (
            sem(n) for n in ("loaded", "zeroed", "stat_done", "avg_done", "gn_step", "gn_log", "gn_ready"))
        w_ready, wdt_ready, wdt_copied, a_exp, a_ready = (
            sem(n) for n in ("w_ready", "wdt_ready", "wdt_copied", "a_exp", "a_ready"))

        with nc.Block() as block:
            @block.sync
            def _(sp):
                for g in range(G):
                    for q in range(4):
                        tt = slice(q * T // 4, (q + 1) * T // 4)
                        sp.dma_start(xm[g * DM:(g + 1) * DM, tt, :],
                                     x_cm[:, tt, g * NG:(g + 1) * NG]).then_inc(loaded, 16)

            @block.scalar
            def _(a):
                for dst, name in ((avg, "avg"), (ident, "ident"), (w_in, "w_in"), (conv_w, "conv_w"), (w_z, "w_z"),
                                  (wx_dt, "wx_dt"), (w_dt, "w_dt"), (w_bc, "w_bc"), (w_out, "w_out"),
                                  (vecs, "vecs"), (a_log, "a_log"), (sel_f32, "sel")):
                    idx = tuple(slice(None) for _ in dst.shape)
                    a.dma_start(dst[idx], w[name]).then_inc(w_ready, 16)
                a.wait_ge(w_ready, 12 * 16)
                nc.scalar.activation(a_neg[:, :], a_log[:, :], ACT.Exp).then_inc(a_exp, 1)
                a.wait_ge(avg_done, 2)
                a.wait_ge(zeroed, 1)
                nc.scalar.activation(gn_scale[:, :], misc[:, 1:2], ACT.Ln, bias=eps[:, 0:1]).then_inc(gn_log, 1)
                a.wait_ge(gn_log, 1)
                nc.scalar.activation(gn_scale[:, :], gn_scale[:, :], ACT.Exp, scale=-0.5).then_inc(gn_ready, 1)
                a.wait_ge(wdt_ready, 1)
                nc.scalar.copy(w_dt2[:, :], pc[:, 0:P]).then_inc(wdt_copied, 1)

            @block.tensor
            def _(pe):
                pe.wait_ge(w_ready, 12 * 16)
                nc.tensor.matmul(pc[:, 0:P], wx_dt[:, :], w_dt[:, :], start=True, stop=True).then_inc(wdt_ready, 1)
                pe.wait_ge(stat_done, 1)
                nc.tensor.matmul(misc[:, 0:1], avg[:, :], mean_var[:, 0:1], start=True, stop=True).then_inc(avg_done, 1)
                pe.wait_ge(stat_done, 2)
                nc.tensor.matmul(misc[:, 1:2], avg[:, :], group_dev[:, 1:2], start=True, stop=True).then_inc(avg_done, 1)

            @block.vector
            def _(v):
                nc.vector.memset(eps[:, :], 1e-5).then_inc(zeroed, 1)
                for i in range(2):
                    nc.vector.memset(xg[i][:, :, 0:TAPS - 1], 0.0)
                nc.vector.memset(da[:, :, :, 0:1], 0.0)
                v.wait_ge(w_ready, 12 * 16)
                for q in range(2):
                    for tap in range(TAPS):
                        nc.vector.tensor_tensor(w_conv[:, q, tap, :], w_in[:, q, :], conv_w[:, tap, :], ALU.mult)
                nc.vector.tensor_copy(sel[:, :, :], sel_f32)
                v.wait_ge(a_exp, 1)
                nc.vector.tensor_scalar(a_neg[:, :], a_neg[:, :], -1.0, None, ALU.mult).then_inc(a_ready, 1)
                v.wait_ge(loaded, 16 * 16)
                for j in range(T * NG // 512):
                    n = 512 // NG
                    last = nc.vector.bn_stats(stats[:, j, :], xm[:, j * n:(j + 1) * n, :])
                last.then_inc(gn_step, 1)
                v.wait_ge(gn_step, 1)
                nc.vector.bn_aggr(mean_var[:, :], stats[:, :, :]).then_inc(stat_done, 1)
                v.wait_ge(avg_done, 1)
                v.wait_ge(stat_done, 1)
                nc.vector.tensor_tensor(group_dev[:, 0:1], misc[:, 0:1], mean_var[:, 0:1], ALU.subtract).then_inc(a_ready, 1)
                v.wait_ge(a_ready, 2)
                nc.vector.scalar_tensor_tensor(group_dev[:, 1:2], group_dev[:, 0:1], group_dev[:, 0:1],
                                               mean_var[:, 1:2], ALU.mult, ALU.add).then_inc(stat_done, 1)
                v.wait_ge(gn_ready, 1)
                nc.vector.scalar_tensor_tensor(gn_bias[:, :], misc[:, 0:1], -1.0, gn_scale[:, :],
                                               ALU.mult, ALU.mult).then_inc(gn_ready, 1)

        names = ("raw_ready", "raw_evac", "silu_done", "dt_psum", "spx_ready", "sp_abs", "sp_exp", "sp_act_done", "sp_step",
                 "dt_done", "bc_psum", "bc_hi_done", "bc_step", "bc_mid_done", "bc_done", "parts_ready", "xg_ready",
                 "xg_used", "b_ready", "c_ready", "c_copied", "da_ready", "u_done", "h_ready", "hc_ready", "hc_used",
                 "y_copied", "yb_ready", "yb_used", "y_gated", "o_ready", "fin_done", "stored")
        (raw_ready, raw_evac, silu_done, dt_psum, spx_ready, sp_abs, sp_exp, sp_act_done, sp_step,
         dt_done, bc_psum, bc_hi_done, bc_step, bc_mid_done, bc_done, parts_ready, xg_ready,
         xg_used, b_ready, c_ready, c_copied, da_ready, u_done, h_ready, hc_ready, hc_used,
         y_copied, yb_ready, yb_used, y_gated, o_ready, fin_done, stored) = map(sem, names)

        POST_AT = {2: ["copy_y"], 3: ["yb0"], 4: ["yb1"], 5: ["out"], 6: ["store"]}
        PRE_AT = {1: ["xg"], 7: ["x0"], 8: ["x1", "z0"], 9: ["z1", "silu"], 10: ["dt0", "dt1"], 11: ["bc"], 12: ["softplus"]}
        POST = [op for s in sorted(POST_AT) for op in POST_AT[s]]
        PRE = [op for s in sorted(PRE_AT) for op in PRE_AT[s]]

        def ops_at(s, first, last):
            return ([] if first else POST_AT.get(s, [])), ([] if last else PRE_AT.get(s, []))

        def schedule(eng, pre, steps, post):
            def chunk(k, par, first=False, last=False):
                for s in range(S):
                    steps(k, par, s, first)
                    after, before = ops_at(s, first, last)
                    for op in after:
                        post(k - 1, 1 - par, op, first)
                    for op in before:
                        pre(k + 1, 1 - par, op)
            for op in PRE:
                pre(0, 0, op)
            chunk(0, 0, first=True)
            with eng.Fori(1, CHUNKS - 2, 2) as k:
                chunk(k, 1)
                chunk(k + 1, 0)
            chunk(CHUNKS - 1, 1, last=True)

        with nc.Block() as block:
            @block.tensor
            def _(pe):
                def pre(k, par, op):
                    if op in ("x0", "x1", "z0", "z1"):
                        i = ("x0", "x1", "z0", "z1").index(op)
                        if i == 0:
                            pe.wait_ge(xg_ready, k + 1)
                            if not isinstance(k, int) or k > 1:
                                pe.wait_ge(fin_done, k - 1)
                        else:
                            pe.wait_ge(raw_evac, 4 * k + i)
                        q = i % 2
                        if i < 2:
                            for tap in range(TAPS):
                                m = nc.tensor.matmul(misc[:, :], w_conv[:, q, tap, :], xg[par][:, :, tap:tap + T],
                                                     start=(tap == 0), stop=(tap == TAPS - 1))
                        else:
                            m = nc.tensor.matmul(misc[:, :], w_z[:, q, :], xg[par][:, :, TAPS - 1:TAPS - 1 + T],
                                                 start=True, stop=True)
                        m.then_inc(raw_ready, 1)
                    elif op in ("dt0", "dt1"):
                        q = int(op[2])
                        if q == 0:
                            pe.wait_ge(raw_evac, 4 * k + 4)
                            pe.wait_ge(silu_done, k + 1)
                        else:
                            pe.wait_ge(spx_ready, 2 * k + 1)
                        nc.tensor.matmul(misc[:, :], w_dt2[:, :], act[par][:, q * HALF:(q + 1) * HALF],
                                         start=True, stop=True).then_inc(dt_psum, 1)
                    elif op == "bc":
                        pe.wait_ge(spx_ready, 2 * k + 2)
                        for bc in range(2):
                            for q in range(2):
                                o = 64 * bc + 32 * q
                                m = nc.tensor.matmul(misc[o:o + 32, :], w_bc[:, bc, :],
                                                     act[par][:, q * HALF:(q + 1) * HALF], start=True, stop=True)
                        m.then_inc(bc_psum, 1)

                def sum_states(k, par, s):
                    g = S * k + s
                    pe.wait_ge(hc_ready, g + 1)
                    if s == 0 and (not isinstance(k, int) or k > 0):
                        pe.wait_ge(y_copied, k)
                    for b in range(BLK):
                        m = nc.tensor.matmul(py[:, b * P:(b + 1) * P], hs[:, s % H_RING, b * P:(b + 1) * P], ident[:, :],
                                             is_transpose=True, start=(s == 0 and b % 4 == 0),
                                             stop=(s == S - 1 and b % 4 == 3), skip_group_check=True)
                    m.then_inc(hc_used, 1)

                def steps(k, par, s, first):
                    g = S * k + s
                    if s == 0:
                        pe.wait_ge(parts_ready, 12 * 16 * (k + 1))
                    if not (first and s < 2):
                        pe.wait_ge(h_ready, g - 1)
                    for q in range(2):
                        m = nc.tensor.matmul(pb[s % 2][:, q * HALF:(q + 1) * HALF], sel[:, s, :],
                                             b_parts[par][:, q * HALF:(q + 1) * HALF], start=True, stop=True)
                    m.then_inc(b_ready, 1)
                    for q in range(2):
                        if not (first and s == 0 and q == 0):
                            pe.wait_ge(c_copied, 2 * g + q)
                        nc.tensor.matmul(pc[:, :], sel[:, s, :], c_parts[par][:, q * HALF:(q + 1) * HALF],
                                         start=True, stop=True).then_inc(c_ready, 1)
                    if s >= LAG:
                        sum_states(k, par, s - LAG)
                    elif not first:
                        sum_states(k - 1, 1 - par, S - LAG + s)

                def post(k, par, op, first=False):
                    if op in ("yb0", "yb1"):
                        q = int(op[2])
                        if q == 0:
                            pe.wait_ge(y_copied, k + 1)
                            pe.wait_ge(bc_done, k + 1 + (1 if not (isinstance(k, int) and k == CHUNKS - 1) else 0))
                        else:
                            pe.wait_ge(yb_used, 2 * k + 1)
                        for b in range(4):
                            m = nc.tensor.matmul(misc[:, b * P:(b + 1) * P], yt[:, (4 * q + b) * P:(4 * q + b + 1) * P],
                                                 ident[:, :], is_transpose=True, start=(b == 0), stop=(b == 3),
                                                 skip_group_check=True)
                        m.then_inc(yb_ready, 1)
                    elif op == "out":
                        pe.wait_ge(yb_used, 2 * k + 2)
                        pe.wait_ge(y_gated, k + 1)
                        for q in range(2):
                            m = nc.tensor.matmul(misc[64 * q:64 * q + 64, :], w_out[:, :],
                                                 gated[:, q * HALF:(q + 1) * HALF], start=True, stop=True)
                        m.then_inc(o_ready, 1)

                schedule(pe, pre, steps, post)
                for s in range(S - LAG, S):
                    sum_states(CHUNKS - 1, 1, s)
                for op in POST:
                    post(CHUNKS - 1, 1, op)

            @block.scalar
            def _(a):
                def pre(k, par, op):
                    if op == "xg":
                        nc.scalar.activation(xg[par][:, :, TAPS - 1:TAPS - 1 + T],
                                             xm[:, :, bass.ds(SUB * k, SUB)].rearrange("p t n -> p n t"),
                                             ACT.Identity, bias=gn_bias[:, 0:1], scale=gn_scale[:, 0:1]).then_inc(xg_ready, 1)
                    elif op in ("x0", "x1", "z0", "z1"):
                        i = ("x0", "x1", "z0", "z1").index(op)
                        a.wait_ge(raw_ready, 4 * k + i + 1)
                        if i == 0 and (not isinstance(k, int) or k > 0):
                            a.wait_ge(dt_done, k)
                        dst = raw[:, i * HALF:(i + 1) * HALF]
                        if i < 2:
                            nc.scalar.activation(dst, misc[:, :], ACT.Identity, bias=conv_b).then_inc(raw_evac, 1)
                        else:
                            nc.scalar.copy(dst, misc[:, :]).then_inc(raw_evac, 1)
                    elif op == "silu":
                        a.wait_ge(raw_evac, 4 * k + 4)
                        if not isinstance(k, int) or k > 1:
                            a.wait_ge(y_gated, k - 1)
                        nc.scalar.activation(act[par][:, :], raw[:, :], ACT.Silu).then_inc(silu_done, 1)
                    elif op in ("dt0", "dt1"):
                        q = int(op[2])
                        a.wait_ge(dt_psum, 2 * k + q + 1)
                        nc.scalar.activation(sp_x[:, q * HALF:(q + 1) * HALF], misc[:, :], ACT.Identity,
                                             bias=b_dt).then_inc(spx_ready, 1)
                    elif op == "bc":
                        a.wait_ge(bc_psum, k + 1)
                        if not isinstance(k, int) or k > 0:
                            a.wait_ge(parts_ready, 12 * 16 * k)
                        nc.scalar.copy(bc_hi[:, :], misc[:, :]).then_inc(bc_hi_done, 1)
                    elif op == "softplus":
                        a.wait_ge(spx_ready, 2 * k + 2)
                        a.wait_ge(silu_done, k + 1)
                        nc.scalar.activation(sp_u, sp_x[:, :], ACT.Abs).then_inc(sp_abs, 1)
                        a.wait_ge(sp_abs, k + 1)
                        nc.scalar.activation(sp_u, sp_u, ACT.Exp, scale=-1.0).then_inc(sp_exp, 1)
                        a.wait_ge(sp_exp, k + 1)
                        nc.scalar.activation(sp_l, sp_u, ACT.Ln, bias=1.0)
                        nc.scalar.activation(sp_v[:, :], sp_u, ACT.Identity, bias=1.0).then_inc(sp_act_done, 1)

                def steps(k, par, s, first):
                    g = S * k + s
                    if s == 0:
                        a.wait_ge(dt_done, k + 1)
                    if not (first and s < DA_RING):
                        a.wait_ge(h_ready, g - DA_RING + 1)
                    nc.scalar.activation(da[:, s % DA_RING, :, 1:T],
                                         dt[par][:, :].rearrange("p (r t) -> p r t", t=T)[:, :, 1:T],
                                         ACT.Exp, scale=a_neg[:, s:s + 1]).then_inc(da_ready, 1)
                    for q in range(2):
                        a.wait_ge(c_ready, 2 * g + q + 1)
                        if q == 0 and not (first and s < C_RING):
                            a.wait_ge(hc_ready, g - C_RING + 1)
                        nc.scalar.copy(cs[:, s % C_RING, q * HALF:(q + 1) * HALF], pc[:, :]).then_inc(c_copied, 1)

                def post(k, par, op, first=False):
                    if op == "copy_y":
                        a.wait_ge(hc_used, S * (k + 1))
                        if not isinstance(k, int) or k > 0:
                            a.wait_ge(yb_ready, 2 * k)
                        nc.scalar.copy(yt[:, :], py[:, :]).then_inc(y_copied, 1)
                    elif op == "store":
                        a.wait_ge(fin_done, k + 1)
                        for g in range(G):
                            a.dma_start(out[:, bass.ds(SUB * k + g * NG, SUB), :],
                                        fin[DM * g:DM * g + DM, :].rearrange("p (n t) -> p n t", n=SUB)).then_inc(stored, 16)

                schedule(a, pre, steps, post)
                for op in POST:
                    post(CHUNKS - 1, 1, op)

            @block.vector
            def _(v):
                def pre(k, par, op):
                    if op == "bc":
                        v.wait_ge(bc_hi_done, k + 1)
                        nc.vector.tensor_tensor(bc_rest[:, :], misc[:, :], bc_hi[:, :], ALU.subtract).then_inc(bc_done, 1)
                        v.wait_ge(bc_done, k + 1)
                        nc.vector.tensor_copy(bc_mid[:, :], bc_rest[:, :]).then_inc(bc_mid_done, 1)
                        v.wait_ge(bc_mid_done, k + 1)
                        nc.vector.tensor_tensor(bc_lo[:, :], bc_rest[:, :], bc_mid[:, :], ALU.subtract).then_inc(bc_step, 1)
                    elif op == "softplus":
                        v.wait_ge(sp_act_done, k + 1)
                        nc.vector.scalar_tensor_tensor(sp_v[:, :], sp_v[:, :], 1.0, sp_u, ALU.subtract,
                                                       ALU.subtract).then_inc(sp_step, 1)
                        v.wait_ge(sp_step, 3 * k + 1)
                        nc.vector.tensor_tensor(sp_l, sp_l, sp_v[:, :], ALU.subtract).then_inc(sp_step, 1)
                        v.wait_ge(sp_step, 3 * k + 2)
                        nc.vector.scalar_tensor_tensor(dt[par][:, :], sp_x[:, :], 0.0, sp_l, ALU.max,
                                                       ALU.add).then_inc(sp_step, 1)
                        v.wait_ge(sp_step, 3 * k + 3)
                        nc.vector.tensor_tensor(dtx[par][:, :], dt[par][:, :], act[par][:, 0:W], ALU.mult).then_inc(dt_done, 1)

                def steps(k, par, s, first):
                    g = S * k + s
                    if s == 0:
                        v.wait_ge(dt_done, k + 1)
                    v.wait_ge(b_ready, g + 1)
                    nc.vector.tensor_tensor(pb[s % 2][:, :], pb[s % 2][:, :], dtx[par][:, :], ALU.mult).then_inc(u_done, 1)
                    v.wait_ge(u_done, g + 1)
                    v.wait_ge(da_ready, g + 1)
                    if not (first and s < H_RING):
                        v.wait_ge(hc_used, g - H_RING + 1)
                    nc.vector.tensor_tensor_scan(hs[:, s % H_RING, :], da[:, s % DA_RING, :, :].rearrange("p r t -> p (r t)"),
                                                 pb[s % 2][:, :], 0.0, ALU.mult, ALU.add).then_inc(h_ready, 1)

                def post(k, par, op, first=False):
                    if op in ("yb0", "yb1"):
                        q = int(op[2])
                        v.wait_ge(yb_ready, 2 * k + q + 1)
                        if q == 0 and (not isinstance(k, int) or k > 0):
                            v.wait_ge(o_ready, k)
                        cols = slice(q * HALF, (q + 1) * HALF)
                        nc.vector.scalar_tensor_tensor(gated[:, cols], act[par][:, cols], d_skip, misc[:, :],
                                                       ALU.mult, ALU.add).then_inc(yb_used, 1)
                    elif op == "out":
                        v.wait_ge(o_ready, k + 1)
                        if not isinstance(k, int) or k > 0:
                            v.wait_ge(stored, 16 * G * k)
                        nc.vector.tensor_tensor(fin[:, :].rearrange("p (n t) -> p n t", n=SUB),
                                                misc[:, :].rearrange("p (n t) -> p n t", n=SUB),
                                                xm[:, :, bass.ds(SUB * k, SUB)].rearrange("p t n -> p n t"),
                                                ALU.add).then_inc(fin_done, 1)

                schedule(v, pre, steps, post)
                for op in POST:
                    post(CHUNKS - 1, 1, op)

            @block.gpsimd
            def _(g_):
                def steps(k, par, s, first):
                    g = S * k + s
                    g_.wait_ge(c_copied, 2 * g + 2)
                    g_.wait_ge(h_ready, g + 1)
                    nc.gpsimd.tensor_tensor(hs[:, s % H_RING, :], hs[:, s % H_RING, :], cs[:, s % C_RING, :],
                                            ALU.mult).then_inc(hc_ready, 1)

                def post(k, par, op, first=False):
                    if op == "yb1":
                        g_.wait_ge(yb_used, 2 * k + 2)
                        nc.gpsimd.tensor_tensor(gated[:, :], gated[:, :], act[par][:, W:2 * W], ALU.mult).then_inc(y_gated, 1)

                schedule(g_, lambda k, par, op: None, steps, post)
                for op in POST:
                    post(CHUNKS - 1, 1, op)

            @block.sync
            def _(sp):
                def pre(k, par, op):
                    if op == "bc":
                        sp.wait_ge(bc_step, k + 1)
                        for part, src in enumerate((bc_hi, bc_mid, bc_lo)):
                            for i, dst in enumerate((b_parts[par], c_parts[par])):
                                for q in range(2):
                                    o = 64 * i + 32 * q
                                    sp.dma_start(dst[32 * part:32 * part + 32, q * HALF:(q + 1) * HALF],
                                                 src[o:o + 32, :]).then_inc(parts_ready, 16)

                schedule(sp, pre, lambda k, par, s, first: None, lambda k, par, op, first: None)
                sp.wait_ge(stored, 16 * G * CHUNKS)
ROWS = COLS = 256
C = 32
HID = 64
BAND = 4
TAPS_B = 2 * BAND + 1
RB = 64
UNIT = 512
UNITS = RB * COLS // UNIT
PADDED = ROWS + 2 * BAND


def triangle_layer(nc, layer, xc, xn, share, w, right_dram):
    BR = 8
    BLOCKS = RB // BR
    SUBS = BR * COLS // UNIT
    LJ = 128 + 2 * BAND

    with ExitStack() as ctx:
        def sb(name, shape, dt=F32):
            return ctx.enter_context(nc.sbuf_tensor(f"l{layer}_{name}", shape, dt))

        def ps(name, shape, dt=F32):
            return ctx.enter_context(nc.psum_tensor(f"l{layer}_{name}", shape, dt))

        def sem(name):
            sems.append(nc.alloc_semaphore(name=f"l{layer}_{name}"))
            return sems[-1]

        sems = []
        avg, center32, mean32, center64, mean64, eps = (
            share[n] for n in ("avg", "center32", "mean32", "center64", "mean64", "eps"))
        w_og = sb("w_og", [P, 2, P])
        w_o = sb("w_o", [P, 2 * C])
        vec32 = sb("vec32", [P, 3])
        vec64 = sb("vec64", [P, 7])
        bias = sb("bias", [P, 5])
        mean_var = sb("mean_var", [P, 2])
        group_dev = sb("group_dev", [P, 2])
        gn_scale = sb("gn_scale", [P, 1])
        gn_mean = sb("gn_mean", [P, 1])
        norm_b = sb("norm_b", [P, 1])
        left = sb("left", [P, LJ, TAPS_B])
        win = [sb(f"win{i}", [P, BR + 2 * BAND, COLS]) for i in range(2)]
        band = [sb(f"band{i}", [P, BR, COLS]) for i in range(2)]
        gate = sb("gate", [P, BR * COLS])
        sq = [sb(f"sq{i}", [P, UNIT]) for i in range(2)]
        early_ctx = ctx.enter_context(ExitStack())
        w_r, w_rg, w_l, w_lg, norm_w, mask_k, mask_rows, mask_sq = (
            early_ctx.enter_context(nc.sbuf_tensor(f"l{layer}_{n}", shape, F32)) for n, shape in (
                ("w_r", [P, 2, P]), ("w_rg", [P, 2, P]), ("w_l", [P, HID]), ("w_lg", [P, HID]),
                ("norm_w", [P, P]),
                ("mask_k", [P, COLS]), ("mask_rows", [P, LJ + 2 * BAND]), ("mask_sq", [P, LJ])))
        first_ctx = ctx.enter_context(ExitStack())
        mask_i, mask_ki, stats = (
            first_ctx.enter_context(nc.sbuf_tensor(f"l{layer}_{n}", shape, dt)) for n, shape, dt in (
                ("mask_i", [P, LJ + 2 * BAND], I32), ("mask_ki", [P, COLS], I32), ("stats", [P, UNITS, 6], F32)))
        bank = [ps(f"bank{i}", [P, UNIT]) for i in range(8)]

        def unit(t, u, n=1):
            return t[:, bass.ds(u * UNIT, UNIT * n)]

        def xn_unit(u):
            return xn[:, bass.ds(u * UNIT + BAND, UNIT)]

        w_ready, masks_done, stat_done, avg_done, gn_log, gn_rs, gn_mid, gn_out = map(sem, (
            "w_ready", "masks_done", "stat_done", "avg_done", "gn_log", "gn_rs", "gn_mid", "gn_out"))
        wb_ready, nb_ready, bias_done, stats_in = map(sem, ("wb_ready", "nb_ready", "bias_done", "stats_in"))
        loads = ((w_r, "w_r"), (w_rg, "w_rg"), (w_og, "w_og"), (w_l, "w_l"), (w_lg, "w_lg"), (w_o, "w_o"),
                 (vec32, "vec32"), (vec64, "vec64"), (mask_i, "mask_rows"), (mask_ki, "mask_cols"))
        ALL_W = 16 * len(loads)

        with nc.Block() as block:
            @block.sync
            def _(sp):
                for dst, name in loads:
                    sp.dma_start(dst[tuple(slice(None) for _ in dst.shape)], w[f"l{layer}_{name}"]).then_inc(w_ready, 16)

            @block.vector
            def _(v):
                for u in range(UNITS):
                    last = nc.vector.bn_stats(stats[:, u, :], xc[:, u * UNIT:(u + 1) * UNIT])
                last.then_inc(stats_in, 1)
                v.wait_ge(stats_in, 1)
                nc.vector.bn_aggr(mean_var[:, :], stats[:, :, :]).then_inc(stat_done, 1)
                v.wait_ge(avg_done, 1)
                v.wait_ge(stat_done, 1)
                nc.vector.tensor_tensor(group_dev[:, 0:1], bank[0][:, 0:1], mean_var[:, 0:1], ALU.subtract).then_inc(gn_mid, 1)
                nc.vector.tensor_copy(gn_mean[:, :], bank[0][:, 0:1]).then_inc(gn_out, 1)
                v.wait_ge(gn_mid, 1)
                nc.vector.scalar_tensor_tensor(group_dev[:, 1:2], group_dev[:, 0:1], group_dev[:, 0:1],
                                               mean_var[:, 1:2], ALU.mult, ALU.add).then_inc(stat_done, 1)
                v.wait_ge(gn_rs, 1)
                nc.vector.tensor_scalar(norm_w[:, :], center32[:, :], gn_scale[:, 0:1], None, ALU.mult).then_inc(gn_out, 1)
                v.wait_ge(nb_ready, 1)
                nc.vector.tensor_scalar(norm_b[:, :], bank[2][:, 0:1], -1.0, None, ALU.mult)
                v.wait_ge(w_ready, ALL_W)
                v.wait_ge(wb_ready, 1)
                nc.vector.tensor_tensor(bias[:, :], bank[3][:, 0:5], vec64[:, 0:5], ALU.add).then_inc(bias_done, 1)
                for t in (w_r, w_rg, w_og):
                    nc.vector.tensor_scalar(t[:, :, :], t[:, :, :], vec32[:, 0:1], None, ALU.mult)
                for t in (w_l, w_lg):
                    nc.vector.tensor_scalar(t[:, :], t[:, :], vec32[:, 0:1], None, ALU.mult)
                nc.vector.tensor_copy(mask_rows[:, :], mask_i[:, :]).then_inc(masks_done, 1)
                nc.vector.tensor_copy(mask_k[:, :], mask_ki[:, :])
                v.wait_ge(masks_done, 1)
                nc.vector.tensor_tensor(mask_sq[:, :], mask_rows[:, BAND:BAND + LJ], mask_rows[:, BAND:BAND + LJ], ALU.mult)
                nc.vector.memset(left[:, :, :], 0.0)

            @block.tensor
            def _(pe):
                pe.wait_ge(stat_done, 1)
                nc.tensor.matmul(bank[0][:, 0:1], avg[:, :], mean_var[:, 0:1], start=True, stop=True).then_inc(avg_done, 1)
                pe.wait_ge(stat_done, 2)
                nc.tensor.matmul(bank[1][:, 0:1], avg[:, :], group_dev[:, 1:2], start=True, stop=True).then_inc(avg_done, 1)
                pe.wait_ge(w_ready, ALL_W)
                first = True
                for col, t in ((1, w_r), (3, w_rg), (4, w_og)):
                    nc.tensor.matmul(bank[3][:, col:col + 1], t[:, 0, :], vec32[:, 1:2], start=first, stop=False,
                                     skip_group_check=True)
                    first = False
                for half in range(2):
                    for col, t in ((0, w_l), (2, w_lg)):
                        last = nc.tensor.matmul(bank[3][HID * half:HID * half + HID, col:col + 1], t[0:C, :],
                                                vec32[0:C, 1:2], start=False, stop=True, skip_group_check=True)
                last.then_inc(wb_ready, 1)
                pe.wait_ge(gn_out, 2)
                nc.tensor.matmul(bank[2][:, 0:1], norm_w[:, :], gn_mean[:, :], start=True, stop=True).then_inc(nb_ready, 1)

            @block.scalar
            def _(a):
                a.wait_ge(avg_done, 2)
                nc.scalar.activation(gn_scale[:, :], bank[1][:, 0:1], ACT.Ln, bias=eps[:, 0:1]).then_inc(gn_log, 1)
                a.wait_ge(gn_log, 1)
                nc.scalar.activation(gn_scale[:, :], gn_scale[:, :], ACT.Exp, scale=-0.5).then_inc(gn_rs, 1)

        first_ctx.close()

        cent_ready, sq_done, var_ready, log_done, rstd_done, xn_done = map(
            sem, ("cent_ready", "sq_done", "var_ready", "log_done", "rstd_done", "xn_done"))
        cent, var = bank[0:4], bank[4:8]
        sq4 = [win[0][:, 2 * i:2 * i + 2, :].rearrange("p r k -> p (r k)") for i in range(4)]
        rstd4 = [win[1][:, 2 * i:2 * i + 2, :].rearrange("p r k -> p (r k)") for i in range(4)]

        def units(eng, body, depth=2):
            peeled = 8 if depth == 4 else depth
            for u in range(peeled):
                body(u, u % depth, u < depth)
            with eng.Fori(peeled, UNITS - depth + 1, depth) as u:
                for i in range(depth):
                    body(u + i, i, False)

        with nc.Block() as block:
            @block.tensor
            def _(pe):
                def body(u, at, first):
                    if not first:
                        pe.wait_ge(xn_done, u - 3)
                    nc.tensor.matmul(cent[at][:, :], norm_w[:, :], unit(xc, u), start=True, stop=True).then_inc(cent_ready, 1)
                    if not (first and u < 2):
                        variance(u - 2, (at - 2) % 4)

                def variance(u, at):
                    pe.wait_ge(sq_done, u + 1)
                    if not (isinstance(u, int) and u < 4):
                        pe.wait_ge(log_done, u - 3)
                    nc.tensor.matmul(var[at][:, :], mean32[:, :], sq4[at], start=True, stop=True).then_inc(var_ready, 1)

                units(pe, body, 4)
                variance(UNITS - 2, 2)
                variance(UNITS - 1, 3)

            @block.scalar
            def _(a):
                a.preload_act_table_set("natural_log_exp_and_others")

                def body(u, at, first):
                    a.wait_ge(cent_ready, u + 1)
                    if not first:
                        a.wait_ge(var_ready, u - 3)
                    nc.scalar.activation(sq4[at], cent[at][:, :], ACT.Square, bias=norm_b[:, 0:1]).then_inc(sq_done, 1)
                    if not (first and u < 3):
                        root(u - 3, (at - 3) % 4)

                def root(u, at):
                    a.wait_ge(var_ready, u + 1)
                    if not (isinstance(u, int) and u < 4):
                        a.wait_ge(xn_done, u - 3)
                    nc.scalar.activation(rstd4[at], var[at][:, :], ACT.Ln, bias=eps[:, 1:2]).then_inc(log_done, 1)
                    a.wait_ge(log_done, u + 1)
                    nc.scalar.activation(rstd4[at], rstd4[at], ACT.Exp, scale=-0.5).then_inc(rstd_done, 1)

                units(a, body, 4)
                for i in range(3):
                    root(UNITS - 3 + i, 1 + i)

            @block.vector
            def _(v):
                def body(u, at, first):
                    v.wait_ge(rstd_done, u + 1)
                    nc.vector.scalar_tensor_tensor(xn_unit(u), cent[at][:, :], norm_b[:, 0:1], rstd4[at],
                                                   ALU.add, ALU.mult).then_inc(xn_done, 1)
                units(v, body, 4)

        left_ready, left_sig, left_done, left_mul = map(sem, ("left_ready", "left_sig", "left_done", "left_mul"))
        pieces = [(32 * h, 32, BAND + 64 * p + 32 * h, [(0, 2 * p), (1, 2 * p + 1)]) for p in range(2) for h in range(2)]
        pieces += [(RB - BAND, BAND, 0, [(1, 2)]),
                   (0, BAND, BAND + 128, [(0, 1)])]

        def first_row(g):
            return 128 * (g % 2) + RB * (g // 2)

        with nc.Block() as block:
            @block.tensor
            def _(pe):
                for n, (r0, nr, _, parts) in enumerate(pieces):
                    if n >= 2:
                        pe.wait_ge(left_done, n - 1)
                    for t, dst in ((w_l, bank[2 * (n % 2)]), (w_lg, bank[2 * (n % 2) + 1])):
                        for half, g in parts:
                            base = xn[C * g:C * g + C, 0:1]
                            diag = bass.AP(base.tensor, base.offset + r0 * (COLS + 1) + first_row(g),
                                           [list(base.ap[0]), [COLS + 1, nr], [1, TAPS_B]])
                            m = nc.tensor.matmul(dst[HID * half:HID * half + HID, 0:nr * TAPS_B],
                                                 t[C * g:C * g + C, :], diag, start=True, stop=True)
                    m.then_inc(left_ready, 1)

            @block.scalar
            def _(a):
                for n, (r0, nr, l0, parts) in enumerate(pieces):
                    a.wait_ge(left_ready, n + 1)
                    if n >= 2:
                        a.wait_ge(left_done, n - 1)
                    lo, hi = HID * parts[0][0], HID * parts[-1][0] + HID
                    nc.scalar.activation(sq[n % 2][lo:hi, 0:nr * TAPS_B], bank[2 * (n % 2) + 1][lo:hi, 0:nr * TAPS_B],
                                         ACT.Sigmoid, bias=bias[lo:hi, 2:3]).then_inc(left_sig, 1)

            @block.vector
            def _(v):
                for n, (r0, nr, l0, parts) in enumerate(pieces):
                    v.wait_ge(left_sig, n + 1)
                    lo, hi = HID * parts[0][0], HID * parts[-1][0] + HID
                    nc.vector.scalar_tensor_tensor(left[lo:hi, l0:l0 + nr, :].rearrange("p j d -> p (j d)"),
                                                   bank[2 * (n % 2)][lo:hi, 0:nr * TAPS_B], bias[lo:hi, 0:1],
                                                   sq[n % 2][lo:hi, 0:nr * TAPS_B], ALU.add, ALU.mult).then_inc(left_done, 1)
                v.wait_ge(left_done, len(pieces))
                for d in range(TAPS_B):
                    nc.vector.tensor_tensor(left[:, :, d], left[:, :, d], mask_sq[:, :], ALU.mult).then_inc(left_mul, 1)
                for d in range(TAPS_B):
                    v.wait_ge(left_mul, d + 1)
                    nc.vector.tensor_tensor(left[:, :, d], left[:, :, d], mask_rows[:, d:d + LJ], ALU.mult).then_inc(left_mul, 1)

        rp_ready, rg_ready, rsig_done, r_done, r_masked = map(
            sem, ("rp_ready", "rg_ready", "rsig_done", "r_done", "r_masked"))
        r_stored = [sem(f"r_stored{i}") for i in range(4)]
        r_tile = [band[i][:, 2 * p:2 * p + 2, :].rearrange("p r k -> p (r k)") for i in range(2) for p in range(2)]
        sig = [gate[:, i * UNIT:(i + 1) * UNIT] for i in range(4)]
        with nc.Block() as block:
            @block.tensor
            def _(pe):
                def body(u, par, first):
                    for p in range(2):
                        n, slot = 2 * u + p, 2 * par + p
                        if not first:
                            pe.wait_ge(r_done, n - 3)
                        nc.tensor.matmul(bank[slot][:, :], w_rg[:, p, :], xn_unit(u), start=True, stop=True).then_inc(rg_ready, 1)
                        nc.tensor.matmul(bank[4 + slot][:, :], w_r[:, p, :], xn_unit(u), start=True, stop=True).then_inc(rp_ready, 1)
                units(pe, body)

            @block.scalar
            def _(a):
                def store(u, par):
                    for p in range(2):
                        a.wait_ge(r_masked, 2 * u + p + 1)
                        for half in range(2):
                            dst = right_dram[:, :, :].rearrange("h r k -> h (r k)")
                            a.dma_start(dst[:, bass.ds(u * UNIT + (BAND + 128 * half + RB * p) * COLS, UNIT)],
                                        r_tile[2 * par + p][HID * half:HID * half + HID, :]).then_inc(r_stored[2 * par + p], 16)

                def body(u, par, first):
                    for p in range(2):
                        n, slot = 2 * u + p, 2 * par + p
                        a.wait_ge(rg_ready, n + 1)
                        if not first:
                            a.wait_ge(r_done, n - 3)
                        nc.scalar.activation(sig[slot], bank[slot][:, :], ACT.Sigmoid, bias=bias[:, 3:4]).then_inc(rsig_done, 1)
                    if not (first and u == 0):
                        store(u - 1, 1 - par)
                units(a, body)
                store(UNITS - 1, 1)
                for slot in range(4):
                    a.wait_ge(r_stored[slot], 32 * (UNITS // 2))

            @block.vector
            def _(v):
                def body(u, par, first):
                    for p in range(2):
                        n, slot = 2 * u + p, 2 * par + p
                        v.wait_ge(rsig_done, n + 1)
                        v.wait_ge(rp_ready, n + 1)
                        if not first:
                            v.wait_ge(r_stored[slot], 16 * u - 16 * par)
                        nc.vector.scalar_tensor_tensor(r_tile[slot], bank[4 + slot][:, :], bias[:, 1:2], sig[slot],
                                                       ALU.add, ALU.mult).then_inc(r_done, 1)
                units(v, body)

            @block.gpsimd
            def _(g):
                def body(u, par, first):
                    for p in range(2):
                        n, slot = 2 * u + p, 2 * par + p
                        g.wait_ge(r_done, n + 1)
                        t = r_tile[slot].rearrange("p (r k) -> p r k", k=COLS)
                        nc.gpsimd.tensor_tensor(t, t, mask_k[:, :].unsqueeze(1).to_broadcast([P, 2, COLS]),
                                                ALU.mult).then_inc(r_masked, 1)
                units(g, body)

        early_ctx.close()
        rstd = [sb(f"rstd{i}", [P, UNIT]) for i in range(2)]
        tap_w = sb("tap_w", [P, TAPS_B, P])
        lslab = [sb(f"lslab{i}", [P, BR + 2 * BAND, TAPS_B]) for i in range(2)]
        DR = BR - 2
        LAST = SUBS - 1
        PE_TAPS = 2 * TAPS_B
        NB = 2 * BLOCKS
        DVE_TAPS = DR * TAPS_B
        win_loaded = [sem(f"win_loaded{i}") for i in range(2)]
        tap_done, slab_done, tapw_done, pe_tap_done, g_ready, gate_done, c_ready, sq2_done, v_ready, log2_done, \
            rstd2_done, z_done, zb_done, zg_done, y_ready, x_done = map(sem, (
                "tap_done", "slab_done", "tapw_done", "pe_tap_done", "g_ready", "gate_done", "c_ready", "sq2_done",
                "v_ready", "log2_done", "rstd2_done", "z_done", "zb_done", "zg_done", "y_ready", "x_done"))
        cb, gb, vb, yb = bank[0:4], bank[4], bank[5], bank[6:8]

        def blocks(eng, turn):
            def at(p, b):
                return (BLOCKS * p + b, p, b)
            turn(at(0, 0), None, 0)
            turn(at(0, 1), at(0, 0), 1)
            with eng.Fori(2, BLOCKS - 1, 2) as b:
                turn(at(0, b), at(0, b - 1), 0)
                turn(at(0, b + 1), at(0, b), 1)
            turn(at(1, 0), at(0, BLOCKS - 1), 0)
            turn(at(1, 1), at(1, 0), 1)
            with eng.Fori(2, BLOCKS - 1, 2) as b:
                turn(at(1, b), at(1, b - 1), 0)
                turn(at(1, b + 1), at(1, b), 1)
            turn(None, at(1, BLOCKS - 1), 0)

        def early(n, limit):
            return isinstance(n, int) and n < limit

        def unit_of(par, j):
            return band[par][:, 2 * j:2 * j + 2, :].rearrange("p r k -> p (r k)")

        with nc.Block() as block:
            @block.sync
            def _(sp):
                for n in range(NB):
                    if n >= 2:
                        sp.wait_ge(tap_done, (n - 1) * DVE_TAPS)
                        sp.wait_ge(pe_tap_done, (n - 1) * PE_TAPS)
                    for half in range(2):
                        r0 = 128 * half + BR * n
                        sp.dma_start(win[n % 2][HID * half:HID * half + HID, :, :],
                                     right_dram[:, r0:r0 + BR + 2 * BAND, :]).then_inc(win_loaded[n % 2], 16)

            @block.vector
            def _(v):
                def taps(n, par, rows, first_tap, end_tap):
                    for tap in range(first_tap, end_tap):
                        for i, r in enumerate(rows):
                            src = win[par][:, r + tap, :]
                            dst = band[par][:, r, :]
                            coef = lslab[par][:, r + tap, TAPS_B - 1 - tap:TAPS_B - tap]
                            if tap == 0:
                                m = nc.vector.tensor_scalar(dst, src, coef, None, ALU.mult)
                            else:
                                v.wait_ge(tap_done, n * DVE_TAPS + rows[0] * TAPS_B + (tap - 1) * len(rows) + i + 1)
                                m = nc.vector.scalar_tensor_tensor(dst, src, coef, dst, ALU.mult, ALU.add)
                            m.then_inc(tap_done, 1)

                def residual(n, p, b, j):
                    v.wait_ge(y_ready, SUBS * n + j + 1)
                    x = xc[2 * C * p:2 * C * p + 2 * C, bass.ds(b * (BR * COLS) + j * UNIT, UNIT)]
                    nc.vector.scalar_tensor_tensor(x, yb[j % 2][2 * C * p:2 * C * p + 2 * C, :],
                                                   vec32[2 * C * p:2 * C * p + 2 * C, 2:3], x,
                                                   ALU.add, ALU.add).then_inc(x_done, 1)

                def turn(now, before, par):
                    if now:
                        n, p, b = now
                        if not early(n, 2):
                            v.wait_ge(tapw_done, PE_TAPS * n - PE_TAPS)
                        nc.vector.tensor_copy(lslab[par][:, :, :].rearrange("p j d -> p (j d)"),
                                              left[:, :, :].rearrange("p j d -> p (j d)")[
                                                  :, bass.ds(b * (BR * TAPS_B) + RB * p * TAPS_B, (BR + 2 * BAND) * TAPS_B)]
                                              ).then_inc(slab_done, 1)
                        v.wait_ge(slab_done, n + 1)
                        v.wait_ge(win_loaded[par], 16 * n + (32 - 16 * par))
                        taps(n, par, range(DR // 2), 0, TAPS_B)
                    if before:
                        m, pm, bm = before
                        for j in range(SUBS):
                            v.wait_ge(rstd2_done, SUBS * m + j + 1)
                            nc.vector.scalar_tensor_tensor(unit_of(1 - par, j), cb[j][:, :], vec64[:, 5:6], rstd[j % 2][:, :],
                                                           ALU.mult, ALU.mult).then_inc(z_done, 1)
                    for part in range(2):
                        if now:
                            taps(n, par, range(DR // 2, DR), (0, 6)[part], (6, TAPS_B)[part])
                        if before:
                            residual(m, pm, bm, 2 * part)
                            residual(m, pm, bm, 2 * part + 1)
                blocks(v, turn)

            @block.tensor
            def _(pe):
                def turn(now, before, par):
                    if before:
                        m, pm, bm = before
                        for j in range(SUBS):
                            i = SUBS * m + j
                            if not (early(m, 1) and j == 0):
                                pe.wait_ge(gate_done, i)
                            nc.tensor.matmul(gb[:, :], w_og[:, pm, :],
                                             xn[:, bass.ds(bm * (BR * COLS) + (j * UNIT + BAND), UNIT)],
                                             start=True, stop=True).then_inc(g_ready, 1)
                            if j == 0:
                                pe.wait_ge(tap_done, DVE_TAPS * m + DVE_TAPS)
                            if j < LAST:
                                nc.tensor.matmul(cb[j][:, :], center64[:, :], unit_of(1 - par, j),
                                                 start=True, stop=True).then_inc(c_ready, 1)
                        for j in range(SUBS):
                            i = SUBS * m + j
                            pe.wait_ge(sq2_done, i + 1)
                            if not (early(m, 1) and j == 0):
                                pe.wait_ge(log2_done, i)
                            nc.tensor.matmul(vb[:, :], mean64[:, :], sq[j % 2][:, :], start=True, stop=True).then_inc(v_ready, 1)
                    if now:
                        n, p, b = now
                        if before:
                            pe.wait_ge(z_done, SUBS * n)
                    for r in range(2):
                        if now:
                            for tap in range(TAPS_B):
                                k = n * PE_TAPS + r * TAPS_B + tap
                                pe.wait_ge(tapw_done, k + 1)
                                if r == 0 and tap == 0:
                                    pe.wait_ge(win_loaded[par], 16 * n + (32 - 16 * par))
                                nc.tensor.matmul(cb[LAST][:, r * COLS:(r + 1) * COLS], tap_w[:, tap, :],
                                                 win[par][:, DR + r + tap, :], start=(r == 0 and tap == 0),
                                                 stop=(tap == TAPS_B - 1), skip_group_check=True).then_inc(pe_tap_done, 1)
                        if before:
                            for j in (2 * r, 2 * r + 1):
                                i = SUBS * m + j
                                pe.wait_ge(zg_done, i + 1)
                                if not (early(m, 1) and j < 2):
                                    pe.wait_ge(x_done, i - 1)
                                nc.tensor.matmul(yb[j % 2][2 * C * pm:2 * C * pm + 2 * C, :], w_o[:, :], unit_of(1 - par, j),
                                                 start=True, stop=True).then_inc(y_ready, 1)
                blocks(pe, turn)

            @block.scalar
            def _(a):
                def turn(now, before, par):
                    if before:
                        m, pm, bm = before
                        for j in range(SUBS):
                            a.wait_ge(g_ready, SUBS * m + j + 1)
                            if j == 0 and not early(m, 1):
                                a.wait_ge(zg_done, SUBS * m)
                            nc.scalar.activation(gate[:, j * UNIT:(j + 1) * UNIT], gb[:, :], ACT.Sigmoid,
                                                 bias=bias[:, 4:5]).then_inc(gate_done, 1)
                        a.preload_act_table_set("natural_log_exp_and_others")
                        for j in range(SUBS):
                            i = SUBS * m + j
                            if j < LAST:
                                a.wait_ge(c_ready, LAST * m + j + 1)
                            else:
                                a.wait_ge(pe_tap_done, PE_TAPS * m + PE_TAPS)
                            if not (early(m, 1) and j < 2):
                                a.wait_ge(v_ready, i - 1)
                            nc.scalar.activation(sq[j % 2][:, :], cb[j][:, :], ACT.Square).then_inc(sq2_done, 1)
                            if j >= 1:
                                root(m, j - 1)
                        root(m, SUBS - 1)
                        a.preload_act_table_set("sigmoid_and_others")
                    if now:
                        n, p, b = now
                        a.wait_ge(slab_done, n + 1)
                        for r in range(2):
                            for tap in range(TAPS_B):
                                k = n * PE_TAPS + r * TAPS_B + tap
                                if not (early(n, 1) and r == 0):
                                    a.wait_ge(pe_tap_done, k + 1 - TAPS_B)
                                nc.scalar.activation(tap_w[:, tap, :], center64[:, :], ACT.Copy,
                                                     scale=lslab[par][:, DR + r + tap, TAPS_B - 1 - tap:TAPS_B - tap]
                                                     ).then_inc(tapw_done, 1)

                def root(m, j):
                    i = SUBS * m + j
                    a.wait_ge(v_ready, i + 1)
                    if not (early(m, 1) and j < 2):
                        a.wait_ge(z_done, i - 1)
                    nc.scalar.activation(rstd[j % 2][:, :], vb[:, :], ACT.Ln, bias=eps[:, 1:2]).then_inc(log2_done, 1)
                    a.wait_ge(log2_done, i + 1)
                    nc.scalar.activation(rstd[j % 2][:, :], rstd[j % 2][:, :], ACT.Exp, scale=-0.5).then_inc(rstd2_done, 1)
                a.preload_act_table_set("sigmoid_and_others")
                blocks(a, turn)

            @block.gpsimd
            def _(g):
                def turn(now, before, par):
                    if before:
                        m, pm, bm = before
                        g.wait_ge(gate_done, SUBS * m + SUBS)
                        for j in range(SUBS):
                            g.wait_ge(z_done, SUBS * m + j + 1)
                            nc.gpsimd.tensor_tensor(unit_of(1 - par, j), unit_of(1 - par, j),
                                                    vec64[:, 6:7].to_broadcast([P, UNIT]), ALU.add).then_inc(zb_done, 1)
                            g.wait_ge(zb_done, SUBS * m + j + 1)
                            nc.gpsimd.tensor_tensor(unit_of(1 - par, j), unit_of(1 - par, j),
                                                    gate[:, j * UNIT:(j + 1) * UNIT], ALU.mult).then_inc(zg_done, 1)
                blocks(g, turn)

        nc.clear_and_free_semaphores(sems)


def build(nc, x_cm, w, right_dram, x3, out):
    with ExitStack() as sems, ExitStack() as ctx:
        def sb(name, shape, dt=F32):
            return ctx.enter_context(nc.sbuf_tensor(name, shape, dt))

        xc = sb("xc", [P, RB * COLS])
        xn = sb("xn", [P, RB * COLS + 2 * BAND])
        share = {n: sb(n, [P, P]) for n in ("avg", "center32", "mean32", "center64", "mean64")}
        share["eps"] = sb("eps", [P, 2])
        zero_ctx = ctx.enter_context(ExitStack())
        zero_rows = zero_ctx.enter_context(nc.sbuf_tensor("zero_rows", [HID, BAND * COLS], F32))
        x_loaded, zeroed, padded, consts = (sems.enter_context(nc.semaphore(n)) for n in (
            "x_loaded", "zeroed", "padded", "consts"))
        x_stored = sems.enter_context(nc.semaphore("x_stored"))
        with nc.Block() as block:
            @block.sync
            def _(sp):
                for g in range(4):
                    r0 = 128 * (g % 2) + RB * (g // 2)
                    for q in range(4):
                        sp.dma_start(xc[C * g:C * g + C, q * 4096:(q + 1) * 4096],
                                     x_cm[:, r0 + 16 * q:r0 + 16 * q + 16, :].rearrange("c r k -> c (r k)")
                                     ).then_inc(x_loaded, 16)
                sp.wait_ge(zeroed, 1)
                for r in (0, BAND + ROWS):
                    sp.dma_start(right_dram[:, r:r + BAND, :].rearrange("h r k -> h (r k)"),
                                 zero_rows[:, :]).then_inc(padded, 16)
                sp.wait_ge(padded, 32)
                sp.wait_ge(x_loaded, 256)

            @block.scalar
            def _(a):
                for n in ("avg", "center32", "mean32", "center64", "mean64"):
                    a.dma_start(share[n][:, :], w[n]).then_inc(consts, 16)
                a.wait_ge(consts, 80)

            @block.vector
            def _(v):
                nc.vector.memset(zero_rows[:, :], 0.0).then_inc(zeroed, 1)
                nc.vector.memset(xn[:, 0:BAND], 0.0)
                nc.vector.memset(xn[:, BAND + RB * COLS:], 0.0)
                nc.vector.memset(share["eps"][:, 0:1], 1e-5)
                nc.vector.memset(share["eps"][:, 1:2], 1e-6)

        zero_ctx.close()
        for layer in range(3):
            triangle_layer(nc, layer, xc, xn, share, w, right_dram)
            nc.all_engine_barrier()

        with nc.Block() as block:
            @block.sync
            def _(sp):
                for g in range(4):
                    r0 = 128 * (g % 2) + RB * (g // 2)
                    sp.dma_start(x3[:, r0:r0 + RB, :].rearrange("c r k -> c (r k)"),
                                 xc[C * g:C * g + C, :]).then_inc(x_stored, 16)
                sp.wait_ge(x_stored, 64)
        ctx.close()
        mamba_layer(nc, x3, w, out)


def _layout(f):
    import numpy as np

    def zeros(*s):
        return np.zeros(s, np.float32)

    a = {"x_cm": f["x"][0].transpose(2, 0, 1), "ident": np.eye(P, dtype=np.float32)}
    a["avg"] = np.kron(np.ones((4, 4), np.float32) / 4, np.eye(C, dtype=np.float32))
    a["mean32"] = np.kron(np.eye(4, dtype=np.float32), np.full((32, 32), 1 / 32, np.float32))
    a["center32"] = np.eye(P, dtype=np.float32) - a["mean32"]
    a["mean64"] = np.kron(np.eye(2, dtype=np.float32), np.full((64, 64), 1 / 64, np.float32))
    a["center64"] = np.eye(P, dtype=np.float32) - a["mean64"]
    for layer in range(3):
        k = lambda n: f[f"L{layer}_conv_{n}"]
        o = f"l{layer}_"
        for dst, name in (("w_r", "Wr"), ("w_rg", "Wrg"), ("w_og", "Wog")):
            t = zeros(P, 2, P)
            for pair in range(2):
                for half in range(2):
                    r = 64 * pair + 32 * half
                    t[r:r + 32, pair, 64 * half:64 * half + 64] = k(name)
            a[o + dst] = t
        a[o + "w_l"], a[o + "w_lg"] = np.tile(k("Wl"), (4, 1)), np.tile(k("Wlg"), (4, 1))
        t = zeros(P, 64)
        for half in range(2):
            t[64 * half:64 * half + 64, 32 * half:32 * half + 32] = k("Wo")
        a[o + "w_o"] = t
        a[o + "vec32"] = np.tile(np.stack([k("norm_scale"), k("norm_bias"), k("bo")], 1), (4, 1))
        a[o + "vec64"] = np.tile(np.stack([k(n) for n in (
            "bl", "br", "blg", "brg", "bog", "out_norm_scale", "out_norm_bias")], 1), (2, 1))
        m = k("src_mask")[0]
        padded = np.zeros(ROWS + 16, m.dtype)
        padded[8:8 + ROWS] = m
        a[o + "mask_rows"] = np.repeat(np.stack([padded[0:144], padded[128:272]]), 64, axis=0)
        a[o + "mask_cols"] = np.repeat(m[None], P, axis=0)
    W_in, conv_w, W_x = f["L3_conv_W_in"], f["L3_conv_conv_w"], f["L3_conv_W_x"]
    w_in, w_z = zeros(P, 2, P), zeros(P, 2, P)
    for q in range(2):
        for n in range(2):
            r = 64 * q + 32 * n
            w_in[r:r + 32, q, 64 * n:64 * n + 64] = W_in[:, :64]
            w_z[r:r + 32, q, 64 * n:64 * n + 64] = W_in[:, 64:]
    a["w_in"], a["w_z"] = w_in, w_z
    a["conv_w"] = np.broadcast_to(np.tile(conv_w.T, (1, 2))[None], (P, 4, P))
    wx_dt, w_dt, w_bc, w_out = zeros(4, P), zeros(4, P), zeros(P, 2, 32), zeros(P, 64)
    for n in range(2):
        wx_dt[2 * n:2 * n + 2, 64 * n:64 * n + 64] = W_x[:, 0:2].T
        w_dt[2 * n:2 * n + 2, 64 * n:64 * n + 64] = f["L3_conv_W_dt"]
        for b in range(2):
            w_bc[64 * n:64 * n + 64, b, 16 * n:16 * n + 16] = W_x[:, 2 + 16 * b:18 + 16 * b]
        w_out[64 * n:64 * n + 64, 32 * n:32 * n + 32] = f["L3_conv_W_out"]
    a["wx_dt"], a["w_dt"], a["w_bc"], a["w_out"] = wx_dt, w_dt, w_bc, w_out
    a["vecs"] = np.tile(np.stack([f["L3_conv_conv_b"], f["L3_conv_b_dt"], f["L3_conv_D_skip"]], 1), (2, 1))
    a["a_log"] = np.tile(f["L3_conv_A_log"], (2, 1))
    sel = zeros(3, 2, 16, 16, 2, 64)
    for n in range(2):
        for s in range(16):
            sel[:, n, s, s, n, :] = 1
    a["sel"] = sel.reshape(96, 16, P)
    return {n: np.ascontiguousarray(t) for n, t in a.items()}


def kernel(**inputs):
    import numpy as np
    import concourse.bacc as bacc
    from concourse.bass_utils import run_bass_kernel_spmd

    nc = bacc.Bacc("TRN2", target_bir_lowering=False, num_devices=1)
    arrays = _layout({n: np.asarray(v) for n, v in inputs.items()})
    w = {n: nc.dram_tensor("in_" + n, t.shape, mybir.dt.from_np(t.dtype), kind="ExternalInput").ap()
         for n, t in arrays.items()}
    right_dram = nc.dram_tensor("right_factor", (HID, PADDED, COLS), F32, kind="Internal").ap()
    x3 = nc.dram_tensor("x_layer3", (C, ROWS, COLS), F32, kind="Internal").ap()
    out = nc.dram_tensor("out_cm", (C, COLS, ROWS), F32, kind="ExternalOutput").ap()
    build(nc, w["x_cm"], w, right_dram, x3, out)
    r = run_bass_kernel_spmd(nc, [{"in_" + n: t for n, t in arrays.items()}], core_ids=[0])
    return r.results[0]["out_cm"].transpose(2, 1, 0)[None]
```

```python
from contextlib import ExitStack

import concourse.bass as bass
from concourse import mybir

P = 128
F32 = mybir.dt.float32
BF16 = mybir.dt.bfloat16
I32 = mybir.dt.int32
ALU = mybir.AluOpType
ACT = mybir.ActivationFunctionType


def mamba_layer(nc, x_cm, w, out):
    T, N = x_cm.shape[1], x_cm.shape[2]
    DM = 32
    S = 16
    TAPS = 4
    G = 4
    NG = N // G
    SUB = 2
    CHUNKS = NG // SUB
    HALF = SUB * T
    W = 2 * HALF
    BLK = W // P
    DA_RING = H_RING = C_RING = 4
    LAG = 3

    with ExitStack() as ctx:
        def sb(name, shape, dt=F32):
            return ctx.enter_context(nc.sbuf_tensor("m_" + name, shape, dt))

        def ps(name, shape, dt=F32):
            return ctx.enter_context(nc.psum_tensor("m_" + name, shape, dt))

        def sem(name):
            return ctx.enter_context(nc.semaphore("m_" + name))

        xm = sb("xm", [P, T, NG])
        ident = sb("ident", [P, P])
        avg = sb("avg", [P, P])
        eps = sb("eps", [P, 1])
        stats = sb("stats", [P, T * NG // 512, 6])
        mean_var = sb("mean_var", [P, 2])
        group_dev = sb("group_dev", [P, 2])
        gn_scale = sb("gn_scale", [P, 1])
        gn_bias = sb("gn_bias", [P, 1])
        w_in = sb("w_in", [P, P])
        conv_w = sb("conv_w", [P, TAPS // 2, P])
        w_conv = sb("w_conv", [P, TAPS // 2, P])
        w_z = sb("w_z", [P // 2, P])
        wx_dt = sb("wx_dt", [4, P])
        w_dt = sb("w_dt", [4, P])
        w_dt2 = sb("w_dt2", [P, P])
        w_bc = sb("w_bc", [P, 2, 32])
        w_out = sb("w_out", [P, 2 * DM])
        vecs = sb("vecs", [P, 3])
        conv_b, b_dt, d_skip = (vecs[:, i:i + 1] for i in range(3))
        a_log = sb("a_log", [P, S])
        a_neg = sb("a_neg", [P, S])
        sel = sb("sel", [P, S, P], BF16)

        xg = [sb(f"xg{i}", [P, 2, SUB, TAPS - 1 + T]) for i in range(2)]
        raw = sb("raw", [P, 4 * HALF])
        act = [sb(f"act{i}", [P, 4 * HALF]) for i in range(2)]
        x_half, z_half = slice(0, W), slice(W, 2 * W)
        sp_x = sb("sp_x", [P, W])
        sp_v = sb("sp_v", [P, W])
        dt = [sb(f"dt{i}", [P, W]) for i in range(2)]
        dtx = [sb(f"dtx{i}", [P, W]) for i in range(2)]
        bc_hi = sb("bc_hi", [P, HALF], BF16)
        bc_mid = sb("bc_mid", [P, HALF], BF16)
        bc_lo = sb("bc_lo", [P, HALF], BF16)
        bc_rest = sb("bc_rest", [P, HALF])
        bc_parts = [sb(f"bc_parts{i}", [P, 4, HALF], BF16) for i in range(2)]
        da = sb("da", [P, DA_RING, 2 * SUB, T])
        cs = sb("cs", [P, C_RING, W])
        hs = sb("hs", [P, H_RING, W])
        yt = sb("yt", [P, W])
        gated = sb("gated", [P, W])
        fin = sb("fin", [P, HALF])
        sel_f32 = raw[0:96, :].rearrange("p (s c) -> p s c", c=P)
        sp_u = raw[:, 0:W]

        pb = [ps(f"pb{i}", [P, W]) for i in range(2)]
        pc = ps("pc", [P, HALF])
        misc = ps("misc", [P, HALF])
        py = ps("py", [P, W])

        loaded, zeroed, stat_done, avg_done, gn_step, gn_log, gn_ready = (
            sem(n) for n in ("loaded", "zeroed", "stat_done", "avg_done", "gn_step", "gn_log", "gn_ready"))
        w_ready, wdt_ready, wdt_copied, a_exp, a_ready = (
            sem(n) for n in ("w_ready", "wdt_ready", "wdt_copied", "a_exp", "a_ready"))

        with nc.Block() as block:
            @block.sync
            def _(sp):
                for g in range(G):
                    for q in range(4):
                        tt = slice(q * T // 4, (q + 1) * T // 4)
                        sp.dma_start(xm[g * DM:(g + 1) * DM, tt, :],
                                     x_cm[:, tt, g * NG:(g + 1) * NG]).then_inc(loaded, 16)

            @block.scalar
            def _(a):
                for dst, name in ((avg, "avg"), (ident, "ident"), (w_in, "w_in"), (conv_w, "conv_w"), (w_z, "w_z"),
                                  (wx_dt, "wx_dt"), (w_dt, "w_dt"), (w_bc, "w_bc"), (w_out, "w_out"),
                                  (vecs, "vecs"), (a_log, "a_log"), (sel_f32, "sel")):
                    idx = tuple(slice(None) for _ in dst.shape)
                    a.dma_start(dst[idx], w[name]).then_inc(w_ready, 16)
                a.wait_ge(w_ready, 12 * 16)
                nc.scalar.activation(a_neg[:, :], a_log[:, :], ACT.Exp).then_inc(a_exp, 1)
                a.wait_ge(avg_done, 2)
                a.wait_ge(zeroed, 1)
                nc.scalar.activation(gn_scale[:, :], misc[:, 1:2], ACT.Ln, bias=eps[:, 0:1]).then_inc(gn_log, 1)
                a.wait_ge(gn_log, 1)
                nc.scalar.activation(gn_scale[:, :], gn_scale[:, :], ACT.Exp, scale=-0.5).then_inc(gn_ready, 1)
                a.wait_ge(wdt_ready, 1)
                nc.scalar.copy(w_dt2[:, :], pc[:, 0:P]).then_inc(wdt_copied, 1)

            @block.tensor
            def _(pe):
                pe.wait_ge(w_ready, 12 * 16)
                nc.tensor.matmul(pc[:, 0:P], wx_dt[:, :], w_dt[:, :], start=True, stop=True).then_inc(wdt_ready, 1)
                pe.wait_ge(stat_done, 1)
                nc.tensor.matmul(misc[:, 0:1], avg[:, :], mean_var[:, 0:1], start=True, stop=True).then_inc(avg_done, 1)
                pe.wait_ge(stat_done, 2)
                nc.tensor.matmul(misc[:, 1:2], avg[:, :], group_dev[:, 1:2], start=True, stop=True).then_inc(avg_done, 1)

            @block.vector
            def _(v):
                nc.vector.memset(eps[:, :], 1e-5).then_inc(zeroed, 1)
                for i in range(2):
                    nc.vector.memset(xg[i][:, :, :, 0:TAPS - 1], 0.0)
                nc.vector.memset(sel[96:P, :, :], 0.0)
                for i in range(2):
                    nc.vector.memset(bc_parts[i][96:P, :, :], 0.0)
                nc.vector.memset(da[:, :, :, 0:1], 0.0)
                v.wait_ge(w_ready, 12 * 16)
                for t in range(TAPS // 2):
                    nc.vector.tensor_tensor(w_conv[:, t, :], w_in[:, :], conv_w[:, t, :], ALU.mult)
                nc.vector.tensor_copy(sel[0:96, :, :], sel_f32)
                v.wait_ge(a_exp, 1)
                nc.vector.tensor_scalar(a_neg[:, :], a_neg[:, :], -1.0, None, ALU.mult).then_inc(a_ready, 1)
                v.wait_ge(loaded, 16 * 16)
                for j in range(T * NG // 512):
                    n = 512 // NG
                    last = nc.vector.bn_stats(stats[:, j, :], xm[:, j * n:(j + 1) * n, :])
                last.then_inc(gn_step, 1)
                v.wait_ge(gn_step, 1)
                nc.vector.bn_aggr(mean_var[:, :], stats[:, :, :]).then_inc(stat_done, 1)
                v.wait_ge(avg_done, 1)
                v.wait_ge(stat_done, 1)
                nc.vector.tensor_tensor(group_dev[:, 0:1], misc[:, 0:1], mean_var[:, 0:1], ALU.subtract).then_inc(a_ready, 1)
                v.wait_ge(a_ready, 2)
                nc.vector.scalar_tensor_tensor(group_dev[:, 1:2], group_dev[:, 0:1], group_dev[:, 0:1],
                                               mean_var[:, 1:2], ALU.mult, ALU.add).then_inc(stat_done, 1)
                v.wait_ge(gn_ready, 1)
                nc.vector.scalar_tensor_tensor(gn_bias[:, :], misc[:, 0:1], -1.0, gn_scale[:, :],
                                               ALU.mult, ALU.mult).then_inc(gn_ready, 1)

        names = ("raw_ready", "raw_evac", "exp_done", "ln_done", "sig_done", "silu_x_done", "silu_z_done", "dt_psum", "spx_ready", "sp_abs", "sp_exp", "sp_act_done", "sp_step",
                 "dt_done", "bc_psum", "bc_hi_done", "bc_step", "bc_mid_done", "bc_done", "parts_ready", "xg_ready",
                 "b_ready", "c_ready", "c_copied", "da_ready", "u_done", "h_ready", "hc_ready", "hc_used",
                 "y_copied", "yb_ready", "yb_used", "y_gated", "o_ready", "fin_done", "stored")
        (raw_ready, raw_evac, exp_done, ln_done, sig_done, silu_x_done, silu_z_done, dt_psum, spx_ready, sp_abs, sp_exp, sp_act_done, sp_step,
         dt_done, bc_psum, bc_hi_done, bc_step, bc_mid_done, bc_done, parts_ready, xg_ready,
         b_ready, c_ready, c_copied, da_ready, u_done, h_ready, hc_ready, hc_used,
         y_copied, yb_ready, yb_used, y_gated, o_ready, fin_done, stored) = map(sem, names)

        PRE, POST = "pre", "post"

        def early(k, n):
            return isinstance(k, int) and k < n

        SHARES = {
            "tensor": {1: [(PRE, "x0")], 2: [(PRE, "x1")], 3: [(POST, "yb0")], 4: [(POST, "yb1")], 6: [(PRE, "dt0")],
                       7: [(PRE, "dt1")], 8: [(POST, "out")], 9: [(PRE, "bc")], 10: [(PRE, "z0")], 11: [(PRE, "z1")]},
            "scalar": {0: [(PRE, "xg0")], 1: [(PRE, "xg1"), (PRE, "x0")], 2: [(POST, "copy_y"), (PRE, "x1")],
                       3: [(PRE, "exp_x"), (PRE, "ln_x")], 4: [(PRE, "sig_x")], 6: [(PRE, "dt0")],
                       7: [(PRE, "dt1"), (PRE, "sp_abs")], 8: [(PRE, "sp_exp")],
                       9: [(PRE, "bc"), (PRE, "sp_ln")], 10: [(POST, "store"), (PRE, "z0")], 11: [(PRE, "z1")],
                       12: [(PRE, "exp_z")], 13: [(PRE, "ln_z")], 14: [(PRE, "sig_z")]},
            "vector": {3: [(POST, "yb0")], 4: [(POST, "yb1")], 5: [(PRE, "silu_x")], 8: [(POST, "out")],
                       10: [(PRE, "bc_rest"), (PRE, "sp_loss")], 11: [(PRE, "bc_mid"), (PRE, "bc_lo"), (PRE, "sp_log")],
                       12: [(PRE, "sp_dt"), (PRE, "dtx")]},
            "gpsimd": {4: [(POST, "gate")], 14: [(PRE, "silu_z")]},
            "sync": {12: [(PRE, "hi"), (PRE, "mid"), (PRE, "lo")]},
        }

        def schedule(eng, name, pre, steps, post):
            def share(k, par, kinds, s):
                for kind, op in SHARES[name].get(s, []):
                    if kind in kinds and kind == PRE:
                        pre(k + 1, 1 - par, op)
                    elif kind in kinds:
                        post(k - 1, 1 - par, op)

            def chunk(k, par, kinds=(PRE, POST), first=False, last=False):
                for s in range(S):
                    steps(k, par, s, first, last)
                    share(k, par, kinds, s)
            for s in range(S):
                share(-1, 1, (PRE,), s)
            chunk(0, 0, (PRE,), first=True)
            with eng.Fori(1, CHUNKS - 2, 2) as k:
                chunk(k, 1)
                chunk(k + 1, 0)
            chunk(CHUNKS - 1, 1, (POST,), last=True)
            if name == "tensor":
                steps(CHUNKS, 0, "drain", False, False)
            for s in range(S):
                share(CHUNKS, 0, (POST,), s)

        with nc.Block() as block:
            @block.tensor
            def _(pe):
                def pre(k, par, op):
                    if op in ("x0", "x1", "z0", "z1"):
                        i = ("x0", "x1", "z0", "z1").index(op)
                        if i < 2:
                            pe.wait_ge(xg_ready, 2 * k + i + 1)
                        if i == 2:
                            pe.wait_ge(bc_done, k + 1)
                        elif not (early(k, 1) and i == 0):
                            pe.wait_ge(raw_evac, 4 * k + i)
                        q = i % 2
                        if i < 2:
                            for t in range(TAPS // 2):
                                m = nc.tensor.matmul(misc[:, :], w_conv[:, t, :], xg[par][:, q, :, t:t + T],
                                                     start=(t == 0), stop=(t == TAPS // 2 - 1))
                        else:
                            m = nc.tensor.matmul(misc[:, :], w_z[:, :], xg[par][0:P // 2, q, :, TAPS - 1:TAPS - 1 + T],
                                                 start=True, stop=True)
                        m.then_inc(raw_ready, 1)
                    elif op in ("dt0", "dt1"):
                        q = int(op[2])
                        if q == 0:
                            pe.wait_ge(silu_x_done, k + 1)
                            if not early(k, 2):
                                pe.wait_ge(yb_used, 2 * k - 2)
                        else:
                            pe.wait_ge(spx_ready, 2 * k + 1)
                        nc.tensor.matmul(misc[:, :], w_dt2[:, :], act[par][:, q * HALF:(q + 1) * HALF],
                                         start=True, stop=True).then_inc(dt_psum, 1)
                    elif op == "bc":
                        pe.wait_ge(spx_ready, 2 * k + 2)
                        if not early(k, 2):
                            pe.wait_ge(fin_done, k - 1)
                        for bc in range(2):
                            for q in range(2):
                                o = 64 * bc + 32 * q
                                m = nc.tensor.matmul(misc[o:o + 32, :], w_bc[:, bc, :],
                                                     act[par][:, q * HALF:(q + 1) * HALF], start=True, stop=True)
                        m.then_inc(bc_psum, 1)

                def sum_states(k, par, s):
                    g = S * k + s
                    pe.wait_ge(hc_ready, g + 1)
                    if s == 0 and (not isinstance(k, int) or k > 0):
                        pe.wait_ge(y_copied, k)
                    for b in range(BLK):
                        m = nc.tensor.matmul(py[:, b * P:(b + 1) * P], hs[:, s % H_RING, b * P:(b + 1) * P], ident[:, :],
                                             is_transpose=True, start=(s == 0 and b % 4 == 0),
                                             stop=(s == S - 1 and b % 4 == 3), skip_group_check=True)
                    m.then_inc(hc_used, 1)

                def spread_c(k, par, s, q):
                    g = S * k + s
                    if not (early(k, 1) and s == 0 and q == 0):
                        pe.wait_ge(c_copied, 2 * g + q)
                    nc.tensor.matmul(pc[:, :], sel[:, s, :], bc_parts[par][:, 2 + q, :],
                                     start=True, stop=True).then_inc(c_ready, 1)

                def steps(k, par, s, first, last):
                    if s == "drain":
                        for late in range(S - LAG, S):
                            sum_states(k - 1, 1 - par, late)
                        return
                    g = S * k + s
                    if s == 0:
                        pe.wait_ge(parts_ready, 12 * 16 * (k + 1))
                    if not (first and s < 2):
                        pe.wait_ge(h_ready, g - 1)
                    for q in range(2):
                        m = nc.tensor.matmul(pb[s % 2][:, q * HALF:(q + 1) * HALF], sel[:, s, :],
                                             bc_parts[par][:, q, :], start=True, stop=True)
                    m.then_inc(b_ready, 1)
                    spread_c(k, par, s, 0)
                    if s >= LAG:
                        sum_states(k, par, s - LAG)
                    elif not first:
                        sum_states(k - 1, 1 - par, S - LAG + s)
                    spread_c(k, par, s, 1)

                def post(k, par, op):
                    if op in ("yb0", "yb1"):
                        q = int(op[2])
                        if q == 1:
                            pe.wait_ge(yb_used, 2 * k + 1)
                        else:
                            pe.wait_ge(y_copied, k + 1)
                            if not isinstance(k, int):
                                pe.wait_ge(raw_evac, 4 * k + 8 + 2)
                            elif k == CHUNKS - 2:
                                pe.wait_ge(raw_evac, 4 * CHUNKS)
                            else:
                                pe.wait_ge(fin_done, k)
                        for b in range(4):
                            m = nc.tensor.matmul(misc[:, b * P:(b + 1) * P], yt[:, (4 * q + b) * P:(4 * q + b + 1) * P],
                                                 ident[:, :], is_transpose=True, start=(b == 0), stop=(b == 3),
                                                 skip_group_check=True)
                        m.then_inc(yb_ready, 1)
                    elif op == "out":
                        if not isinstance(k, int):
                            pe.wait_ge(spx_ready, 2 * k + 4 + 2)
                        pe.wait_ge(y_gated, k + 1)
                        for q in range(2):
                            m = nc.tensor.matmul(misc[64 * q:64 * q + 64, :], w_out[:, :],
                                                 gated[:, q * HALF:(q + 1) * HALF], start=True, stop=True)
                        m.then_inc(o_ready, 1)

                schedule(pe, "tensor", pre, steps, post)

            @block.scalar
            def _(a):
                a.preload_act_table_set("natural_log_exp_and_others")

                def pre(k, par, op):
                    if op in ("xg0", "xg1"):
                        q = int(op[2])
                        rows = slice(2 * DM * q, 2 * DM * q + 2 * DM)
                        for shift in (0, 2):
                            first = TAPS - 1 - shift
                            m = nc.scalar.activation(
                                xg[par][P // 4 * shift:P // 4 * shift + P // 2, q, :, first:first + T],
                                xm[rows, :, bass.ds(SUB * k, SUB)].rearrange("p t n -> p n t"),
                                ACT.Identity, bias=gn_bias[rows, 0:1], scale=gn_scale[rows, 0:1])
                        m.then_inc(xg_ready, 1)
                    elif op in ("x0", "x1", "z0", "z1"):
                        i = ("x0", "x1", "z0", "z1").index(op)
                        a.wait_ge(raw_ready, 4 * k + i + 1)
                        if i == 0 and not early(k, 1):
                            a.wait_ge(dt_done, k)
                        if i == 2 and not early(k, 1):
                            a.wait_ge(silu_z_done, k)
                        dst = raw[:, i * HALF:(i + 1) * HALF]
                        if i < 2:
                            nc.scalar.activation(dst, misc[:, :], ACT.Identity, bias=conv_b).then_inc(raw_evac, 1)
                        else:
                            nc.scalar.copy(dst, misc[:, :]).then_inc(raw_evac, 1)
                    elif op == "exp_x":
                        a.wait_ge(raw_evac, 4 * k + 2)
                        if not early(k, 1):
                            a.wait_ge(dt_done, k)
                        nc.scalar.activation(sp_v[:, :], raw[:, x_half], ACT.Exp, scale=-1.0).then_inc(exp_done, 1)
                    elif op in ("ln_x", "ln_z"):
                        i = 2 * k + (op == "ln_z")
                        a.wait_ge(exp_done, i + 1)
                        e = sp_v[:, :] if op == "ln_x" else act[par][:, z_half]
                        nc.scalar.activation(e, e, ACT.Ln, bias=1.0).then_inc(ln_done, 1)
                    elif op in ("sig_x", "sig_z"):
                        i = 2 * k + (op == "sig_z")
                        a.wait_ge(ln_done, i + 1)
                        e = sp_v[:, :] if op == "sig_x" else act[par][:, z_half]
                        nc.scalar.activation(e, e, ACT.Exp, scale=-1.0).then_inc(sig_done, 1)
                    elif op == "exp_z":
                        a.wait_ge(raw_evac, 4 * k + 4)
                        if not early(k, 2):
                            a.wait_ge(y_gated, k - 1)
                        nc.scalar.activation(act[par][:, z_half], raw[:, z_half], ACT.Exp, scale=-1.0).then_inc(exp_done, 1)
                    elif op in ("dt0", "dt1"):
                        q = int(op[2])
                        a.wait_ge(dt_psum, 2 * k + q + 1)
                        nc.scalar.activation(sp_x[:, q * HALF:(q + 1) * HALF], misc[:, :], ACT.Identity,
                                             bias=b_dt).then_inc(spx_ready, 1)
                    elif op == "bc":
                        a.wait_ge(bc_psum, k + 1)
                        if not isinstance(k, int) or k > 0:
                            a.wait_ge(parts_ready, 12 * 16 * k)
                        nc.scalar.copy(bc_hi[:, :], misc[:, :]).then_inc(bc_hi_done, 1)
                    elif op == "sp_abs":
                        a.wait_ge(spx_ready, 2 * k + 2)
                        nc.scalar.activation(sp_u, sp_x[:, :], ACT.Abs).then_inc(sp_abs, 1)
                    elif op == "sp_exp":
                        a.wait_ge(sp_abs, k + 1)
                        nc.scalar.activation(sp_u, sp_u, ACT.Exp, scale=-1.0).then_inc(sp_exp, 1)
                    elif op == "sp_ln":
                        a.wait_ge(sp_exp, k + 1)
                        nc.scalar.activation(dt[par][:, :], sp_u, ACT.Ln, bias=1.0)
                        nc.scalar.activation(sp_v[:, :], sp_u, ACT.Identity, bias=1.0).then_inc(sp_act_done, 1)

                def steps(k, par, s, first, last):
                    g = S * k + s
                    for q in range(2):
                        a.wait_ge(c_ready, 2 * g + q + 1)
                        if q == 0 and not (first and s < C_RING):
                            a.wait_ge(hc_ready, g - C_RING + 1)
                        nc.scalar.copy(cs[:, s % C_RING, q * HALF:(q + 1) * HALF], pc[:, :]).then_inc(c_copied, 1)
                    if first and s == 0:
                        decay(k, par, 0, True)
                    if s + 1 < S:
                        decay(k, par, s + 1, first)
                    elif not last:
                        decay(k + 1, 1 - par, 0, False)

                def decay(k, par, s, first):
                    g = S * k + s
                    if s == 0:
                        a.wait_ge(dt_done, k + 1)
                    if not (first and s < DA_RING):
                        a.wait_ge(h_ready, g - DA_RING + 1)
                    nc.scalar.activation(da[:, s % DA_RING, :, 1:T],
                                         dt[par][:, :].rearrange("p (r t) -> p r t", t=T)[:, :, 1:T],
                                         ACT.Exp, scale=a_neg[:, s:s + 1]).then_inc(da_ready, 1)

                def post(k, par, op):
                    if op == "copy_y":
                        a.wait_ge(hc_used, S * (k + 1))
                        if not isinstance(k, int) or k > 0:
                            a.wait_ge(yb_ready, 2 * k)
                        nc.scalar.copy(yt[:, :], py[:, :]).then_inc(y_copied, 1)
                    elif op == "store":
                        a.wait_ge(fin_done, k + 1)
                        for g in range(G):
                            a.dma_start(out[:, bass.ds(SUB * k + g * NG, SUB), :],
                                        fin[DM * g:DM * g + DM, :].rearrange("p (n t) -> p n t", n=SUB)).then_inc(stored, 16)

                schedule(a, "scalar", pre, steps, post)

            @block.vector
            def _(v):
                def pre(k, par, op):
                    if op == "silu_x":
                        v.wait_ge(sig_done, 2 * k + 1)
                        nc.vector.tensor_tensor(act[par][:, x_half], sp_v[:, :], raw[:, x_half], ALU.mult).then_inc(silu_x_done, 1)
                    if op == "bc_rest":
                        v.wait_ge(bc_hi_done, k + 1)
                        nc.vector.tensor_tensor(bc_rest[:, :], misc[:, :], bc_hi[:, :], ALU.subtract).then_inc(bc_done, 1)
                    elif op == "bc_mid":
                        v.wait_ge(bc_done, k + 1)
                        nc.vector.tensor_copy(bc_mid[:, :], bc_rest[:, :]).then_inc(bc_mid_done, 1)
                    elif op == "bc_lo":
                        v.wait_ge(bc_mid_done, k + 1)
                        nc.vector.tensor_tensor(bc_lo[:, :], bc_rest[:, :], bc_mid[:, :], ALU.subtract).then_inc(bc_step, 1)
                    elif op == "sp_loss":
                        v.wait_ge(sp_act_done, k + 1)
                        nc.vector.scalar_tensor_tensor(sp_v[:, :], sp_v[:, :], 1.0, sp_u, ALU.subtract,
                                                       ALU.subtract).then_inc(sp_step, 1)
                    elif op == "sp_log":
                        v.wait_ge(sp_step, 3 * k + 1)
                        nc.vector.tensor_tensor(dt[par][:, :], dt[par][:, :], sp_v[:, :], ALU.subtract).then_inc(sp_step, 1)
                    elif op == "sp_dt":
                        v.wait_ge(sp_step, 3 * k + 2)
                        nc.vector.scalar_tensor_tensor(dt[par][:, :], sp_x[:, :], 0.0, dt[par][:, :], ALU.max,
                                                       ALU.add).then_inc(sp_step, 1)
                    elif op == "dtx":
                        v.wait_ge(sp_step, 3 * k + 3)
                        nc.vector.tensor_tensor(dtx[par][:, :], dt[par][:, :], act[par][:, 0:W], ALU.mult).then_inc(dt_done, 1)

                def steps(k, par, s, first, last):
                    g = S * k + s
                    if s == 0:
                        v.wait_ge(dt_done, k + 1)
                    v.wait_ge(b_ready, g + 1)
                    nc.vector.tensor_tensor(pb[s % 2][:, :], pb[s % 2][:, :], dtx[par][:, :], ALU.mult).then_inc(u_done, 1)
                    v.wait_ge(u_done, g + 1)
                    v.wait_ge(da_ready, g + 1)
                    if not (first and s < H_RING):
                        v.wait_ge(hc_used, g - H_RING + 1)
                    nc.vector.tensor_tensor_scan(hs[:, s % H_RING, :], da[:, s % DA_RING, :, :].rearrange("p r t -> p (r t)"),
                                                 pb[s % 2][:, :], 0.0, ALU.mult, ALU.add).then_inc(h_ready, 1)

                def post(k, par, op):
                    if op in ("yb0", "yb1"):
                        q = int(op[2])
                        v.wait_ge(yb_ready, 2 * k + q + 1)
                        if q == 0 and (not isinstance(k, int) or k > 0):
                            v.wait_ge(o_ready, k)
                        cols = slice(q * HALF, (q + 1) * HALF)
                        nc.vector.scalar_tensor_tensor(gated[:, cols], act[par][:, cols], d_skip, misc[:, :],
                                                       ALU.mult, ALU.add).then_inc(yb_used, 1)
                    elif op == "out":
                        v.wait_ge(o_ready, k + 1)
                        if not isinstance(k, int) or k > 0:
                            v.wait_ge(stored, 16 * G * k)
                        nc.vector.tensor_tensor(fin[:, :].rearrange("p (n t) -> p n t", n=SUB),
                                                misc[:, :].rearrange("p (n t) -> p n t", n=SUB),
                                                xm[:, :, bass.ds(SUB * k, SUB)].rearrange("p t n -> p n t"),
                                                ALU.add).then_inc(fin_done, 1)

                schedule(v, "vector", pre, steps, post)

            @block.gpsimd
            def _(g_):
                def steps(k, par, s, first, last):
                    g = S * k + s
                    g_.wait_ge(c_copied, 2 * g + 2)
                    g_.wait_ge(h_ready, g + 1)
                    nc.gpsimd.tensor_tensor(hs[:, s % H_RING, :], hs[:, s % H_RING, :], cs[:, s % C_RING, :],
                                            ALU.mult).then_inc(hc_ready, 1)

                def pre(k, par, op):
                    if op == "silu_z":
                        g_.wait_ge(sig_done, 2 * k + 2)
                        nc.gpsimd.tensor_tensor(act[par][:, z_half], act[par][:, z_half], raw[:, z_half],
                                                ALU.mult).then_inc(silu_z_done, 1)

                def post(k, par, op):
                    if op == "gate":
                        g_.wait_ge(yb_used, 2 * k + 2)
                        g_.wait_ge(silu_z_done, k + 1)
                        nc.gpsimd.tensor_tensor(gated[:, :], gated[:, :], act[par][:, W:2 * W], ALU.mult).then_inc(y_gated, 1)

                schedule(g_, "gpsimd", pre, steps, post)

            @block.sync
            def _(sp):
                def pre(k, par, op):
                    part = ("hi", "mid", "lo").index(op)
                    sp.wait_ge((bc_hi_done, bc_mid_done, bc_step)[part], k + 1)
                    for i in range(4):
                        sp.dma_start(bc_parts[par][32 * part:32 * part + 32, i, :],
                                     (bc_hi, bc_mid, bc_lo)[part][32 * i:32 * i + 32, :]).then_inc(parts_ready, 16)

                schedule(sp, "sync", pre, lambda *_: None, None)
                sp.wait_ge(stored, 16 * G * CHUNKS)
ROWS = COLS = 256
C = 32
HID = 64
BAND = 4
TAPS_B = 2 * BAND + 1
RB = 64
UNIT = 512
UNITS = RB * COLS // UNIT
PADDED = ROWS + 2 * BAND


def triangle_layer(nc, layer, xc, xn, share, w, right_dram):
    BR = 8
    BLOCKS = RB // BR
    SUBS = BR * COLS // UNIT
    LJ = 128 + 2 * BAND

    with ExitStack() as ctx:
        def sb(name, shape, dt=F32):
            return ctx.enter_context(nc.sbuf_tensor(f"l{layer}_{name}", shape, dt))

        def ps(name, shape, dt=F32):
            return ctx.enter_context(nc.psum_tensor(f"l{layer}_{name}", shape, dt))

        def sem(name):
            sems.append(nc.alloc_semaphore(name=f"l{layer}_{name}"))
            return sems[-1]

        sems = []
        avg, center32, mean32, center64, mean64, eps = (
            share[n] for n in ("avg", "center32", "mean32", "center64", "mean64", "eps"))
        w_og = sb("w_og", [P, 2, P])
        w_o = sb("w_o", [P, 2 * C])
        vec32 = sb("vec32", [P, 3])
        vec64 = sb("vec64", [P, 7])
        bias = sb("bias", [P, 5])
        mean_var = sb("mean_var", [P, 2])
        group_dev = sb("group_dev", [P, 2])
        gn_scale = sb("gn_scale", [P, 1])
        gn_mean = sb("gn_mean", [P, 1])
        norm_b = sb("norm_b", [P, 1])
        left = sb("left", [P, LJ, TAPS_B])
        win = [sb(f"win{i}", [P, BR + 2 * BAND, COLS]) for i in range(2)]
        band = [sb(f"band{i}", [P, BR, COLS]) for i in range(2)]
        gate = sb("gate", [P, BR * COLS])
        sq = [sb(f"sq{i}", [P, UNIT]) for i in range(2)]
        early_ctx = ctx.enter_context(ExitStack())
        w_r, w_rg, w_l, w_lg, norm_w, mask_k, mask_rows, mask_sq = (
            early_ctx.enter_context(nc.sbuf_tensor(f"l{layer}_{n}", shape, F32)) for n, shape in (
                ("w_r", [P, 2, P]), ("w_rg", [P, 2, P]), ("w_l", [P, HID]), ("w_lg", [P, HID]),
                ("norm_w", [P, P]),
                ("mask_k", [P, COLS]), ("mask_rows", [P, LJ + 2 * BAND]), ("mask_sq", [P, LJ])))
        first_ctx = ctx.enter_context(ExitStack())
        mask_i, mask_ki, stats = (
            first_ctx.enter_context(nc.sbuf_tensor(f"l{layer}_{n}", shape, dt)) for n, shape, dt in (
                ("mask_i", [P, LJ + 2 * BAND], I32), ("mask_ki", [P, COLS], I32), ("stats", [P, UNITS, 6], F32)))
        bank = [ps(f"bank{i}", [P, UNIT]) for i in range(8)]

        def unit(t, u, n=1):
            return t[:, bass.ds(u * UNIT, UNIT * n)]

        def xn_unit(u):
            return xn[:, bass.ds(u * UNIT + BAND, UNIT)]

        w_ready, masks_done, stat_done, avg_done, gn_log, gn_rs, gn_mid, gn_out = map(sem, (
            "w_ready", "masks_done", "stat_done", "avg_done", "gn_log", "gn_rs", "gn_mid", "gn_out"))
        wb_ready, nb_ready, bias_done, stats_in = map(sem, ("wb_ready", "nb_ready", "bias_done", "stats_in"))
        loads = ((w_r, "w_r"), (w_rg, "w_rg"), (w_og, "w_og"), (w_l, "w_l"), (w_lg, "w_lg"), (w_o, "w_o"),
                 (vec32, "vec32"), (vec64, "vec64"), (mask_i, "mask_rows"), (mask_ki, "mask_cols"))
        ALL_W = 16 * len(loads)

        with nc.Block() as block:
            @block.sync
            def _(sp):
                for dst, name in loads:
                    sp.dma_start(dst[tuple(slice(None) for _ in dst.shape)], w[f"l{layer}_{name}"]).then_inc(w_ready, 16)

            @block.vector
            def _(v):
                for u in range(UNITS):
                    last = nc.vector.bn_stats(stats[:, u, :], xc[:, u * UNIT:(u + 1) * UNIT])
                last.then_inc(stats_in, 1)
                v.wait_ge(stats_in, 1)
                nc.vector.bn_aggr(mean_var[:, :], stats[:, :, :]).then_inc(stat_done, 1)
                v.wait_ge(avg_done, 1)
                v.wait_ge(stat_done, 1)
                nc.vector.tensor_tensor(group_dev[:, 0:1], bank[0][:, 0:1], mean_var[:, 0:1], ALU.subtract).then_inc(gn_mid, 1)
                nc.vector.tensor_copy(gn_mean[:, :], bank[0][:, 0:1]).then_inc(gn_out, 1)
                v.wait_ge(gn_mid, 1)
                nc.vector.scalar_tensor_tensor(group_dev[:, 1:2], group_dev[:, 0:1], group_dev[:, 0:1],
                                               mean_var[:, 1:2], ALU.mult, ALU.add).then_inc(stat_done, 1)
                v.wait_ge(gn_rs, 1)
                nc.vector.tensor_scalar(norm_w[:, :], center32[:, :], gn_scale[:, 0:1], None, ALU.mult).then_inc(gn_out, 1)
                v.wait_ge(nb_ready, 1)
                nc.vector.tensor_scalar(norm_b[:, :], bank[2][:, 0:1], -1.0, None, ALU.mult)
                v.wait_ge(w_ready, ALL_W)
                v.wait_ge(wb_ready, 1)
                nc.vector.tensor_tensor(bias[:, :], bank[3][:, 0:5], vec64[:, 0:5], ALU.add).then_inc(bias_done, 1)
                for t in (w_r, w_rg, w_og):
                    nc.vector.tensor_scalar(t[:, :, :], t[:, :, :], vec32[:, 0:1], None, ALU.mult)
                for t in (w_l, w_lg):
                    nc.vector.tensor_scalar(t[:, :], t[:, :], vec32[:, 0:1], None, ALU.mult)
                nc.vector.tensor_copy(mask_rows[:, :], mask_i[:, :]).then_inc(masks_done, 1)
                nc.vector.tensor_copy(mask_k[:, :], mask_ki[:, :])
                v.wait_ge(masks_done, 1)
                nc.vector.tensor_tensor(mask_sq[:, :], mask_rows[:, BAND:BAND + LJ], mask_rows[:, BAND:BAND + LJ], ALU.mult)
                nc.vector.memset(left[:, :, :], 0.0)

            @block.tensor
            def _(pe):
                pe.wait_ge(stat_done, 1)
                nc.tensor.matmul(bank[0][:, 0:1], avg[:, :], mean_var[:, 0:1], start=True, stop=True).then_inc(avg_done, 1)
                pe.wait_ge(stat_done, 2)
                nc.tensor.matmul(bank[1][:, 0:1], avg[:, :], group_dev[:, 1:2], start=True, stop=True).then_inc(avg_done, 1)
                pe.wait_ge(w_ready, ALL_W)
                first = True
                for col, t in ((1, w_r), (3, w_rg), (4, w_og)):
                    nc.tensor.matmul(bank[3][:, col:col + 1], t[:, 0, :], vec32[:, 1:2], start=first, stop=False,
                                     skip_group_check=True)
                    first = False
                for half in range(2):
                    for col, t in ((0, w_l), (2, w_lg)):
                        last = nc.tensor.matmul(bank[3][HID * half:HID * half + HID, col:col + 1], t[0:C, :],
                                                vec32[0:C, 1:2], start=False, stop=True, skip_group_check=True)
                last.then_inc(wb_ready, 1)
                pe.wait_ge(gn_out, 2)
                nc.tensor.matmul(bank[2][:, 0:1], norm_w[:, :], gn_mean[:, :], start=True, stop=True).then_inc(nb_ready, 1)

            @block.scalar
            def _(a):
                a.wait_ge(avg_done, 2)
                nc.scalar.activation(gn_scale[:, :], bank[1][:, 0:1], ACT.Ln, bias=eps[:, 0:1]).then_inc(gn_log, 1)
                a.wait_ge(gn_log, 1)
                nc.scalar.activation(gn_scale[:, :], gn_scale[:, :], ACT.Exp, scale=-0.5).then_inc(gn_rs, 1)

        first_ctx.close()

        cent_ready, sq_done, var_ready, log_done, rstd_done, xn_done = map(
            sem, ("cent_ready", "sq_done", "var_ready", "log_done", "rstd_done", "xn_done"))
        cent, var = bank[0:4], bank[4:8]
        sq4 = [win[0][:, 2 * i:2 * i + 2, :].rearrange("p r k -> p (r k)") for i in range(4)]
        rstd4 = [win[1][:, 2 * i:2 * i + 2, :].rearrange("p r k -> p (r k)") for i in range(4)]

        def units(eng, body, depth=2):
            peeled = 8 if depth == 4 else depth
            for u in range(peeled):
                body(u, u % depth, u < depth)
            with eng.Fori(peeled, UNITS - depth + 1, depth) as u:
                for i in range(depth):
                    body(u + i, i, False)

        with nc.Block() as block:
            @block.tensor
            def _(pe):
                def body(u, at, first):
                    if not first:
                        pe.wait_ge(xn_done, u - 3)
                    nc.tensor.matmul(cent[at][:, :], norm_w[:, :], unit(xc, u), start=True, stop=True).then_inc(cent_ready, 1)
                    if not (first and u < 1):
                        variance(u - 1, (at - 1) % 4)

                def variance(u, at):
                    pe.wait_ge(sq_done, u + 1)
                    if not (isinstance(u, int) and u < 4):
                        pe.wait_ge(log_done, u - 3)
                    nc.tensor.matmul(var[at][:, :], mean32[:, :], sq4[at], start=True, stop=True).then_inc(var_ready, 1)

                units(pe, body, 4)
                variance(UNITS - 1, 3)

            @block.scalar
            def _(a):
                a.preload_act_table_set("natural_log_exp_and_others")

                def body(u, at, first):
                    a.wait_ge(cent_ready, u + 1)
                    if not first:
                        a.wait_ge(var_ready, u - 3)
                    nc.scalar.activation(sq4[at], cent[at][:, :], ACT.Square, bias=norm_b[:, 0:1]).then_inc(sq_done, 1)
                    if not (first and u < 2):
                        root(u - 2, (at - 2) % 4)

                def root(u, at):
                    a.wait_ge(var_ready, u + 1)
                    if not (isinstance(u, int) and u < 4):
                        a.wait_ge(xn_done, u - 3)
                    nc.scalar.activation(rstd4[at], var[at][:, :], ACT.Ln, bias=eps[:, 1:2]).then_inc(log_done, 1)
                    a.wait_ge(log_done, u + 1)
                    nc.scalar.activation(rstd4[at], rstd4[at], ACT.Exp, scale=-0.5).then_inc(rstd_done, 1)

                units(a, body, 4)
                for i in range(2):
                    root(UNITS - 2 + i, 2 + i)

            @block.vector
            def _(v):
                def body(u, at, first):
                    v.wait_ge(rstd_done, u + 1)
                    nc.vector.scalar_tensor_tensor(xn_unit(u), cent[at][:, :], norm_b[:, 0:1], rstd4[at],
                                                   ALU.add, ALU.mult).then_inc(xn_done, 1)
                units(v, body, 4)

        left_ready, left_sig, left_done, left_mul = map(sem, ("left_ready", "left_sig", "left_done", "left_mul"))
        pieces = [(32 * h, 32, BAND + 64 * p + 32 * h, [(0, 2 * p), (1, 2 * p + 1)]) for p in range(2) for h in range(2)]
        pieces += [(RB - BAND, BAND, 0, [(1, 2)]),
                   (0, BAND, BAND + 128, [(0, 1)])]

        def first_row(g):
            return 128 * (g % 2) + RB * (g // 2)

        with nc.Block() as block:
            @block.tensor
            def _(pe):
                for n, (r0, nr, _, parts) in enumerate(pieces):
                    if n >= 2:
                        pe.wait_ge(left_done, n - 1)
                    for t, dst in ((w_l, bank[2 * (n % 2)]), (w_lg, bank[2 * (n % 2) + 1])):
                        for half, g in parts:
                            base = xn[C * g:C * g + C, 0:1]
                            diag = bass.AP(base.tensor, base.offset + r0 * (COLS + 1) + first_row(g),
                                           [list(base.ap[0]), [COLS + 1, nr], [1, TAPS_B]])
                            m = nc.tensor.matmul(dst[HID * half:HID * half + HID, 0:nr * TAPS_B],
                                                 t[C * g:C * g + C, :], diag, start=True, stop=True)
                    m.then_inc(left_ready, 1)

            @block.scalar
            def _(a):
                for n, (r0, nr, l0, parts) in enumerate(pieces):
                    a.wait_ge(left_ready, n + 1)
                    if n >= 2:
                        a.wait_ge(left_done, n - 1)
                    lo, hi = HID * parts[0][0], HID * parts[-1][0] + HID
                    nc.scalar.activation(sq[n % 2][lo:hi, 0:nr * TAPS_B], bank[2 * (n % 2) + 1][lo:hi, 0:nr * TAPS_B],
                                         ACT.Sigmoid, bias=bias[lo:hi, 2:3]).then_inc(left_sig, 1)

            @block.vector
            def _(v):
                for n, (r0, nr, l0, parts) in enumerate(pieces):
                    v.wait_ge(left_sig, n + 1)
                    lo, hi = HID * parts[0][0], HID * parts[-1][0] + HID
                    nc.vector.scalar_tensor_tensor(left[lo:hi, l0:l0 + nr, :].rearrange("p j d -> p (j d)"),
                                                   bank[2 * (n % 2)][lo:hi, 0:nr * TAPS_B], bias[lo:hi, 0:1],
                                                   sq[n % 2][lo:hi, 0:nr * TAPS_B], ALU.add, ALU.mult).then_inc(left_done, 1)
                v.wait_ge(left_done, len(pieces))
                for d in range(TAPS_B):
                    nc.vector.tensor_tensor(left[:, :, d], left[:, :, d], mask_sq[:, :], ALU.mult).then_inc(left_mul, 1)
                for d in range(TAPS_B):
                    v.wait_ge(left_mul, d + 1)
                    nc.vector.tensor_tensor(left[:, :, d], left[:, :, d], mask_rows[:, d:d + LJ], ALU.mult).then_inc(left_mul, 1)

        rp_ready, rg_ready, rsig_done, r_done, r_masked = map(
            sem, ("rp_ready", "rg_ready", "rsig_done", "r_done", "r_masked"))
        r_stored = [sem(f"r_stored{i}") for i in range(4)]
        r_tile = [band[i][:, 2 * p:2 * p + 2, :].rearrange("p r k -> p (r k)") for i in range(2) for p in range(2)]
        sig = [gate[:, i * UNIT:(i + 1) * UNIT] for i in range(4)]
        with nc.Block() as block:
            @block.tensor
            def _(pe):
                def body(u, par, first):
                    for p in range(2):
                        n, slot = 2 * u + p, 2 * par + p
                        if not first:
                            pe.wait_ge(r_done, n - 3)
                        nc.tensor.matmul(bank[slot][:, :], w_rg[:, p, :], xn_unit(u), start=True, stop=True).then_inc(rg_ready, 1)
                        nc.tensor.matmul(bank[4 + slot][:, :], w_r[:, p, :], xn_unit(u), start=True, stop=True).then_inc(rp_ready, 1)
                units(pe, body)

            @block.scalar
            def _(a):
                def store(u, par):
                    for p in range(2):
                        a.wait_ge(r_masked, 2 * u + p + 1)
                        for half in range(2):
                            dst = right_dram[:, :, :].rearrange("h r k -> h (r k)")
                            a.dma_start(dst[:, bass.ds(u * UNIT + (BAND + 128 * half + RB * p) * COLS, UNIT)],
                                        r_tile[2 * par + p][HID * half:HID * half + HID, :]).then_inc(r_stored[2 * par + p], 16)

                def body(u, par, first):
                    for p in range(2):
                        n, slot = 2 * u + p, 2 * par + p
                        a.wait_ge(rg_ready, n + 1)
                        if not first:
                            a.wait_ge(r_done, n - 3)
                        nc.scalar.activation(sig[slot], bank[slot][:, :], ACT.Sigmoid, bias=bias[:, 3:4]).then_inc(rsig_done, 1)
                    if not (first and u == 0):
                        store(u - 1, 1 - par)
                units(a, body)
                store(UNITS - 1, 1)
                for slot in range(4):
                    a.wait_ge(r_stored[slot], 32 * (UNITS // 2))

            @block.vector
            def _(v):
                def body(u, par, first):
                    for p in range(2):
                        n, slot = 2 * u + p, 2 * par + p
                        v.wait_ge(rsig_done, n + 1)
                        v.wait_ge(rp_ready, n + 1)
                        if not first:
                            v.wait_ge(r_stored[slot], 16 * u - 16 * par)
                        nc.vector.scalar_tensor_tensor(r_tile[slot], bank[4 + slot][:, :], bias[:, 1:2], sig[slot],
                                                       ALU.add, ALU.mult).then_inc(r_done, 1)
                units(v, body)

            @block.gpsimd
            def _(g):
                def body(u, par, first):
                    for p in range(2):
                        n, slot = 2 * u + p, 2 * par + p
                        g.wait_ge(r_done, n + 1)
                        t = r_tile[slot].rearrange("p (r k) -> p r k", k=COLS)
                        nc.gpsimd.tensor_tensor(t, t, mask_k[:, :].unsqueeze(1).to_broadcast([P, 2, COLS]),
                                                ALU.mult).then_inc(r_masked, 1)
                units(g, body)

        early_ctx.close()
        rstd = sq + [sb(f"rstd{i}", [P, UNIT]) for i in range(2)]
        tap_w = sb("tap_w", [P, TAPS_B, P])
        lslab = [sb(f"lslab{i}", [P, BR + 2 * BAND, TAPS_B]) for i in range(2)]
        DR = BR - 2
        LAST = SUBS - 1
        PE_TAPS = 2 * TAPS_B
        NB = 2 * BLOCKS
        DVE_TAPS = DR * TAPS_B
        win_loaded = [sem(f"win_loaded{i}") for i in range(2)]
        tap_done, slab_done, tapw_done, pe_tap_done, g_ready, gate_done, c_ready, sq2_done, v_ready, log2_done, \
            rstd2_done, z_done, zb_done, zg_done, y_ready, x_done = map(sem, (
                "tap_done", "slab_done", "tapw_done", "pe_tap_done", "g_ready", "gate_done", "c_ready", "sq2_done",
                "v_ready", "log2_done", "rstd2_done", "z_done", "zb_done", "zg_done", "y_ready", "x_done"))
        cb, gb, vb, yb = bank[0:3], bank[4], bank[5], bank[6]
        cb_last = (bank[3], bank[7])

        def blocks(eng, turn):
            def at(p, b):
                return (BLOCKS * p + b, p, b)
            turn(at(0, 0), None, 0)
            turn(at(0, 1), at(0, 0), 1)
            with eng.Fori(2, BLOCKS - 1, 2) as b:
                turn(at(0, b), at(0, b - 1), 0)
                turn(at(0, b + 1), at(0, b), 1)
            turn(at(1, 0), at(0, BLOCKS - 1), 0)
            turn(at(1, 1), at(1, 0), 1)
            with eng.Fori(2, BLOCKS - 1, 2) as b:
                turn(at(1, b), at(1, b - 1), 0)
                turn(at(1, b + 1), at(1, b), 1)
            turn(None, at(1, BLOCKS - 1), 0)

        def early(n, limit):
            return isinstance(n, int) and n < limit

        def centred(par, j):
            return cb[j] if j < LAST else cb_last[par]

        def unit_of(par, j):
            return band[par][:, 2 * j:2 * j + 2, :].rearrange("p r k -> p (r k)")

        with nc.Block() as block:
            @block.sync
            def _(sp):
                for n in range(NB):
                    if n >= 2:
                        sp.wait_ge(tap_done, (n - 1) * DVE_TAPS)
                        sp.wait_ge(pe_tap_done, (n - 1) * PE_TAPS)
                    for half in range(2):
                        r0 = 128 * half + BR * n
                        sp.dma_start(win[n % 2][HID * half:HID * half + HID, :, :],
                                     right_dram[:, r0:r0 + BR + 2 * BAND, :]).then_inc(win_loaded[n % 2], 16)

            @block.vector
            def _(v):
                def taps(n, par, rows, first_tap, end_tap):
                    for tap in range(first_tap, end_tap):
                        for i, r in enumerate(rows):
                            src = win[par][:, r + tap, :]
                            dst = band[par][:, r, :]
                            coef = lslab[par][:, r + tap, TAPS_B - 1 - tap:TAPS_B - tap]
                            if tap == 0:
                                m = nc.vector.tensor_scalar(dst, src, coef, None, ALU.mult)
                            else:
                                v.wait_ge(tap_done, n * DVE_TAPS + rows[0] * TAPS_B + (tap - 1) * len(rows) + i + 1)
                                m = nc.vector.scalar_tensor_tensor(dst, src, coef, dst, ALU.mult, ALU.add)
                            m.then_inc(tap_done, 1)

                def residual(n, p, b, j):
                    v.wait_ge(y_ready, SUBS * n + j + 1)
                    x = xc[2 * C * p:2 * C * p + 2 * C, bass.ds(b * (BR * COLS) + j * UNIT, UNIT)]
                    nc.vector.scalar_tensor_tensor(x, yb[2 * C * p:2 * C * p + 2 * C, :],
                                                   vec32[2 * C * p:2 * C * p + 2 * C, 2:3], x,
                                                   ALU.add, ALU.add).then_inc(x_done, 1)

                def turn(now, before, par):
                    if now:
                        n, p, b = now
                        if not early(n, 2):
                            v.wait_ge(tapw_done, PE_TAPS * n - PE_TAPS)
                        nc.vector.tensor_copy(lslab[par][:, :, :].rearrange("p j d -> p (j d)"),
                                              left[:, :, :].rearrange("p j d -> p (j d)")[
                                                  :, bass.ds(b * (BR * TAPS_B) + RB * p * TAPS_B, (BR + 2 * BAND) * TAPS_B)]
                                              ).then_inc(slab_done, 1)
                        v.wait_ge(slab_done, n + 1)
                        v.wait_ge(win_loaded[par], 16 * n + (32 - 16 * par))
                        taps(n, par, range(DR // 2), 0, TAPS_B)
                    if before:
                        m, pm, bm = before
                        for j in range(SUBS):
                            v.wait_ge(rstd2_done, SUBS * m + j + 1)
                            nc.vector.scalar_tensor_tensor(unit_of(1 - par, j), centred(1 - par, j)[:, :], vec64[:, 5:6], rstd[j][:, :],
                                                           ALU.mult, ALU.mult).then_inc(z_done, 1)
                    for j in range(SUBS):
                        if now:
                            taps(n, par, range(DR // 2, DR), (0, 5, 7, 8)[j], (5, 7, 8, TAPS_B)[j])
                        if before:
                            residual(m, pm, bm, j)
                blocks(v, turn)

            @block.tensor
            def _(pe):
                def turn(now, before, par):
                    if now:
                        n, p, b = now
                    if before:
                        m, pm, bm = before
                        pe.wait_ge(tap_done, DVE_TAPS * m + DVE_TAPS)
                        if not early(m, 1):
                            pe.wait_ge(z_done, SUBS * m)
                        for j in range(LAST):
                            nc.tensor.matmul(cb[j][:, :], center64[:, :], unit_of(1 - par, j),
                                             start=True, stop=True).then_inc(c_ready, 1)
                    def taps(r, first_tap, end_tap):
                        if now:
                            for tap in range(first_tap, end_tap):
                                pe.wait_ge(tapw_done, n * PE_TAPS + r * TAPS_B + tap + 1)
                                if r == 0 and tap == 0:
                                    pe.wait_ge(win_loaded[par], 16 * n + (32 - 16 * par))
                                nc.tensor.matmul(cb_last[par][:, r * COLS:(r + 1) * COLS], tap_w[:, tap, :],
                                                 win[par][:, DR + r + tap, :], start=(r == 0 and tap == 0),
                                                 stop=(tap == TAPS_B - 1), skip_group_check=True).then_inc(pe_tap_done, 1)

                    def project(j):
                        if before:
                            i = SUBS * m + j
                            pe.wait_ge(zg_done, i + 1)
                            if not (early(m, 1) and j == 0):
                                pe.wait_ge(x_done, i)
                            nc.tensor.matmul(yb[2 * C * pm:2 * C * pm + 2 * C, :], w_o[:, :], unit_of(1 - par, j),
                                             start=True, stop=True).then_inc(y_ready, 1)

                    def open_gate(j):
                        if now:
                            if not (early(n, 1) and j == 0):
                                pe.wait_ge(gate_done, SUBS * n + j)
                            nc.tensor.matmul(gb[:, :], w_og[:, p, :],
                                             xn[:, bass.ds(b * (BR * COLS) + (j * UNIT + BAND), UNIT)],
                                             start=True, stop=True).then_inc(g_ready, 1)

                    def variance(j):
                        if before:
                            i = SUBS * m + j
                            pe.wait_ge(sq2_done, i + 1)
                            if not (early(m, 1) and j == 0):
                                pe.wait_ge(log2_done, i)
                            nc.tensor.matmul(vb[:, :], mean64[:, :], rstd[j][:, :], start=True, stop=True).then_inc(v_ready, 1)

                    for j in range(SUBS):
                        variance(j)
                        taps(0, 3 * j, min(3 * j + 3, TAPS_B))
                    for j in range(SUBS):
                        project(j)
                        open_gate(j)
                        taps(1, 3 * j, min(3 * j + 3, TAPS_B))
                blocks(pe, turn)

            @block.scalar
            def _(a):
                def turn(now, before, par):
                    if before:
                        m, pm, bm = before
                    if now:
                        n, p, b = now
                        a.wait_ge(slab_done, n + 1)

                    def matrices(r, first_tap, end_tap):
                        for tap in range(first_tap, end_tap):
                            if not (early(n, 1) and r == 0):
                                a.wait_ge(pe_tap_done, n * PE_TAPS + r * TAPS_B + tap + 1 - TAPS_B)
                            nc.scalar.activation(tap_w[:, tap, :], center64[:, :], ACT.Copy,
                                                 scale=lslab[par][:, DR + r + tap, TAPS_B - 1 - tap:TAPS_B - tap]
                                                 ).then_inc(tapw_done, 1)

                    for j in range(SUBS):
                        if now and j < LAST:
                            matrices(0, 3 * j, 3 * j + 3)
                        if before:
                            if j < LAST:
                                a.wait_ge(c_ready, LAST * m + j + 1)
                            else:
                                a.wait_ge(pe_tap_done, PE_TAPS * m + PE_TAPS)
                            if not early(m, 1):
                                a.wait_ge(z_done, SUBS * m + j - SUBS + 1)
                            nc.scalar.activation(rstd[j][:, :], centred(1 - par, j)[:, :], ACT.Square).then_inc(sq2_done, 1)
                            if j >= 1:
                                root(m, j - 1)
                    if before:
                        root(m, SUBS - 1)
                    if now:
                        matrices(1, 0, TAPS_B)
                        a.preload_act_table_set("sigmoid_and_others")
                        for j in range(SUBS):
                            a.wait_ge(g_ready, SUBS * n + j + 1)
                            if before:
                                a.wait_ge(zg_done, SUBS * m + j + 1)
                            nc.scalar.activation(gate[:, j * UNIT:(j + 1) * UNIT], gb[:, :], ACT.Sigmoid,
                                                 bias=bias[:, 4:5]).then_inc(gate_done, 1)
                        a.preload_act_table_set("natural_log_exp_and_others")

                def root(m, j):
                    i = SUBS * m + j
                    a.wait_ge(v_ready, i + 1)
                    nc.scalar.activation(rstd[j][:, :], vb[:, :], ACT.Ln, bias=eps[:, 1:2]).then_inc(log2_done, 1)
                    a.wait_ge(log2_done, i + 1)
                    nc.scalar.activation(rstd[j][:, :], rstd[j][:, :], ACT.Exp, scale=-0.5).then_inc(rstd2_done, 1)
                blocks(a, turn)

            @block.gpsimd
            def _(g):
                def turn(now, before, par):
                    if before:
                        m, pm, bm = before
                        g.wait_ge(gate_done, SUBS * m + SUBS)
                        for j in range(SUBS):
                            g.wait_ge(z_done, SUBS * m + j + 1)
                            nc.gpsimd.tensor_tensor(unit_of(1 - par, j), unit_of(1 - par, j),
                                                    vec64[:, 6:7].to_broadcast([P, UNIT]), ALU.add).then_inc(zb_done, 1)
                            g.wait_ge(zb_done, SUBS * m + j + 1)
                            nc.gpsimd.tensor_tensor(unit_of(1 - par, j), unit_of(1 - par, j),
                                                    gate[:, j * UNIT:(j + 1) * UNIT], ALU.mult).then_inc(zg_done, 1)
                blocks(g, turn)

        nc.clear_and_free_semaphores(sems)


def build(nc, x_cm, w, right_dram, x3, out):
    with ExitStack() as sems, ExitStack() as ctx:
        def sb(name, shape, dt=F32):
            return ctx.enter_context(nc.sbuf_tensor(name, shape, dt))

        xc = sb("xc", [P, RB * COLS])
        xn = sb("xn", [P, RB * COLS + 2 * BAND])
        share = {n: sb(n, [P, P]) for n in ("avg", "center32", "mean32", "center64", "mean64")}
        share["eps"] = sb("eps", [P, 2])
        zero_ctx = ctx.enter_context(ExitStack())
        zero_rows = zero_ctx.enter_context(nc.sbuf_tensor("zero_rows", [HID, BAND * COLS], F32))
        x_loaded, zeroed, padded, consts = (sems.enter_context(nc.semaphore(n)) for n in (
            "x_loaded", "zeroed", "padded", "consts"))
        x_stored = sems.enter_context(nc.semaphore("x_stored"))
        with nc.Block() as block:
            @block.sync
            def _(sp):
                for g in range(4):
                    r0 = 128 * (g % 2) + RB * (g // 2)
                    for q in range(4):
                        sp.dma_start(xc[C * g:C * g + C, q * 4096:(q + 1) * 4096],
                                     x_cm[:, r0 + 16 * q:r0 + 16 * q + 16, :].rearrange("c r k -> c (r k)")
                                     ).then_inc(x_loaded, 16)
                sp.wait_ge(zeroed, 1)
                for r in (0, BAND + ROWS):
                    sp.dma_start(right_dram[:, r:r + BAND, :].rearrange("h r k -> h (r k)"),
                                 zero_rows[:, :]).then_inc(padded, 16)
                sp.wait_ge(padded, 32)
                sp.wait_ge(x_loaded, 256)

            @block.scalar
            def _(a):
                for n in ("avg", "center32", "mean32", "center64", "mean64"):
                    a.dma_start(share[n][:, :], w[n]).then_inc(consts, 16)
                a.wait_ge(consts, 80)

            @block.vector
            def _(v):
                nc.vector.memset(zero_rows[:, :], 0.0).then_inc(zeroed, 1)
                nc.vector.memset(xn[:, 0:BAND], 0.0)
                nc.vector.memset(xn[:, BAND + RB * COLS:], 0.0)
                nc.vector.memset(share["eps"][:, 0:1], 1e-5)
                nc.vector.memset(share["eps"][:, 1:2], 1e-6)

        zero_ctx.close()
        for layer in range(3):
            triangle_layer(nc, layer, xc, xn, share, w, right_dram)
            nc.all_engine_barrier()

        with nc.Block() as block:
            @block.sync
            def _(sp):
                for g in range(4):
                    r0 = 128 * (g % 2) + RB * (g // 2)
                    sp.dma_start(x3[:, r0:r0 + RB, :].rearrange("c r k -> c (r k)"),
                                 xc[C * g:C * g + C, :]).then_inc(x_stored, 16)
                sp.wait_ge(x_stored, 64)
        ctx.close()
        mamba_layer(nc, x3, w, out)


def _layout(f):
    import numpy as np

    def zeros(*s):
        return np.zeros(s, np.float32)

    a = {"x_cm": f["x"][0].transpose(2, 0, 1), "ident": np.eye(P, dtype=np.float32)}
    a["avg"] = np.kron(np.ones((4, 4), np.float32) / 4, np.eye(C, dtype=np.float32))
    a["mean32"] = np.kron(np.eye(4, dtype=np.float32), np.full((32, 32), 1 / 32, np.float32))
    a["center32"] = np.eye(P, dtype=np.float32) - a["mean32"]
    a["mean64"] = np.kron(np.eye(2, dtype=np.float32), np.full((64, 64), 1 / 64, np.float32))
    a["center64"] = np.eye(P, dtype=np.float32) - a["mean64"]
    for layer in range(3):
        k = lambda n: f[f"L{layer}_conv_{n}"]
        o = f"l{layer}_"
        for dst, name in (("w_r", "Wr"), ("w_rg", "Wrg"), ("w_og", "Wog")):
            t = zeros(P, 2, P)
            for pair in range(2):
                for half in range(2):
                    r = 64 * pair + 32 * half
                    t[r:r + 32, pair, 64 * half:64 * half + 64] = k(name)
            a[o + dst] = t
        a[o + "w_l"], a[o + "w_lg"] = np.tile(k("Wl"), (4, 1)), np.tile(k("Wlg"), (4, 1))
        t = zeros(P, 64)
        for half in range(2):
            t[64 * half:64 * half + 64, 32 * half:32 * half + 32] = k("Wo")
        a[o + "w_o"] = t
        a[o + "vec32"] = np.tile(np.stack([k("norm_scale"), k("norm_bias"), k("bo")], 1), (4, 1))
        a[o + "vec64"] = np.tile(np.stack([k(n) for n in (
            "bl", "br", "blg", "brg", "bog", "out_norm_scale", "out_norm_bias")], 1), (2, 1))
        m = k("src_mask")[0]
        padded = np.zeros(ROWS + 16, m.dtype)
        padded[8:8 + ROWS] = m
        a[o + "mask_rows"] = np.repeat(np.stack([padded[0:144], padded[128:272]]), 64, axis=0)
        a[o + "mask_cols"] = np.repeat(m[None], P, axis=0)
    W_in, conv_w, W_x = f["L3_conv_W_in"], f["L3_conv_conv_w"], f["L3_conv_W_x"]
    w_in, w_z, taps = zeros(P, P), zeros(P // 2, P), zeros(P, 2, P)
    for shift in range(2):
        for n in range(2):
            r = 64 * shift + 32 * n
            w_in[r:r + 32, 64 * n:64 * n + 64] = W_in[:, :64]
            if shift == 0:
                w_z[r:r + 32, 64 * n:64 * n + 64] = W_in[:, 64:]
        for t in range(2):
            taps[64 * shift:64 * shift + 64, t, :] = np.tile(conv_w[:, 2 * shift + t], 2)
    a["w_in"], a["w_z"], a["conv_w"] = w_in, w_z, taps
    wx_dt, w_dt, w_bc, w_out = zeros(4, P), zeros(4, P), zeros(P, 2, 32), zeros(P, 64)
    for n in range(2):
        wx_dt[2 * n:2 * n + 2, 64 * n:64 * n + 64] = W_x[:, 0:2].T
        w_dt[2 * n:2 * n + 2, 64 * n:64 * n + 64] = f["L3_conv_W_dt"]
        for b in range(2):
            w_bc[64 * n:64 * n + 64, b, 16 * n:16 * n + 16] = W_x[:, 2 + 16 * b:18 + 16 * b]
        w_out[64 * n:64 * n + 64, 32 * n:32 * n + 32] = f["L3_conv_W_out"]
    a["wx_dt"], a["w_dt"], a["w_bc"], a["w_out"] = wx_dt, w_dt, w_bc, w_out
    a["vecs"] = np.tile(np.stack([f["L3_conv_conv_b"], f["L3_conv_b_dt"], f["L3_conv_D_skip"]], 1), (2, 1))
    a["a_log"] = np.tile(f["L3_conv_A_log"], (2, 1))
    sel = zeros(3, 2, 16, 16, 2, 64)
    for n in range(2):
        for s in range(16):
            sel[:, n, s, s, n, :] = 1
    a["sel"] = sel.reshape(96, 16, P)
    return {n: np.ascontiguousarray(t) for n, t in a.items()}


def kernel(**inputs):
    import numpy as np
    import concourse.bacc as bacc
    from concourse.bass_utils import run_bass_kernel_spmd

    nc = bacc.Bacc("TRN2", target_bir_lowering=False, num_devices=1)
    arrays = _layout({n: np.asarray(v) for n, v in inputs.items()})
    w = {n: nc.dram_tensor("in_" + n, t.shape, mybir.dt.from_np(t.dtype), kind="ExternalInput").ap()
         for n, t in arrays.items()}
    right_dram = nc.dram_tensor("right_factor", (HID, PADDED, COLS), F32, kind="Internal").ap()
    x3 = nc.dram_tensor("x_layer3", (C, ROWS, COLS), F32, kind="Internal").ap()
    out = nc.dram_tensor("out_cm", (C, COLS, ROWS), F32, kind="ExternalOutput").ap()
    build(nc, w["x_cm"], w, right_dram, x3, out)
    r = run_bass_kernel_spmd(nc, [{"in_" + n: t for n, t in arrays.items()}], core_ids=[0])
    return r.results[0]["out_cm"].transpose(2, 1, 0)[None]
```
